# Optimizing a Trainium2 kernel written in Bass

```python
import numpy as np
import jax
import jax.numpy as jnp

def _softmax(x, axis=-1):
    return jax.nn.softmax(x, axis=axis)

def _gelu(x):
    return jax.nn.gelu(x, approximate=True)

def _silu(x):
    return jax.nn.silu(x)

def _sigmoid(x):
    return jax.nn.sigmoid(x)

def _layernorm(x, axis=-1, eps=1e-05):
    m = jnp.mean(x, axis=axis, keepdims=True)
    v = jnp.var(x, axis=axis, keepdims=True)
    return (x - m) / jnp.sqrt(v + eps)

def _scatter_add(tgt, idx, src, axis=0):
    return tgt.at[idx].add(src)

def _segment_sum(src, seg, n):
    return jax.ops.segment_sum(src, seg, n)
kernel_name = 'mk_recurrent_d1_jaxref_r8_0770d9'

def setup_inputs(seed: int=0):
    np.random.seed(seed)
    _w = jnp.asarray

    def _L0_attn_setup():
        import jax, jax.numpy as jnp
        import numpy as np
        K_FACTOR = 0.5
        key = jax.random.key(seed)
        k1, k2, k3, k4 = jax.random.split(key, 4)
        B, S, H, I = (1, 256, 512, 1376)
        x = jax.random.normal(k1, (B, S, H), dtype=jnp.float32)
        w_gate = jax.random.normal(k2, (I, H), dtype=jnp.float32) * 0.02
        w_up = jax.random.normal(k3, (I, H), dtype=jnp.float32) * 0.02
        w_down = jax.random.normal(k4, (H, I), dtype=jnp.float32) * 0.02
        return {'x': x, 'w_gate': w_gate, 'w_up': w_up, 'w_down': w_down}
    _L0_attn_in = _L0_attn_setup()

    def _L0_ffn_setup():
        import jax, jax.numpy as jnp
        import numpy as np
        DIM = 512
        INTER = 128
        E = 16
        GROUPS = 4
        LIM = 2
        K = 2
        SHARED_INTER = 2 * INTER
        SCALE = 1.0
        key = jax.random.key(seed)
        ks = jax.random.split(key, 16)

        def n(k, shape, s=0.02):
            return jax.random.normal(k, shape, jnp.float32) * s
        return {'x': jax.random.normal(ks[0], (1, 256, DIM), jnp.float32), 'router_w': n(ks[1], (DIM, E)), 'router_b': n(ks[2], (E,)), 'router_bias': n(ks[3], (E,), 1.0), 'ew1': n(ks[4], (E, DIM, INTER)), 'eb1': n(ks[5], (E, INTER)), 'ew2': n(ks[6], (E, DIM, INTER)), 'eb2': n(ks[7], (E, INTER)), 'ew3': n(ks[8], (E, INTER, DIM)), 'eb3': n(ks[9], (E, DIM)), 'sw1': n(ks[10], (DIM, SHARED_INTER)), 'sb1': n(ks[11], (SHARED_INTER,)), 'sw2': n(ks[12], (DIM, SHARED_INTER)), 'sb2': n(ks[13], (SHARED_INTER,)), 'sw3': n(ks[14], (SHARED_INTER, DIM)), 'sb3': n(ks[15], (DIM,))}
    _L0_ffn_in = _L0_ffn_setup()
    _d = {'L0_attn_x': _L0_attn_in['x'], 'L0_attn_w_gate': _L0_attn_in['w_gate'], 'L0_attn_w_up': _L0_attn_in['w_up'], 'L0_attn_w_down': _L0_attn_in['w_down'], 'L0_ffn_router_w': _L0_ffn_in['router_w'], 'L0_ffn_router_b': _L0_ffn_in['router_b'], 'L0_ffn_router_bias': _L0_ffn_in['router_bias'], 'L0_ffn_ew1': _L0_ffn_in['ew1'], 'L0_ffn_eb1': _L0_ffn_in['eb1'], 'L0_ffn_ew2': _L0_ffn_in['ew2'], 'L0_ffn_eb2': _L0_ffn_in['eb2'], 'L0_ffn_ew3': _L0_ffn_in['ew3'], 'L0_ffn_eb3': _L0_ffn_in['eb3'], 'L0_ffn_sw1': _L0_ffn_in['sw1'], 'L0_ffn_sb1': _L0_ffn_in['sb1'], 'L0_ffn_sw2': _L0_ffn_in['sw2'], 'L0_ffn_sb2': _L0_ffn_in['sb2'], 'L0_ffn_sw3': _L0_ffn_in['sw3'], 'L0_ffn_sb3': _L0_ffn_in['sb3']}
    _x0 = _d['L0_attn_x']
    _d['L0_attn_x'] = jax.random.normal(jax.random.fold_in(jax.random.key(seed), 1), (4, 256, 512), dtype=_x0.dtype)
    del _x0
    return _d

def reference(L0_attn_x, L0_attn_w_gate, L0_attn_w_up, L0_attn_w_down, L0_ffn_router_w, L0_ffn_router_b, L0_ffn_router_bias, L0_ffn_ew1, L0_ffn_eb1, L0_ffn_ew2, L0_ffn_eb2, L0_ffn_ew3, L0_ffn_eb3, L0_ffn_sw1, L0_ffn_sb1, L0_ffn_sw2, L0_ffn_sb2, L0_ffn_sw3, L0_ffn_sb3):

    def _L0_attn_ref(x, w_gate, w_up, w_down):
        import jax, jax.numpy as jnp
        import numpy as np
        K_FACTOR = 0.5
        s = jax.nn.silu(jnp.einsum('bsh,ih->bsi', x, w_gate))
        B, S, I = s.shape
        k = int(K_FACTOR * I)
        _, idx = jax.lax.top_k(-jnp.abs(s), k)
        flat = s.reshape(B * S, I)
        rows = jnp.arange(B * S)[:, None]
        flat = flat.at[rows, idx.reshape(B * S, k)].set(0.0)
        s = flat.reshape(B, S, I)
        s = s * jnp.einsum('bsh,ih->bsi', x, w_up)
        return jnp.einsum('bsi,hi->bsh', s, w_down)

    def _L0_ffn_ref(x, router_w, router_b, router_bias, ew1, eb1, ew2, eb2, ew3, eb3, sw1, sb1, sw2, sb2, sw3, sb3):
        import jax, jax.numpy as jnp
        import numpy as np
        DIM = 512
        INTER = 128
        E = 16
        GROUPS = 4
        LIM = 2
        K = 2
        SHARED_INTER = 2 * INTER
        SCALE = 1.0
        shape = x.shape
        xt = x.reshape(-1, DIM)
        T = xt.shape[0]
        logits = xt @ router_w + router_b
        scores = jax.nn.softmax(logits.astype(jnp.float32), axis=-1) + router_bias
        g = scores.reshape(T, GROUPS, E // GROUPS)
        _, gidx = jax.lax.top_k(g.max(axis=-1), LIM)
        keep = jnp.zeros((T, GROUPS), bool).at[jnp.arange(T)[:, None], gidx].set(True)
        masked = jnp.where(keep[:, :, None], g, -jnp.inf).reshape(T, E)
        _, idx = jax.lax.top_k(masked, K)
        vals = (jnp.take_along_axis(scores, idx, axis=1) * SCALE).astype(x.dtype)
        gate = jnp.zeros((T, E), x.dtype).at[jnp.arange(T)[:, None], idx].add(vals)

        def step(y, p):
            w1, b1, w2, b2, w3, b3, ge = p
            h = jax.nn.silu(xt @ w1 + b1) * (xt @ w2 + b2)
            return (y + ge[:, None] * (h @ w3 + b3), None)
        y, _ = jax.lax.scan(step, jnp.zeros_like(xt), (ew1, eb1, ew2, eb2, ew3, eb3, gate.T))
        z = jax.nn.silu(xt @ sw1 + sb1) * (xt @ sw2 + sb2) @ sw3 + sb3
        return (y + z).reshape(shape)
    x = L0_attn_x
    xn = _layernorm(x, axis=-1)
    s = _L0_attn_ref(xn, L0_attn_w_gate, L0_attn_w_up, L0_attn_w_down)
    g = _silu(_L0_ffn_ref(xn, L0_ffn_router_w, L0_ffn_router_b, L0_ffn_router_bias, L0_ffn_ew1, L0_ffn_eb1, L0_ffn_ew2, L0_ffn_eb2, L0_ffn_ew3, L0_ffn_eb3, L0_ffn_sw1, L0_ffn_sb1, L0_ffn_sw2, L0_ffn_sb2, L0_ffn_sw3, L0_ffn_sb3))
    x = x + s * g
    return x

_drawn_inputs = setup_inputs


def setup_inputs(seed=0):
    import zlib

    import numpy as np

    out = dict(_drawn_inputs(seed))
    spreads = {}
    factors = {}
    for name, (base, spread) in spreads.items():
        noise = np.random.default_rng([zlib.crc32(name.encode()), seed]).standard_normal(out[name].shape)
        drawn = base * np.exp(spread * noise) if base else spread * noise
        out[name] = jnp.asarray(drawn.astype(out[name].dtype))
    for name, factor in factors.items():
        out[name] = (out[name] * factor).astype(out[name].dtype)
    return out
```

```python
from contextlib import ExitStack

import concourse.bass as bass
from concourse import mybir

F32 = mybir.dt.float32
BF16 = mybir.dt.bfloat16
I32 = mybir.dt.int32
ALU = mybir.AluOpType
ACT = mybir.ActivationFunctionType
AX_X = mybir.AxisListType.X

P = 128
EPS = 1e-5
GROUPS, GROUP_LIMIT, TOP_K = 4, 2, 2
KEEP_FACTOR = 0.5
BIG = 3e38
BANK = 512


def gated_block_kernel(nc, x, w_gate_t, w_up_t, w_down_t, router_w, router_b, router_bias, expert_w12,
                       expert_w3b, expert_b3, shared_w12, shared_b12, shared_w3, shared_b3, out):
    T, H = x.shape
    I = w_gate_t.shape[1]
    E = router_w.shape[1]
    M = P
    SM = shared_w3.shape[0]
    NT = T // P
    HC = H // P
    IC = -(-I // P)
    I_LAST = I - (IC - 1) * P
    SC = SM // P
    N_DROP = int(KEEP_FACTOR * I)
    PER_GROUP = E // GROUPS
    FULL = T * TOP_K // P
    SLOT_TILES = FULL + E
    SLOTS = SLOT_TILES * P
    PAIRS, FULL_PAIRS = SLOT_TILES // 2, FULL // 2
    W12 = 2 * HC * M
    W3B = H + 2
    PIECES = [(a, min(a + BANK, I)) for a in range(0, I, BANK)]
    NP_ = len(PIECES)
    HALF = NT // 2
    BITS = 31
    ROUNDS = 7
    WINDOW = 7
    CHUNKS = [(k * P, min((k + 1) * P, I)) for k in range(IC)]
    assert H == BANK and FULL % 2 == 0 and E % 2 == 0 and T == 8 * P and I % 2 == 0

    with ExitStack() as ctx:
        def sb(name, shape, dt=F32):
            return ctx.enter_context(nc.sbuf_tensor(name, shape, dt))

        def sem(name):
            return ctx.enter_context(nc.semaphore(name))

        bank = [ctx.enter_context(nc.psum_tensor(f"bank{i}", [P, BANK], F32)) for i in range(8)]

        xn_rows = nc.dram_tensor("xn_rows", [T, H], F32).ap()
        slot_token_dram = nc.dram_tensor("slot_token_dram", [SLOTS, 1], I32).ap()
        slot_y = nc.dram_tensor("slot_y", [SLOTS, H], F32).ap()

        wgd = sb("wgd", [P, max(HC * I, IC * H)])
        wg = wgd[:, 0:HC * I].rearrange("p (k n) -> p k n", k=HC)
        wd = wgd[:, 0:IC * H].rearrange("p (k n) -> p k n", k=IC)
        wu = sb("wu", [P, HC, I])
        sw12 = sb("sw12", [P, 2 * HC, SM])
        sw3 = sb("sw3", [P, SC, H])
        sb12 = sb("sb12", [P, 2 * SC])
        rw = sb("rw", [P, HC, E])
        b3_all = sb("b3_all", [E + 1, H])
        rb_all = sb("rb_all", [P, 2, E])
        w12 = sb("w12", [P, 2, W12])
        w3b = sb("w3b", [P, 2, W3B])

        x_in = wu[:].rearrange("p k n -> p (k n)")[:, 0:NT * H].rearrange("p (t h) -> p t h", t=NT)
        xnT = sb("xnT", [P, HC, T])
        s = sb("s", [P, NT, I])
        mag_rows = sb("mag_rows", [P, HALF * I])
        mag = mag_rows[:].rearrange("p (t n) -> p t n", t=HALF)
        xn = mag_rows[:, 0:NT * H].rearrange("p (t h) -> p t h", t=NT)
        x_end = sb("x_end", [P, 2, H])
        shT = sb("shT", [P, SC, T])
        gateT = sb("gateT", [E + 1, T])
        ident = sb("ident", [P, P])
        before = sb("before", [P, P])
        ones = sb("ones", [P, P])
        zero1 = sb("zero1", [P, 1])

        stats = sb("stats", [P, NT, 6])
        mv = sb("mv", [P, NT, 2])
        ln = sb("ln", [P, 3, NT])

        sc_t = sb("sc_t", [P, NT, E])
        spare = sb("spare", [P, 4 * NT * E + SLOT_TILES * E])
        table = lambda n: spare[:, n * NT * E:(n + 1) * NT * E].rearrange("p (t e) -> p t e", t=NT)
        ex_t = table(0)
        tmp_t = sb("tmp_t", [P, NT, E])
        msk_t = table(1)
        pick = [sb(f"pick{k}", [P, NT, E]) for k in range(TOP_K)]
        hits = sb("hits", [P, NT, E])
        pos_t = table(2)
        tot_t = table(3)
        run_t = sb("run_t", [P, E])
        tiles_i = sb("tiles_i", [P, E], I32)
        tiles_f = sb("tiles_f", [P, E])
        tiles_end = sb("tiles_end", [P, E])
        first_tile = sb("first_tile", [P, E])
        gm = sb("gm", [P, NT, GROUPS])
        gtmp = sb("gtmp", [P, NT, GROUPS])
        gpick = [sb(f"gpick{k}", [P, NT, GROUPS]) for k in range(GROUP_LIMIT)]
        red = sb("red", [P, NT])
        red2 = sb("red2", [P, NT])
        val = [sb(f"val{k}", [P, NT]) for k in range(TOP_K)]
        gates = sb("gates", [P, NT, E + 1])
        rank_e = sb("rank_e", [P, E])
        iota_j = sb("iota_j", [P, SLOT_TILES])
        iota_i = sb("iota_i", [P, SLOT_TILES], I32)
        te_cmp = spare[:, 4 * NT * E:4 * NT * E + SLOT_TILES * E].rearrange("p (j e) -> p j e", e=E)
        te_f = sb("te_f", [P, SLOT_TILES])
        tile_expert = sb("tile_expert", [P, SLOT_TILES], I32)
        slot_f = sb("slot_f", [P, NT])
        slot_of = [sb(f"slot_of{k}", [P, NT], I32) for k in range(TOP_K)]
        slot_blk = sb("slot_blk", [P, NT], I32)
        slot_bf = sb("slot_bf", [P, NT])
        list_at = [sb(f"list_at{k}", [P, NT], I32) for k in range(TOP_K)]
        extra_pairs = sb("extra_pairs", [P, 1], I32)
        token_no = sb("token_no", [P, NT], I32)
        zero_list = sb("zero_list", [P, SLOT_TILES], I32)
        slot_token = sb("slot_token", [P, SLOT_TILES], I32)

        low = [sb(f"low{h}", [P, 2, HALF]) for h in range(2)]
        high = [sb(f"high{h}", [P, 2, HALF]) for h in range(2)]
        cur = [sb(f"cur{h}", [P, 2, HALF]) for h in range(2)]
        sums = [sb(f"sums{h}", [P, HALF]) for h in range(2)]
        signs = [sb(f"signs{h}", [P, HALF]) for h in range(2)]
        span = sb("span", [P, 2, HALF])
        step_a = sb("step_a", [P, HALF])
        step_b = sb("step_b", [P, HALF])
        top8 = sb("top8", [P, HALF, 8])
        hit8 = sb("hit8", [P, HALF, 8])
        kept = sb("kept", [P, HALF])
        bad = sb("bad", [P, 1])
        bad_all = sb("bad_all", [P, 1])
        bad_i = [sb(f"bad_i{h}", [P, 1], I32) for h in range(2)]
        cnt = sb("cnt", [P, HALF])
        thr = sb("thr", [P, HALF], I32)
        cand = sb("cand", [P, HALF], I32)
        add = sb("add", [P, HALF], I32)
        bit_f = sb("bit_f", [P, 1])
        bit_i = sb("bit_i", [P, 1], I32)
        need = sb("need", [P, HALF])
        work = sb("work", [P, I])
        junk = work[:].bitcast(BF16)[:, 0:I]
        eq = work[:].bitcast(BF16)[:, I:2 * I]
        act_junk = sb("act_junk", [P, I], BF16)
        ties = act_junk[:].bitcast(mybir.dt.int16)

        xg = sb("xg", [P, 2, H])
        xgT = sb("xgT", [P, 2, H])
        sil = sb("sil", [P, 2, P])
        hT = sb("hT", [P, 2, P])
        y_sb = sb("y_sb", [P, 2, H])
        ssil = y_sb

        sdT = w12[:].rearrange("p b n -> p (b n)")[:, 0:IC * P]
        yk = [xg, xgT]
        mix_g = sb("mix_g", [P, 2, H])
        mix, g = mix_g[:, 0, :], mix_g[:, 1, :]
        o_sb = y_sb

        names = """const_ready x_loaded0 x_loaded1 router_loaded gate_w_loaded shared_loaded up_w_loaded down_w_loaded
            ln_var ln_root xn_ready xn_stored xnT_psum xnT_ready logits_ready exp_in exp_out picks_ready
            rank_ready gates_ready gateT_psum gateT_ready lists_ready list_zeroed list_scattered list_loaded
            gate_psum s_ready thr_ready0 thr_ready1 act_counted0 act_counted1 bad_ready0 bad_ready1
            bad_summed0 bad_summed1 fall_step0 fall_step1 s_masked
            shared_psum ssil_ready shT_ready
            w12_loaded0 w12_loaded1 w3b_loaded0 w3b_loaded1 xg_loaded0 xg_loaded1 xgT_psum xgT_ready
            h_psum sil_ready hT_ready y_psum y_ready y_stored0 y_stored1 all_y_stored y_zero y_zeroed
            up_psum su_ready sdT_psum sdT_ready down_psum z_psum yk_loaded0 yk_loaded1
            x_again0 x_again1 mix_ready g_ready o_ready out_stored0 out_stored1 dve_step""".split()
        S = {n: sem(n) for n in names}
        pair_of = lambda n: [S[n + "0"], S[n + "1"]]
        x_loaded, out_stored, yk_loaded = pair_of("x_loaded"), pair_of("out_stored"), pair_of("yk_loaded")
        w12_loaded, w3b_loaded, xg_loaded = pair_of("w12_loaded"), pair_of("w3b_loaded"), pair_of("xg_loaded")
        y_stored, x_again = pair_of("y_stored"), pair_of("x_again")
        thr_ready, act_counted = pair_of("thr_ready"), pair_of("act_counted")
        bad_ready, bad_summed, fall_step = pair_of("bad_ready"), pair_of("bad_summed"), pair_of("fall_step")

        def extra(eng):
            eng.wait_ge(S["lists_ready"], 1)
            return eng.value_load(extra_pairs[0:1, 0:1], min_val=0, max_val=PAIRS - FULL_PAIRS)

        block = ctx.enter_context(nc.Block())

        @block.sync
        def _(sp):
            for b in range(2):
                sp.dma_start(x_in[:, b * HALF:(b + 1) * HALF, :],
                             x[b * HALF * P:(b + 1) * HALF * P, :].rearrange("(t p) n -> p t n", p=P)
                             ).then_inc(x_loaded[b], 16)
            sp.dma_start(rw[:], router_w.rearrange("(k p) e -> p k e", p=P)).then_inc(S["router_loaded"], 16)
            sp.dma_start(rb_all[:, 0, :], router_b.broadcast_to([P, E])).then_inc(S["router_loaded"], 16)
            sp.dma_start(rb_all[:, 1, :], router_bias.broadcast_to([P, E])).then_inc(S["router_loaded"], 16)
            sp.dma_start(wg, w_gate_t.rearrange("(k p) n -> p k n", p=P)).then_inc(S["gate_w_loaded"], 16)
            sp.wait_ge(S["xn_ready"], NT)
            sp.dma_start(xn_rows.rearrange("(t p) n -> p t n", p=P), xn).then_inc(S["xn_stored"], 16)
            sp.dma_start(sw12[:], shared_w12.rearrange("(k p) n -> p k n", p=P)).then_inc(S["shared_loaded"], 16)
            sp.dma_start(sw3[:], shared_w3.rearrange("(k p) n -> p k n", p=P)).then_inc(S["shared_loaded"], 16)
            sp.dma_start(sb12[:], shared_b12).then_inc(S["shared_loaded"], 16)
            sp.dma_start(b3_all[0:E, :], expert_b3).then_inc(S["shared_loaded"], 16)
            sp.dma_start(b3_all[E:E + 1, :], shared_b3).then_inc(S["shared_loaded"], 16)
            sp.dma_start(wu[:], w_up_t.rearrange("(k p) n -> p k n", p=P)).then_inc(S["up_w_loaded"], 16)

            sp.wait_ge(S["y_zero"], 1)
            sp.dma_start(slot_y[FULL * P:SLOTS, :].rearrange("(j p) n -> p j n", p=P),
                         y_sb[:, 0:1, :].to_broadcast([P, SLOT_TILES - FULL, H])).then_inc(S["y_zeroed"], 16)

            def load_w12(j, b):
                e = sp.value_load(tile_expert[0:1, bass.ds(j, 1)], min_val=0, max_val=E - 1)
                sp.dma_start(w12[:, b, :], expert_w12[bass.ds(e * P, P), :]).then_inc(w12_loaded[b], 16)
                return e

            def load_w3b(e, b):
                sp.dma_start(w3b[:, b, :], expert_w3b[bass.ds(e * P, P), :]).then_inc(w3b_loaded[b], 16)

            def store_y(j, b):
                sp.dma_start(slot_y[bass.ds(j * P, P), :], y_sb[:, b, :]).then_inc(y_stored[b], 16)

            def next_pair(p):
                for b in range(2):
                    j = p * 2 + b
                    sp.wait_ge(S["h_psum"], j - 1)
                    e = load_w12(j, b)
                    sp.wait_ge(S["y_psum"], j - 1)
                    load_w3b(e, b)
                    sp.wait_ge(S["y_ready"], j - 1)
                    store_y(j - 2, b)

            n_extra = extra(sp)
            for b in range(2):
                load_w3b(load_w12(b, b), b)
            with sp.Fori(1, FULL_PAIRS) as p:
                next_pair(p)
            sp.wait_ge(S["gate_psum"], NT * NP_)
            sp.dma_start(wd[:, 0:IC - 1, :], w_down_t[0:(IC - 1) * P, :].rearrange("(k p) n -> p k n", p=P)
                         ).then_inc(S["down_w_loaded"], 16)
            sp.dma_start(wd[0:I_LAST, IC - 1, :], w_down_t[(IC - 1) * P:I, :]).then_inc(S["down_w_loaded"], 16)
            with sp.Fori(0, PAIRS - FULL_PAIRS) as q:
                with sp.If(q < n_extra):
                    next_pair(q + FULL_PAIRS)
            last = n_extra * 2 + FULL
            for b in range(2):
                sp.wait_ge(S["y_ready"], last - 1 + b)
                store_y(last - 2 + b, b)
            for b in range(2):
                sp.wait_ge(y_stored[b], (n_extra + FULL_PAIRS) * 16)
            sp.sem_inc(S["all_y_stored"], 1)

            for t in range(2):
                sp.dma_start(x_end[:, t, :], x[t * P:(t + 1) * P, :]).then_inc(x_again[t], 16)
            for t in range(NT):
                sp.wait_ge(S["o_ready"], t + 1)
                sp.dma_start(out[t * P:(t + 1) * P, :], o_sb[:, t % 2, :]).then_inc(out_stored[t % 2], 16)
                if t + 2 < NT:
                    sp.dma_start(x_end[:, t % 2, :], x[(t + 2) * P:(t + 3) * P, :]).then_inc(x_again[t % 2], 16)
            for b in range(2):
                sp.wait_ge(out_stored[b], 16 * (NT // 2))

        @block.gpsimd
        def _(pool):
            pool.memset(y_sb[:, 0, :], 0.0).then_inc(S["y_zero"], 1)
            pool.memset(ident[:], 0.0).then_inc(S["const_ready"], 1)
            pool.memset(ones[:], 1.0).then_inc(S["const_ready"], 1)
            pool.memset(zero1[:], 0.0).then_inc(S["const_ready"], 1)
            pool.memset(zero_list[:], 0).then_inc(S["const_ready"], 1)
            pool.iota(token_no[:], [[P, NT]], base=0, channel_multiplier=1).then_inc(S["const_ready"], 1)
            pool.iota(iota_i[:], [[1, SLOT_TILES]], base=0, channel_multiplier=0).then_inc(S["const_ready"], 1)
            pool.memset(gates[:, :, E:E + 1], 1.0).then_inc(S["const_ready"], 1)
            pool.wait_ge(S["const_ready"], 7)
            pool.affine_select(out=ident[:], in_=ident[:], compare_op=ALU.not_equal, fill=1.0, base=0,
                               pattern=[[-1, P]], channel_multiplier=1).then_inc(S["const_ready"], 1)
            pool.affine_select(out=before[:], in_=ones[:], compare_op=ALU.is_gt, fill=0.0, base=0,
                               pattern=[[1, P]], channel_multiplier=-1).then_inc(S["const_ready"], 1)
            list_view = slot_token_dram.rearrange("(p j) a -> p (j a)", p=P)
            pool.dma_start(list_view, zero_list[:]).then_inc(S["list_zeroed"], 16)

            pool.wait_ge(S["list_zeroed"], 16)
            n_extra = extra(pool)
            for t in range(NT):
                for k in range(TOP_K):
                    pool.indirect_dma_start(
                        out=slot_token_dram, out_offset=bass.IndirectOffsetOnAxis(ap=list_at[k][:, t:t + 1], axis=0),
                        in_=token_no[:, t:t + 1], in_offset=None).then_inc(S["list_scattered"], 16)
            pool.wait_ge(S["list_scattered"], 16 * NT * TOP_K)
            pool.dma_start(slot_token[:], list_view).then_inc(S["list_loaded"], 16)
            pool.wait_ge(S["list_loaded"], 16)
            pool.wait_ge(S["xn_stored"], 16)

            def gather_tokens(j):
                if j >= 2:
                    pool.wait_ge(S["xgT_psum"], j - 1)
                pool.indirect_dma_start(
                    out=xg[:, j % 2, :], out_offset=None, in_=xn_rows,
                    in_offset=bass.IndirectOffsetOnAxis(ap=slot_token[:, j:j + 1], axis=0)
                ).then_inc(xg_loaded[j % 2], 16)

            def sum_bad(h):
                pool.wait_ge(bad_ready[h], 1)
                pool.partition_all_reduce(bad_all[:], bad[:], P, bass.bass_isa.ReduceOp.add).then_inc(bad_summed[h], 1)

            for j in range(FULL):
                gather_tokens(j)
                if j == 1:
                    sum_bad(0)
            for q in range(PAIRS - FULL_PAIRS):
                with pool.If(n_extra > q):
                    for b in range(2):
                        gather_tokens(FULL + 2 * q + b)

            pool.wait_ge(S["all_y_stored"], 1)
            for t in range(NT):
                if t >= 2:
                    pool.wait_ge(S["mix_ready"], t - 1)
                for k in range(TOP_K):
                    pool.indirect_dma_start(
                        out=yk[k][:, t % 2, :], out_offset=None, in_=slot_y,
                        in_offset=bass.IndirectOffsetOnAxis(ap=slot_of[k][:, t:t + 1], axis=0)
                    ).then_inc(yk_loaded[t % 2], 16)
                if t == HALF - 1:
                    sum_bad(1)

        @block.scalar
        def _(act):
            def silu_gate(t):
                for c, (a, b) in enumerate(PIECES):
                    act.wait_ge(S["gate_psum"], t * NP_ + c + 1)
                    nc.scalar.activation(s[:, t, a:b], bank[c][:, 0:b - a], ACT.Silu).then_inc(S["s_ready"], 1)

            def count_tile(h, i, n_round):
                act.wait_ge(thr_ready[h], n_round + 1)
                act.wait_ge(act_counted[h], (n_round * 2) + i - HALF // 2)
                nc.scalar.activation(act_junk[:], mag[:, i, :], ACT.Sign, bias=cur[h][:, 0, i:i + 1], scale=-1.0,
                                     accum_out=signs[h][:, i:i + 1]).then_inc(act_counted[h], 1)

            def count_first(h):
                act.wait_ge(thr_ready[h], 1)
                nc.scalar.activation(act_junk[:], mag[:, 2, :], ACT.Sign, bias=cur[h][:, 0, 2:3], scale=-1.0,
                                     accum_out=signs[h][:, 2:3]).then_inc(act_counted[h], 1)
                count_tile(h, 3, 0)

            for b in range(2):
                act.wait_ge(S["ln_var"], b + 1)
                nc.scalar.activation(ln[:, 1, b * HALF:(b + 1) * HALF], ln[:, 0, b * HALF:(b + 1) * HALF],
                                     ACT.Sqrt).then_inc(S["ln_root"], 1)
            for t in range(NT):
                act.wait_ge(S["xnT_psum"], t + 1)
                nc.scalar.activation(xnT[:, :, t * P:(t + 1) * P], bank[6 + t % 2][:].rearrange("p (k m) -> p k m", k=HC),
                                     ACT.Copy).then_inc(S["xnT_ready"], 1)
            act.wait_ge(S["exp_in"], 1)
            nc.scalar.activation(ex_t, tmp_t[:], ACT.Exp).then_inc(S["exp_out"], 1)
            for t in range(HALF):
                silu_gate(t)
            count_round = 0
            for t in range(HALF, NT):
                silu_gate(t)
                for _ in range(2):
                    if count_round == 0:
                        count_first(0)
                    elif count_round < ROUNDS:
                        for i in (2, 3):
                            count_tile(0, i, count_round)
                    count_round += 1

            act.wait_ge(S["y_zeroed"], 16)
            act.wait_ge(S["shared_loaded"], 16 * 5)
            for u in range(2 * SC):
                c = u // 2
                act.wait_ge(S["shared_psum"], 2 * u + 1)
                if u >= 2:
                    act.wait_ge(S["shT_ready"], u - 1)
                nc.scalar.activation(ssil[:, u % 2, :], bank[(3, 6)[u % 2]][:], ACT.Silu,
                                     bias=sb12[:, c:c + 1]).then_inc(S["ssil_ready"], 1)

            def copy_xgT(j, b):
                act.wait_ge(S["xgT_psum"], j + 1)
                nc.scalar.activation(xgT[:, b, :], bank[b][:], ACT.Copy).then_inc(S["xgT_ready"], 1)

            def silu_h(j, b, loaded):
                act.wait_ge(w3b_loaded[b], loaded)
                act.wait_ge(S["h_psum"], j + 1)
                nc.scalar.activation(sil[:, b, :], bank[2 + b][:, 0:P], ACT.Silu,
                                     bias=w3b[:, b, H:H + 1]).then_inc(S["sil_ready"], 1)

            def copy_y(j, b, stored):
                act.wait_ge(S["y_psum"], j + 1)
                if stored is not None:
                    act.wait_ge(y_stored[b], stored)
                nc.scalar.activation(y_sb[:, b, :], bank[4 + b][:], ACT.Copy).then_inc(S["y_ready"], 1)

            def pair(p, count=None):
                for b in range(2):
                    copy_xgT(p * 2 + b, b)
                copy_y(p * 2 - 1, 1, p * 16 - 16)
                for b in range(2):
                    if count is not None:
                        count_tile(1, 2 + b, count)
                    silu_h(p * 2 + b, b, p * 16 + 16)
                copy_y(p * 2, 0, p * 16)

            n_extra = extra(act)
            for p in range(2):
                for b in range(2):
                    copy_xgT(p * 2 + b, b)
                if p == 1:
                    copy_y(1, 1, None)
                for b in range(2):
                    silu_h(p * 2 + b, b, p * 16 + 16)
                copy_y(p * 2, 0, 16 * p or None)
            act.wait_ge(y_stored[0], 16)
            count_first(1)
            with act.Fori(2, FULL_PAIRS) as p:
                pair(p, p - 1)
            with act.Fori(0, PAIRS - FULL_PAIRS) as q:
                with act.If(q < n_extra):
                    pair(q + FULL_PAIRS)
            act.wait_ge(S["y_psum"], n_extra * 2 + FULL)
            act.wait_ge(y_stored[1], n_extra * 16 + (FULL_PAIRS - 1) * 16)
            nc.scalar.activation(y_sb[:, 1, :], bank[5][:], ACT.Copy).then_inc(S["y_ready"], 1)

            for t in range(NT):
                for q in range(3):
                    n = min(4, IC - 4 * q)
                    act.wait_ge(S["sdT_psum"], 3 * t + q + 1)
                    if t >= 1 and q == 0:
                        act.wait_ge(S["down_psum"], t)
                    nc.scalar.activation(sdT[:, 4 * q * P:(4 * q + n) * P], bank[3 + q][:, 0:n * P],
                                         ACT.Copy).then_inc(S["sdT_ready"], 1)
                act.wait_ge(S["mix_ready"], t + 1)
                if t >= 1:
                    act.wait_ge(S["o_ready"], t)
                nc.scalar.activation(g, mix, ACT.Silu).then_inc(S["g_ready"], 1)

        @block.vector
        def _(dve):
            V = nc.vector
            steps = [0]

            def step(ins):
                steps[0] += 1
                ins.then_inc(S["dve_step"], 1)
                dve.wait_ge(S["dve_step"], steps[0])

            def link(ins, sem_, at):
                ins.then_inc(sem_, 1)
                dve.wait_ge(sem_, at)

            for b in range(2):
                dve.wait_ge(x_loaded[b], 16)
                for t in range(b * HALF, (b + 1) * HALF):
                    step(V.bn_stats(stats[:, t, :], x_in[:, t, :]))
                    step(V.bn_aggr(mv[:, t, :], stats[:, t, :]))
                V.tensor_scalar(ln[:, 0, b * HALF:(b + 1) * HALF], mv[:, b * HALF:(b + 1) * HALF, 1], EPS, None,
                                ALU.add).then_inc(S["ln_var"], 1)
            for b in range(2):
                var, r, u = (ln[:, q, b * HALF:(b + 1) * HALF] for q in range(3))
                dve.wait_ge(S["ln_root"], b + 1)
                step(V.reciprocal(r, r))
                step(V.tensor_tensor(u, r, r, ALU.mult))
                step(V.tensor_tensor(u, u, var, ALU.mult))
                step(V.tensor_scalar(u, u, -0.5, 1.5, ALU.mult, ALU.add))
                step(V.tensor_tensor(r, r, u, ALU.mult))
                for t in range(b * HALF, (b + 1) * HALF):
                    V.tensor_scalar(xn[:, t, :], x_in[:, t, :], mv[:, t, 0:1], ln[:, 1, t:t + 1], ALU.subtract,
                                    ALU.mult).then_inc(S["xn_ready"], 1)

            dve.wait_ge(S["const_ready"], 9)
            dve.wait_ge(S["router_loaded"], 16 * 3)
            step(V.tensor_scalar(rank_e[:], iota_i[:, 0:E], -1.0, float(E), ALU.mult, ALU.add))
            step(V.tensor_copy(iota_j[:], iota_i[:]))
            dve.wait_ge(S["logits_ready"], 1)
            lg = bank[5][:, 0:NT * E].rearrange("p (t e) -> p t e", t=NT)
            over_t = lambda v: v[:, None, :].to_broadcast([P, NT, E])
            over_e = lambda v, n=E: v[:, :, None].to_broadcast([P, NT, n])
            step(V.tensor_tensor(sc_t[:], lg, over_t(rb_all[:, 0, :]), ALU.add))
            step(V.tensor_reduce(red[:], sc_t[:], AX_X, ALU.max))
            V.tensor_tensor(tmp_t[:], sc_t[:], over_e(red[:]), ALU.subtract).then_inc(S["exp_in"], 1)
            dve.wait_ge(S["exp_out"], 1)
            step(V.tensor_reduce(red[:], ex_t, AX_X, ALU.add))
            step(V.reciprocal(red[:], red[:]))
            step(V.tensor_tensor(sc_t[:], ex_t, over_e(red[:]), ALU.mult))
            step(V.tensor_tensor(sc_t[:], sc_t[:], over_t(rb_all[:, 1, :]), ALU.add))

            def first_max(onehot, table, tmp, n):
                weight = rank_e[:, E - n:E]
                w = weight[:, None, :].to_broadcast([P, NT, n])
                step(V.tensor_reduce(red[:], table, AX_X, ALU.max))
                step(V.tensor_tensor(tmp, table, over_e(red[:], n), ALU.is_equal))
                step(V.tensor_tensor(tmp, tmp, w, ALU.mult))
                step(V.tensor_reduce(red2[:], tmp, AX_X, ALU.max))
                step(V.tensor_tensor(onehot, w, over_e(red2[:], n), ALU.is_equal))

            step(V.tensor_reduce(gm[:], sc_t[:].rearrange("p t (g e) -> p t g e", g=GROUPS), AX_X, ALU.max))
            first_max(gpick[0][:], gm[:], gtmp[:], GROUPS)
            step(V.scalar_tensor_tensor(gm[:], gpick[0][:], -BIG, gm[:], ALU.mult, ALU.add))
            first_max(gpick[1][:], gm[:], gtmp[:], GROUPS)
            step(V.tensor_tensor(gtmp[:], gpick[0][:], gpick[1][:], ALU.add))
            step(V.tensor_scalar(gtmp[:], gtmp[:], BIG, -BIG, ALU.mult, ALU.add))
            step(V.tensor_tensor(msk_t.rearrange("p t (g e) -> p t g e", g=GROUPS),
                                 sc_t[:].rearrange("p t (g e) -> p t g e", g=GROUPS),
                                 gtmp[:, :, :, None].to_broadcast([P, NT, GROUPS, PER_GROUP]), ALU.add))
            first_max(pick[0][:], msk_t, tmp_t[:], E)
            step(V.scalar_tensor_tensor(msk_t, pick[0][:], -BIG, msk_t, ALU.mult, ALU.add))
            first_max(pick[1][:], msk_t, tmp_t[:], E)
            V.tensor_tensor(hits[:], pick[0][:], pick[1][:], ALU.add).then_inc(S["picks_ready"], 1)
            for k in range(TOP_K):
                step(V.tensor_tensor(tmp_t[:], pick[k][:], sc_t[:], ALU.mult))
                step(V.tensor_reduce(val[k][:], tmp_t[:], AX_X, ALU.add))
            step(V.tensor_tensor(tmp_t[:], pick[0][:], over_e(val[0][:]), ALU.mult))
            step(V.tensor_tensor(msk_t, pick[1][:], over_e(val[1][:]), ALU.mult))
            V.tensor_tensor(gates[:, :, 0:E], tmp_t[:], msk_t, ALU.add).then_inc(S["gates_ready"], 1)

            dve.wait_ge(S["rank_ready"], 1)
            rank_ps = bank[5][:, P:2 * P].rearrange("p (t e) -> p t e", t=NT)
            total_ps = bank[5][:, 2 * P:3 * P].rearrange("p (t e) -> p t e", t=NT)
            step(V.tensor_copy(tot_t, total_ps))
            step(V.memset(run_t[:], 0.0))
            for t in range(NT):
                step(V.tensor_tensor(pos_t[:, t, :], run_t[:], rank_ps[:, t, :], ALU.add))
                step(V.tensor_tensor(run_t[:], run_t[:], tot_t[:, t, :], ALU.add))
            step(V.tensor_scalar(tiles_i[:], run_t[:], float(P - 1), None, ALU.add))
            step(V.tensor_scalar(tiles_i[:], tiles_i[:], P.bit_length() - 1, None, ALU.arith_shift_right))
            step(V.tensor_copy(tiles_f[:], tiles_i[:]))
            step(V.tensor_tensor_scan(tiles_end[:], zero1[:].to_broadcast([P, E]), tiles_f[:], 0.0, ALU.add, ALU.add))
            step(V.tensor_tensor(first_tile[:], tiles_end[:], tiles_f[:], ALU.subtract))
            step(V.tensor_scalar(run_t[:], first_tile[:], float(P), None, ALU.mult))
            step(V.tensor_tensor(pos_t, pos_t, over_t(run_t[:]), ALU.add))
            for k in range(TOP_K):
                step(V.tensor_tensor(tmp_t[:], pick[k][:], pos_t, ALU.mult))
                step(V.tensor_reduce(slot_f[:], tmp_t[:], AX_X, ALU.add))
                step(V.tensor_copy(slot_of[k][:], slot_f[:]))
                step(V.tensor_scalar(slot_blk[:], slot_of[k][:], P.bit_length() - 1, None, ALU.arith_shift_right))
                step(V.tensor_copy(slot_bf[:], slot_blk[:]))
                step(V.tensor_scalar(slot_f[:], slot_f[:], float(SLOT_TILES), None, ALU.mult))
                step(V.scalar_tensor_tensor(list_at[k][:], slot_bf[:], float(1 - P * SLOT_TILES), slot_f[:],
                                            ALU.mult, ALU.add))
            step(V.tensor_scalar(extra_pairs[:], tiles_end[:, E - 1:E], float(1 - FULL), None, ALU.add))
            step(V.tensor_scalar(extra_pairs[:], extra_pairs[:], 1, None, ALU.arith_shift_right))
            step(V.tensor_tensor(te_cmp, first_tile[:, None, :].to_broadcast([P, SLOT_TILES, E]),
                                 iota_j[:, :, None].to_broadcast([P, SLOT_TILES, E]), ALU.is_le))
            step(V.tensor_reduce(te_f[:], te_cmp, AX_X, ALU.add))
            V.tensor_scalar(tile_expert[:], te_f[:], -1.0, None, ALU.add).then_inc(S["lists_ready"], 1)
            dve.wait_ge(S["gateT_psum"], 1)
            for q in range(2):
                ins = V.tensor_copy(gateT[:, q * BANK:(q + 1) * BANK], bank[6 + q][0:E + 1, :])
            ins.then_inc(S["gateT_ready"], 1)

            def magnitude(h, i):
                t = h * HALF + i
                dve.wait_ge(S["s_ready"], NP_ * (t + 1))
                step(V.scalar_tensor_tensor(mag[:, i, :], s[:, t, :], -1.0, s[:, t, :], ALU.mult, ALU.max,
                                            accum_out=sums[h][:, i:i + 1]))

            def search_start(h):
                step(V.memset(low[h][:], 0.0))
                step(V.memset(high[h][:], 0.9 * I))
                step(V.tensor_scalar(high[h][:, 0, :], sums[h][:], 2.001 / I, None, ALU.mult))
                V.tensor_scalar(cur[h][:, 0, :], sums[h][:], 0.79 / I, None, ALU.mult).then_inc(thr_ready[h], 1)
                dve.wait_ge(thr_ready[h], 1)

            def count(h, i, at=None):
                ins = V.tensor_scalar(junk, mag[:, i, :], cur[h][:, 0, i:i + 1], None, ALU.is_le, ALU.add,
                                      accum_out=cur[h][:, 1, i:i + 1])
                step(ins) if at is None else link(ins, S["dve_step"], at)

            def narrow(h, n_round, at=None):
                n = [0]

                def done(ins):
                    n[0] += 1
                    step(ins) if at is None else link(ins, S["dve_step"], at + n[0])

                dve.wait_ge(act_counted[h], n_round * 2 + 2)
                done(V.tensor_scalar(cur[h][:, 1, 2:4], signs[h][:, 2:4], 0.5, 0.5 * I, ALU.mult, ALU.add))
                c = cur[h][:, 1:2, :].to_broadcast([P, 2, HALF])
                done(V.scalar_tensor_tensor(span[:], c, float(N_DROP + WINDOW), cur[h][:], ALU.is_le, ALU.mult))
                done(V.tensor_tensor(low[h][:], low[h][:], span[:], ALU.max))
                done(V.tensor_scalar(span[:], c, float(N_DROP), BIG, ALU.is_lt, ALU.mult))
                done(V.tensor_tensor(span[:], span[:], cur[h][:], ALU.max))
                done(V.tensor_tensor(high[h][:], high[h][:], span[:], ALU.min))
                done(V.tensor_tensor(span[:], high[h][:], low[h][:], ALU.subtract))
                done(V.tensor_scalar(step_a[:], span[:, 1, :], 1.0, None, ALU.add))
                done(V.reciprocal(step_a[:], step_a[:]))
                done(V.scalar_tensor_tensor(step_b[:], low[h][:, 1, :], -(N_DROP + 0.5 * WINDOW + 0.75), span[:, 0, :],
                                            ALU.add, ALU.mult))
                done(V.tensor_tensor(step_b[:], step_b[:], step_a[:], ALU.mult))
                V.tensor_tensor(cur[h][:, 0, :], low[h][:, 0, :], step_b[:], ALU.subtract).then_inc(thr_ready[h], 1)
                dve.wait_ge(thr_ready[h], n_round + 2)

            NARROW = 11

            def largest_counted(h, i):
                step(V.scalar_tensor_tensor(work[:], mag[:, i, :], low[h][:, 0, i:i + 1], mag[:, i, :], ALU.is_le, ALU.mult))
                step(V.max(top8[:, i, :], work[:]))

            def exact_threshold(h):
                step(V.tensor_scalar(step_a[:], low[h][:, 1, :], -float(N_DROP), None, ALU.add))
                step(V.tensor_tensor(hit8[:], iota_j[:, None, 0:8].to_broadcast([P, HALF, 8]),
                                     step_a[:, :, None].to_broadcast([P, HALF, 8]), ALU.is_equal))
                step(V.tensor_tensor(hit8[:], hit8[:], top8[:], ALU.mult))
                step(V.tensor_reduce(step_b[:], hit8[:], AX_X, ALU.add))

            def mask(h, i):
                step(V.tensor_scalar(mag[:, i, :], mag[:, i, :], step_b[:, i:i + 1], None, ALU.is_gt, ALU.add,
                                     accum_out=kept[:, i:i + 1]))

            def check_counts(h):
                step(V.tensor_scalar(step_a[:], kept[:], float(I - N_DROP), None, ALU.not_equal))
                V.tensor_reduce(bad[:], step_a[:], AX_X, ALU.add).then_inc(bad_ready[h], 1)

            def general_search(h):
                dve.wait_ge(bad_summed[h], 1)
                step(V.tensor_copy(bad_i[h][:], bad_all[:]))
                n_bad = dve.value_load(bad_i[h][0:1, 0:1], min_val=0, max_val=T)
                F = fall_step[h]
                with dve.If(n_bad > 0):
                    for i in range(HALF):
                        link(V.scalar_tensor_tensor(mag[:, i, :], s[:, h * HALF + i, :], -1.0, s[:, h * HALF + i, :],
                                                    ALU.mult, ALU.max), F, i + 1)
                    link(V.memset(bit_f[:], float(2 ** (BITS - 1))), F, HALF + 1)
                    link(V.memset(thr[:], 0), F, HALF + 2)
                    with dve.Fori(0, BITS) as bit:
                        at = bit * (HALF + 5) + (HALF + 2)
                        link(V.tensor_copy(bit_i[:], bit_f[:]), F, at + 1)
                        link(V.tensor_tensor(cand[:], thr[:], bit_i[:].to_broadcast([P, HALF]), ALU.bitwise_or), F, at + 2)
                        for i in range(HALF):
                            link(V.tensor_scalar(junk, mag[:, i, :], cand[:, i:i + 1].bitcast(F32), None, ALU.is_lt,
                                                 ALU.add, accum_out=cnt[:, i:i + 1]), F, at + 3 + i)
                        link(V.tensor_scalar(add[:], cnt[:], float(N_DROP), bit_f[:], ALU.is_lt, ALU.mult), F, at + HALF + 3)
                        link(V.tensor_tensor(thr[:], thr[:], add[:], ALU.bitwise_or), F, at + HALF + 4)
                        link(V.tensor_scalar(bit_f[:], bit_f[:], 0.5, None, ALU.mult), F, at + HALF + 5)
                    at = BITS * (HALF + 5) + HALF + 2
                    thr_f = thr[:].bitcast(F32)
                    for i in range(HALF):
                        link(V.tensor_scalar(junk, mag[:, i, :], thr_f[:, i:i + 1], None, ALU.is_lt, ALU.add,
                                             accum_out=cnt[:, i:i + 1]), F, at + 1 + i)
                    at += HALF + 1
                    link(V.tensor_scalar(need[:], cnt[:], -1.0, float(N_DROP), ALU.mult, ALU.add), F, at)
                    for i in range(HALF):
                        th = thr_f[:, i:i + 1]
                        link(V.tensor_scalar(eq, mag[:, i, :], th, None, ALU.is_equal), F, at + 1)
                        link(V.tensor_tensor_scan(ties, zero1[:].to_broadcast([P, I]), eq, 0.0, ALU.add, ALU.add), F, at + 2)
                        link(V.scalar_tensor_tensor(eq, ties, need[:, i:i + 1], eq, ALU.is_gt, ALU.mult), F, at + 3)
                        link(V.scalar_tensor_tensor(mag[:, i, :], mag[:, i, :], th, eq, ALU.is_gt, ALU.add), F, at + 4)
                        at += 4

            def apply_mask(h, i):
                t = h * HALF + i
                V.tensor_tensor(s[:, t, :], s[:, t, :], mag[:, i, :], ALU.mult).then_inc(S["s_masked"], 1)

            dve.wait_ge(S["xn_stored"], 16)
            dve.wait_ge(S["xnT_psum"], NT)
            for i in range(HALF):
                magnitude(0, i)
            search_start(0)
            for n in range(ROUNDS):
                for i in range(2):
                    count(0, i)
                narrow(0, n)

            dve.wait_ge(S["shared_loaded"], 16 * 5)
            for u in range(2 * SC):
                c, half = u // 2, u % 2
                largest_counted(0, u)
                dve.wait_ge(S["ssil_ready"], u + 1)
                dve.wait_ge(S["shared_psum"], 2 * u + 2)
                V.scalar_tensor_tensor(shT[:, c, half * BANK:(half + 1) * BANK], bank[(4, 7)[u % 2]][:],
                                       sb12[:, SC + c:SC + c + 1], ssil[:, u % 2, :],
                                       ALU.add, ALU.mult).then_inc(S["shT_ready"], 1)
            exact_threshold(0)
            for i in range(HALF):
                mask(0, i)
            check_counts(0)

            def mul_h(j, b):
                dve.wait_ge(S["sil_ready"], j + 1)
                V.scalar_tensor_tensor(hT[:, b, :], bank[2 + b][:, P:2 * P], w3b[:, b, H + 1:H + 2],
                                       sil[:, b, :], ALU.add, ALU.mult).then_inc(S["hT_ready"], 1)

            n_extra = extra(dve)
            mul_h(0, 0)
            mul_h(1, 1)
            general_search(0)
            for i in range(HALF):
                apply_mask(0, i)
            dve.wait_ge(S["s_masked"], HALF)
            mul_h(2, 0)
            magnitude(1, 0)
            magnitude(1, 1)
            mul_h(3, 1)
            magnitude(1, 2)
            magnitude(1, 3)
            search_start(1)
            for i in range(2):
                count(1, i)
            narrow(1, 0)
            base = steps[0]
            with dve.Fori(2, FULL_PAIRS) as p:
                at = (p - 2) * (NARROW + 2) + base
                for b in range(2):
                    count(1, b, at + 1 + b)
                    mul_h(p * 2 + b, b)
                narrow(1, p - 1, at + 2)
            steps[0] = base + (FULL_PAIRS - 2) * (NARROW + 2)
            with dve.Fori(0, PAIRS - FULL_PAIRS) as q:
                with dve.If(q < n_extra):
                    for b in range(2):
                        mul_h(q * 2 + (FULL + b), b)

            def multiply_up(t, c):
                a, b = PIECES[c]
                dve.wait_ge(S["up_psum"], t * NP_ + c + 1)
                V.tensor_tensor(s[:, t, a:b], s[:, t, a:b], bank[c][:, 0:b - a], ALU.mult).then_inc(S["su_ready"], 1)

            def finish(t):
                b = t % 2
                dve.wait_ge(yk_loaded[b], 16 * TOP_K * (t // 2 + 1))
                dve.wait_ge(S["z_psum"], t + 1)
                if t >= 1:
                    dve.wait_ge(S["g_ready"], t)
                step(V.scalar_tensor_tensor(mix, yk[0][:, b, :], val[0][:, t:t + 1], bank[7][:], ALU.mult, ALU.add))
                V.scalar_tensor_tensor(mix, yk[1][:, b, :], val[1][:, t:t + 1], mix, ALU.mult,
                                       ALU.add).then_inc(S["mix_ready"], 1)
                dve.wait_ge(S["g_ready"], t + 1)
                dve.wait_ge(S["down_psum"], t + 1)
                if t >= 2:
                    dve.wait_ge(out_stored[b], 16 * (t // 2))
                step(V.tensor_tensor(o_sb[:, b, :], g, bank[6][:], ALU.mult))
                dve.wait_ge(x_again[b], 16 * (t // 2 + 1))
                V.tensor_tensor(o_sb[:, b, :], o_sb[:, b, :], x_end[:, b, :], ALU.add).then_inc(S["o_ready"], 1)

            for t in range(NT):
                for c in range(NP_):
                    multiply_up(t, c)
                    if t < HALF and c == 0:
                        largest_counted(1, t)
                if t == HALF - 1:
                    exact_threshold(1)
                    for i in range(HALF):
                        mask(1, i)
                    check_counts(1)
                if t >= 1:
                    finish(t - 1)
                if t == HALF - 1:
                    general_search(1)
                    for i in range(HALF):
                        apply_mask(1, i)
                    dve.wait_ge(S["s_masked"], NT)
            finish(NT - 1)

        @block.tensor
        def _(pe):
            TE = nc.tensor
            pe.wait_ge(S["const_ready"], 9)
            for t in range(NT):
                pe.wait_ge(S["xn_ready"], t + 1)
                if t >= 2:
                    pe.wait_ge(S["xnT_ready"], t - 1)
                for k in range(HC):
                    ins = TE.transpose(bank[6 + t % 2][:, k * P:(k + 1) * P], xn[:, t, k * P:(k + 1) * P], ident[:])
                ins.then_inc(S["xnT_psum"], 1)
            pe.wait_ge(S["xnT_ready"], NT)
            pe.wait_ge(S["router_loaded"], 16 * 3)
            for t in range(NT):
                for k in range(HC):
                    ins = TE.matmul(bank[5][:, t * E:(t + 1) * E], xnT[:, k, t * P:(t + 1) * P], rw[:, k, :],
                                    start=(k == 0), stop=(k == HC - 1))
            ins.then_inc(S["logits_ready"], 1)

            def project(t, w, done, emptied):
                for c, (a, b) in enumerate(PIECES):
                    if t >= 1:
                        pe.wait_ge(emptied, (t - 1) * NP_ + c + 1)
                    for k in range(HC):
                        ins = TE.matmul(bank[c][:, 0:b - a], xnT[:, k, t * P:(t + 1) * P], w[:, k, a:b],
                                        start=(k == 0), stop=(k == HC - 1))
                    ins.then_inc(done, 1)

            pe.wait_ge(S["gate_w_loaded"], 16)
            for t in range(NT):
                project(t, wg, S["gate_psum"], S["s_ready"])
                if t == 1:
                    pe.wait_ge(S["picks_ready"], 1)
                    flat = hits[:].rearrange("p t e -> p (t e)")
                    TE.matmul(bank[5][:, P:2 * P], before[:], flat, start=True, stop=True)
                    TE.matmul(bank[5][:, 2 * P:3 * P], ones[:], flat, start=True, stop=True).then_inc(S["rank_ready"], 1)
                    pe.wait_ge(S["gates_ready"], 1)
                    for q in range(NT):
                        ins = TE.transpose(bank[6 + q // 4][0:E + 1, (q % 4) * P:(q % 4 + 1) * P], gates[:, q, :], ident[:])
                    ins.then_inc(S["gateT_psum"], 1)

            pe.wait_ge(S["shared_loaded"], 16 * 5)
            pe.wait_ge(S["gateT_ready"], 1)
            for u in range(2 * SC):
                c, half = u // 2, u % 2
                for m in range(2):
                    if u >= 2:
                        pe.wait_ge(S["shT_ready"], u - 1)
                    dst = bank[((3, 4), (6, 7))[u % 2][m]]
                    for k in range(HC):
                        ins = TE.matmul(dst[:], sw12[:, m * HC + k, c * P:(c + 1) * P],
                                        xnT[:, k, half * BANK:(half + 1) * BANK], start=(k == 0), stop=(k == HC - 1))
                    ins.then_inc(S["shared_psum"], 1)

            def transpose_xg(j, b, loaded):
                pe.wait_ge(xg_loaded[b], loaded)
                for k in range(HC):
                    ins = TE.transpose(bank[b][:, k * P:(k + 1) * P], xg[:, b, k * P:(k + 1) * P], ident[:])
                ins.then_inc(S["xgT_psum"], 1)

            def project_h(j, b, loaded):
                pe.wait_ge(S["xgT_ready"], j + 1)
                pe.wait_ge(w12_loaded[b], loaded)
                for m in range(2):
                    for k in range(HC):
                        ins = TE.matmul(bank[2 + b][:, m * P:(m + 1) * P], w12[:, b, (m * HC + k) * M:(m * HC + k + 1) * M],
                                        xgT[:, b, k * P:(k + 1) * P], start=(k == 0), stop=(k == HC - 1))
                ins.then_inc(S["h_psum"], 1)

            def project_y(j, b, emptied):
                pe.wait_ge(S["hT_ready"], j + 1)
                if emptied is not None:
                    pe.wait_ge(S["y_ready"], emptied)
                TE.matmul(bank[4 + b][:], hT[:, b, :], w3b[:, b, 0:H], start=True,
                          stop=True).then_inc(S["y_psum"], 1)

            def pair(p, first=False):
                for b in range(2):
                    transpose_xg(p * 2 + b, b, p * 16 + 16)
                if not first:
                    project_y(p * 2 - 1, 1, None if isinstance(p, int) and p == 1 else p * 2 - 2)
                for b in range(2):
                    project_h(p * 2 + b, b, p * 16 + 16)
                project_y(p * 2, 0, None if first else p * 2 - 1)

            n_extra = extra(pe)
            pe.wait_ge(S["s_ready"], NT * NP_)
            pe.wait_ge(S["shT_ready"], 2 * SC)
            pair(0, first=True)
            pair(1)
            with pe.Fori(2, FULL_PAIRS) as p:
                pair(p)
            with pe.Fori(0, PAIRS - FULL_PAIRS) as q:
                with pe.If(q < n_extra):
                    pair(q + FULL_PAIRS)
            pe.wait_ge(S["hT_ready"], n_extra * 2 + FULL)
            pe.wait_ge(S["y_ready"], n_extra * 2 + (FULL - 2))
            TE.matmul(bank[5][:], hT[:, 1, :], w3b[:, 1, 0:H], start=True, stop=True).then_inc(S["y_psum"], 1)

            pe.wait_ge(S["up_w_loaded"], 16)
            project(0, wu, S["up_psum"], S["su_ready"])
            for t in range(NT):
                if t + 1 < NT:
                    project(t + 1, wu, S["up_psum"], S["su_ready"])
                if t >= 1:
                    pe.wait_ge(S["mix_ready"], t)
                for k in range(SC):
                    TE.matmul(bank[7][:], shT[:, k, t * P:(t + 1) * P], sw3[:, k, :], start=(k == 0), stop=False)
                TE.matmul(bank[7][:], gateT[:, t * P:(t + 1) * P], b3_all[:], start=False, stop=True).then_inc(S["z_psum"], 1)
                pe.wait_ge(S["su_ready"], NP_ * (t + 1))
                if t == 0:
                    pe.wait_ge(S["y_ready"], n_extra * 2 + FULL)
                for q in range(3):
                    if t >= 1:
                        pe.wait_ge(S["sdT_ready"], 3 * (t - 1) + q + 1)
                    for k in range(4 * q, min(4 * q + 4, IC)):
                        a, b = CHUNKS[k]
                        ins = TE.transpose(bank[3 + q][0:b - a, (k % 4) * P:(k % 4 + 1) * P], s[:, t, a:b], ident[:])
                    ins.then_inc(S["sdT_psum"], 1)
                if t == 0:
                    pe.wait_ge(S["down_w_loaded"], 32)
                else:
                    pe.wait_ge(S["o_ready"], t)
                for k in range(IC):
                    a, b = CHUNKS[k]
                    if k % 4 == 0:
                        pe.wait_ge(S["sdT_ready"], 3 * t + k // 4 + 1)
                    ins = TE.matmul(bank[6][:], sdT[0:b - a, k * P:(k + 1) * P], wd[0:b - a, k, :],
                                    start=(k == 0), stop=(k == IC - 1))
                ins.then_inc(S["down_psum"], 1)


def kernel(L0_attn_x, L0_attn_w_gate, L0_attn_w_up, L0_attn_w_down, L0_ffn_router_w, L0_ffn_router_b,
           L0_ffn_router_bias, L0_ffn_ew1, L0_ffn_eb1, L0_ffn_ew2, L0_ffn_eb2, L0_ffn_ew3, L0_ffn_eb3,
           L0_ffn_sw1, L0_ffn_sb1, L0_ffn_sw2, L0_ffn_sb2, L0_ffn_sw3, L0_ffn_sb3):
    import numpy as np
    import concourse.bacc as bacc
    from concourse.bass_utils import run_bass_kernel_spmd

    x = np.asarray(L0_attn_x)
    B, S_, H = x.shape
    ew1, ew2, ew3 = (np.asarray(w) for w in (L0_ffn_ew1, L0_ffn_ew2, L0_ffn_ew3))
    E, _, M = ew1.shape

    def by_partition(w):
        return w.reshape(E, H // P, P, M).transpose(0, 2, 1, 3).reshape(E * P, H // P * M)

    eb = [np.asarray(b).reshape(E * M, 1) for b in (L0_ffn_eb1, L0_ffn_eb2)]
    expert_w12 = np.concatenate([by_partition(ew1), by_partition(ew2)], axis=1)
    expert_w3b = np.concatenate([ew3.reshape(E * M, H), *eb], axis=1)
    sb1, sb2 = (np.asarray(b).reshape(-1, P).T for b in (L0_ffn_sb1, L0_ffn_sb2))
    arrays = {
        "x": x.reshape(B * S_, H),
        "w_gate_t": np.asarray(L0_attn_w_gate).T,
        "w_up_t": np.asarray(L0_attn_w_up).T,
        "w_down_t": np.asarray(L0_attn_w_down).T,
        "router_w": np.asarray(L0_ffn_router_w),
        "router_b": np.asarray(L0_ffn_router_b).reshape(1, E),
        "router_bias": np.asarray(L0_ffn_router_bias).reshape(1, E),
        "expert_w12": expert_w12,
        "expert_w3b": expert_w3b,
        "expert_b3": np.asarray(L0_ffn_eb3),
        "shared_w12": np.concatenate([np.asarray(L0_ffn_sw1), np.asarray(L0_ffn_sw2)], axis=0),
        "shared_b12": np.concatenate([sb1, sb2], axis=1),
        "shared_w3": np.asarray(L0_ffn_sw3),
        "shared_b3": np.asarray(L0_ffn_sb3).reshape(1, H),
    }
    arrays = {n: np.ascontiguousarray(a) for n, a in arrays.items()}
    nc = bacc.Bacc("TRN2", target_bir_lowering=False, num_devices=1)
    args = [nc.dram_tensor(n, a.shape, mybir.dt.from_np(a.dtype), kind="ExternalInput").ap() for n, a in arrays.items()]
    out = nc.dram_tensor("out", (B * S_, H), F32, kind="ExternalOutput").ap()
    gated_block_kernel(nc, *args, out)
    r = run_bass_kernel_spmd(nc, [arrays], core_ids=[0])
    return r.results[0]["out"].reshape(B, S_, H)
```

```python
from contextlib import ExitStack

import concourse.bass as bass
from concourse import mybir

F32 = mybir.dt.float32
F32R = mybir.dt.float32r
BF16 = mybir.dt.bfloat16
I32 = mybir.dt.int32
ALU = mybir.AluOpType
ACT = mybir.ActivationFunctionType
AX_X = mybir.AxisListType.X

P = 128
EPS = 1e-5
GROUPS, GROUP_LIMIT, TOP_K = 4, 2, 2
KEEP_FACTOR = 0.5
BIG = 3e38
BANK = 512


def gated_block_kernel(nc, x, w_gate_t, w_up_t, w_down_t, router_w, router_b, router_bias, expert_w12,
                       expert_w3, expert_b12, expert_b3, shared_w12, shared_b12, shared_w3, shared_b3, out):
    T, H = x.shape
    I = w_gate_t.shape[1]
    E = router_w.shape[1]
    M = P
    SM = shared_w3.shape[0]
    NT = T // P
    HC = H // P
    IC = -(-I // P)
    I_LAST = I - (IC - 1) * P
    SC = SM // P
    N_DROP = int(KEEP_FACTOR * I)
    PER_GROUP = E // GROUPS
    FULL = T * TOP_K // P
    SLOT_TILES = FULL + E
    SLOTS = SLOT_TILES * P
    LISTED = SLOT_TILES + 2
    TABLES = max(4 * NT * E, LISTED * E)
    PAIRS, FULL_PAIRS = SLOT_TILES // 2, FULL // 2
    W12 = 2 * HC * M
    PIECES = [(a, min(a + BANK, I)) for a in range(0, I, BANK)]
    NP_ = len(PIECES)
    HALF = NT // 2
    BITS = 31
    ROUNDS = 6
    STACKED = [slice(32 * n, 32 * n + E + 1) for n in range(3)]
    STACK = 64 + E + 1
    X_PARTS = ((0, 2), (2, HALF), (HALF, NT))
    BY_DVE = (1, 2)
    BY_POOL = IC - HALF
    UP_ROUNDS = 3
    WINDOW = 7
    CHUNKS = [(k * P, min((k + 1) * P, I)) for k in range(IC)]
    assert (ROUNDS - UP_ROUNDS) * 2 + 2 * HALF + 2 == FULL and BY_DVE[1] == 2
    assert HC == HALF and H == BANK and FULL % 2 == 0 and E % 2 == 0 and T == 8 * P and I % 2 == 0

    with ExitStack() as ctx:
        def sb(name, shape, dt=F32):
            return ctx.enter_context(nc.sbuf_tensor(name, shape, dt))

        def sem(name):
            return ctx.enter_context(nc.semaphore(name))

        bank = [ctx.enter_context(nc.psum_tensor(f"bank{i}", [P, BANK], F32)) for i in range(8)]

        xn_rows = nc.dram_tensor("xn_rows", [T, H], F32).ap()
        slot_token_dram = nc.dram_tensor("slot_token_dram", [SLOTS, 1], I32).ap()
        slot_y = nc.dram_tensor("slot_y", [SLOTS, H], F32).ap()

        def overlay(*layouts):
            made = []
            for layout in layouts[:-1]:
                with ExitStack() as phase:
                    made += [phase.enter_context(nc.sbuf_tensor(n, shape, dt)) for n, shape, dt in layout]
            return made + [sb(n, shape, dt) for n, shape, dt in layouts[-1]]

        W_SIZE = max(HC * I, IC * H)
        w_high = sb("w_high", [P, W_SIZE], F32R)
        w_raw, w_low = overlay([("w_raw", [P, W_SIZE], F32)], [("w_low", [P, W_SIZE], F32R)])
        proj = lambda w: w[:, 0:HC * I].rearrange("p (k n) -> p k n", k=HC)
        down = lambda w: w[:, 0:IC * H].rearrange("p (k n) -> p k n", k=IC)
        sw12_raw, sw12_low, w12 = overlay([("sw12_raw", [P, 2 * HC, SM], F32)], [("sw12_low", [P, 2 * HC, SM], F32R)],
                                          [("w12", [P, 2, W12], F32)])
        sw12_high, xg, xgT = overlay([("sw12_high", [P, 2 * HC, SM], F32R)],
                                     [("xg", [P, 2, H], F32), ("xgT", [P, 2, H], F32)])
        sw3, sw3_low = overlay([("sw3", [P, SC, H], F32)], [("sw3_low", [P, SC, H], F32R)])
        sb12 = sb("sb12", [P, 2 * SC])
        rw = sb("rw", [P, HC, E])
        rw_high = sb("rw_high", [P, HC, E], F32R)
        rw_low = sb("rw_low", [P, HC, E], F32R)
        b3_stack = sb("b3_stack", [STACK, H], F32R)
        rb_all = sb("rb_all", [P, 2, E])
        sdT_high, mix_g, xnT_high = overlay(
            [("sdT_high", [P, 2, IC * P], F32R), ("mix_g", [P, 2, H], F32)],
            [("xnT_high", [P, HC, T], F32R)])
        sdT_low, x_end, xnT_low = overlay([("sdT_low", [P, 2, IC * P], F32R), ("x_end", [P, 2, H], F32)],
                                          [("xnT_low", [P, HC, T], F32R)])
        mix, g = mix_g[:, 0, :], mix_g[:, 1, :]
        s = sb("s", [P, NT, I])
        wg_raw = s[:, NT - HC:NT, :]
        w3 = sb("w3", [P, 2, H])
        b12 = sb("b12", [P, 2, E])
        tile_b12 = sb("tile_b12", [P, 2, LISTED])
        x_in = s[:].rearrange("p t n -> p (t n)")[:, 0:NT * H].rearrange("p (t h) -> p t h", t=NT)
        shT_high, sw3_high, mag_rows = overlay([("shT_high", [P, SC, T], F32R), ("sw3_high", [P, SC, H], F32R)],
                                               [("mag_rows", [P, HALF * I], F32)])
        mag = mag_rows[:].rearrange("p (t n) -> p t n", t=HALF)
        xn = mag_rows[:, 0:NT * H].rearrange("p (t h) -> p t h", t=NT)
        shT, shT_low = overlay([("shT", [P, SC, T], F32)], [("shT_low", [P, SC, T], F32R)])
        gateT = sb("gateT", [STACK, T], F32R)
        ident = sb("ident", [P, P])
        before = sb("before", [P, P])
        ones = sb("ones", [P, P])
        zero1 = sb("zero1", [P, 1])
        logitsT = shT[0:E, 0, :]

        stats = sb("stats", [P, NT, 6])
        mv = sb("mv", [P, NT, 2])
        ln = sb("ln", [P, 3, NT])

        sc_t = sb("sc_t", [P, NT, E])
        spare = sb("spare", [P, TABLES + LISTED * E])
        table = lambda n: spare[:, n * NT * E:(n + 1) * NT * E].rearrange("p (t e) -> p t e", t=NT)
        ex_t = table(0)
        tmp_t = sb("tmp_t", [P, NT, E])
        msk_t = table(1)
        pick = [sb(f"pick{k}", [P, NT, E]) for k in range(TOP_K)]
        hits = sb("hits", [P, NT, E])
        pos_t = table(2)
        tot_t = table(3)
        run_t = sb("run_t", [P, E])
        tiles_i = sb("tiles_i", [P, E], I32)
        tiles_f = sb("tiles_f", [P, E])
        tiles_end = sb("tiles_end", [P, E])
        first_tile = sb("first_tile", [P, E])
        gm = sb("gm", [P, NT, GROUPS])
        gtmp = sb("gtmp", [P, NT, GROUPS])
        gpick = [sb(f"gpick{k}", [P, NT, GROUPS]) for k in range(GROUP_LIMIT)]
        red = sb("red", [P, NT])
        red2 = sb("red2", [P, NT])
        val = [sb(f"val{k}", [P, NT]) for k in range(TOP_K)]
        gates = sb("gates", [P, NT, E + 1])
        rank_e = sb("rank_e", [P, E])
        iota_j = sb("iota_j", [P, LISTED])
        iota_i = sb("iota_i", [P, LISTED], I32)
        te_cmp = spare[:, TABLES:TABLES + LISTED * E].rearrange("p (j e) -> p j e", e=E)
        te_bias = spare[:, 0:LISTED * E].rearrange("p (j e) -> p j e", e=E)
        te_f = sb("te_f", [P, LISTED])
        tile_expert = sb("tile_expert", [P, LISTED], I32)
        slot_f = sb("slot_f", [P, NT])
        slot_of = [sb(f"slot_of{k}", [P, NT], I32) for k in range(TOP_K)]
        slot_blk = sb("slot_blk", [P, NT], I32)
        slot_bf = sb("slot_bf", [P, NT])
        list_at = [sb(f"list_at{k}", [P, NT], I32) for k in range(TOP_K)]
        extra_pairs = sb("extra_pairs", [P, 1], I32)
        token_no = sb("token_no", [P, NT], I32)
        zero_list = sb("zero_list", [P, SLOT_TILES], I32)
        slot_token = sb("slot_token", [P, SLOT_TILES], I32)

        low = [sb(f"low{h}", [P, 2, HALF]) for h in range(2)]
        high = [sb(f"high{h}", [P, 2, HALF]) for h in range(2)]
        cur = [sb(f"cur{h}", [P, 2, HALF]) for h in range(2)]
        sums = [sb(f"sums{h}", [P, HALF]) for h in range(2)]
        signs = [sb(f"signs{h}", [P, HALF]) for h in range(2)]
        span = sb("span", [P, 2, HALF])
        step_a = sb("step_a", [P, HALF])
        step_b = sb("step_b", [P, HALF])
        top8 = sb("top8", [P, HALF, 8])
        hit8 = sb("hit8", [P, HALF, 8])
        cut = [sb(f"cut{h}", [P, HALF]) for h in range(2)]
        above = sb("above", [P, HALF])
        bad = sb("bad", [P, 1])
        bad_all = sb("bad_all", [P, 1])
        bad_i = [sb(f"bad_i{h}", [P, 1], I32) for h in range(2)]
        cnt = sb("cnt", [P, HALF])
        thr = sb("thr", [P, HALF], I32)
        cand = sb("cand", [P, HALF], I32)
        add = sb("add", [P, HALF], I32)
        bit_f = sb("bit_f", [P, 1])
        bit_i = sb("bit_i", [P, 1], I32)
        need = sb("need", [P, HALF])
        work = sb("work", [P, I])
        junk = work[:].bitcast(BF16)[:, 0:I]
        eq = work[:].bitcast(BF16)[:, I:2 * I]
        act_junk = sb("act_junk", [P, I], BF16)
        ties = act_junk[:].bitcast(mybir.dt.int16)

        sil = sb("sil", [P, 2, P])
        hT = sb("hT", [P, 2, P])
        y_sb = sb("y_sb", [P, 2, H])
        ssil = y_sb
        b3_all = y_sb[0:E + 1, 1, :]

        yk = [xg, xgT]
        o_sb = y_sb

        names = """const_ready x_loaded0 x_loaded1 x_loaded2 router_loaded gate_w_loaded0 gate_w_loaded1 gate_w_loaded2
            up_w_loaded0 up_w_loaded1 up_w_loaded2 shared_loaded down_w_loaded
            ln_var ln_root xn_ready xn_stored xnT_psum xnT_high_ready xnT_split w_high_ready w_split
            rw_high_ready rw_split sw12_high_ready sw12_split wd_high_ready wd_split
            logitsT_psum logitsT_ready logits_ready exp_in exp_out picks_ready
            rank_ready gates_ready gateT_psum gateT_high_ready gateT_ready b3_high_ready b3_split z_high_ready z_split lists_ready b12_loaded tile_b12_ready list_zeroed list_scattered list_loaded
            gate_psum s_ready mag_ready thr_ready0 thr_ready1 act_counted0 act_counted1 bad_ready0 bad_ready1
            bad_summed0 bad_summed1 fall_step0 fall_step1 s_masked
            shared_psum ssil_ready shT_ready
            w12_loaded0 w12_loaded1 w3_loaded0 w3_loaded1 xg_loaded0 xg_loaded1 xgT_psum xgT_ready
            h_psum sil_ready hT_ready y_psum y_ready y_stored0 y_stored1 all_y_stored y_zero y_zeroed
            up_psum su_ready sdT_psum sdT_high_ready sdT_split down_psum z_psum yk_loaded0 yk_loaded1
            x_again0 x_again1 mix_ready g_ready o_ready out_stored0 out_stored1 dve_step""".split()
        S = {n: sem(n) for n in names}
        pair_of = lambda n: [S[n + "0"], S[n + "1"]]
        x_loaded = [S[f"x_loaded{n}"] for n in range(len(X_PARTS))]
        out_stored, yk_loaded = pair_of("out_stored"), pair_of("yk_loaded")
        w12_loaded, w3_loaded, xg_loaded = pair_of("w12_loaded"), pair_of("w3_loaded"), pair_of("xg_loaded")
        y_stored, x_again = pair_of("y_stored"), pair_of("x_again")
        thr_ready, act_counted = pair_of("thr_ready"), pair_of("act_counted")
        gate_w_loaded = [S[f"gate_w_loaded{c}"] for c in range(NP_)]
        up_w_loaded = [S[f"up_w_loaded{c}"] for c in range(NP_)]
        bad_ready, bad_summed, fall_step = pair_of("bad_ready"), pair_of("bad_summed"), pair_of("fall_step")

        GATE_UNITS = [(t, 0) for t in range(HALF)] + [(t, c) for t in range(HALF) for c in range(1, NP_)] + \
                     [(t, c) for t in range(HALF, NT) for c in range(NP_)]
        tile_done = lambda t: max(n for n, u in enumerate(GATE_UNITS) if u[0] == t) + 1

        DOWN_BANKS, Z_BANKS = (3, 6), (7, 4)
        xnT_bank = lambda t: bank[(3, 4, 6, 7)[t % 4]][:].rearrange("p (k m) -> p k m", k=HC)

        DOWN_PARTS = [(slice(0, P), slice(k, min(k + 4, IC - 1))) for k in range(0, IC - 1, 4)] + \
                     [(slice(0, I_LAST), slice(IC - 1, IC))]

        def extra(eng):
            eng.wait_ge(S["lists_ready"], 1)
            return eng.value_load(extra_pairs[0:1, 0:1], min_val=0, max_val=PAIRS - FULL_PAIRS)

        block = ctx.enter_context(nc.Block())

        @block.sync
        def _(sp):
            def load_gate_piece(c):
                a, b = PIECES[c]
                sp.dma_start(wg_raw[:, :, a:b], w_gate_t[:, a:b].rearrange("(k p) n -> p k n", p=P)
                             ).then_inc(gate_w_loaded[c], 16)

            def load_x(n):
                a, b = X_PARTS[n]
                sp.dma_start(x_in[:, a:b, :], x[a * P:b * P, :].rearrange("(t p) n -> p t n", p=P)
                             ).then_inc(x_loaded[n], 16)

            load_x(0)
            load_x(1)
            load_gate_piece(0)
            load_x(2)
            load_gate_piece(1)
            sp.dma_start(rw[:], router_w.rearrange("(k p) e -> p k e", p=P)).then_inc(S["router_loaded"], 16)
            sp.dma_start(rb_all[:, 0, :], router_b.broadcast_to([P, E])).then_inc(S["router_loaded"], 16)
            sp.dma_start(rb_all[:, 1, :], router_bias.broadcast_to([P, E])).then_inc(S["router_loaded"], 16)
            load_gate_piece(2)
            sp.dma_start(b12[:], expert_b12.rearrange("p (m e) -> p m e", m=2)).then_inc(S["b12_loaded"], 16)
            sp.wait_ge(S["xn_ready"], NT)
            sp.dma_start(xn_rows.rearrange("(t p) n -> p t n", p=P), xn).then_inc(S["xn_stored"], 16)
            sp.dma_start(sw12_raw[:], shared_w12.rearrange("(k p) n -> p k n", p=P)).then_inc(S["shared_loaded"], 16)
            sp.dma_start(sw3[:], shared_w3.rearrange("(k p) n -> p k n", p=P)).then_inc(S["shared_loaded"], 16)
            sp.dma_start(sb12[:], shared_b12).then_inc(S["shared_loaded"], 16)
            sp.dma_start(b3_all[0:E, :], expert_b3).then_inc(S["shared_loaded"], 16)
            sp.dma_start(b3_all[E:E + 1, :], shared_b3).then_inc(S["shared_loaded"], 16)
            sp.wait_ge(S["y_zero"], 1)
            sp.dma_start(slot_y[FULL * P:SLOTS, :].rearrange("(j p) n -> p j n", p=P),
                         y_sb[:, 0:1, :].to_broadcast([P, SLOT_TILES - FULL, H])).then_inc(S["y_zeroed"], 16)

            def expert_of(j):
                return sp.value_load(tile_expert[0:1, bass.ds(j, 1)], min_val=0, max_val=E - 1)

            def load_w12(j, b):
                e = expert_of(j)
                sp.dma_start(w12[:, b, :], expert_w12[bass.ds(e * P, P), :]).then_inc(w12_loaded[b], 16)

            def load_w3(j, b):
                e = expert_of(j)
                sp.dma_start(w3[:, b, :], expert_w3[bass.ds(e * P, P), :]).then_inc(w3_loaded[b], 16)

            def store_y(j, b):
                sp.dma_start(slot_y[bass.ds(j * P, P), :], y_sb[:, b, :]).then_inc(y_stored[b], 16)

            def serve_pair(p):
                for b in range(2):
                    j = p * 2 + b
                    sp.wait_ge(S["y_psum"], j - 1)
                    load_w3(j, b)
                    sp.wait_ge(S["y_ready"], j - 1)
                    store_y(j - 2, b)
                    sp.wait_ge(S["h_psum"], j + 1)
                    load_w12(j + 2, b)

            sp.wait_ge(S["gate_psum"], NT * NP_)
            for c, (a, b) in enumerate(PIECES):
                sp.dma_start(proj(w_raw)[:, :, a:b], w_up_t[:, a:b].rearrange("(k p) n -> p k n", p=P)
                             ).then_inc(up_w_loaded[c], 16)
            n_extra = extra(sp)
            sp.wait_ge(S["shared_psum"], 4 * SC)
            for b in range(2):
                load_w12(b, b)
            for b in range(2):
                load_w3(b, b)
            sp.wait_ge(S["up_psum"], NT * NP_)
            sp.dma_start(down(w_raw)[:, 0:IC - 1, :], w_down_t[0:(IC - 1) * P, :].rearrange("(k p) n -> p k n", p=P)
                         ).then_inc(S["down_w_loaded"], 16)
            sp.dma_start(down(w_raw)[0:I_LAST, IC - 1, :], w_down_t[(IC - 1) * P:I, :]).then_inc(S["down_w_loaded"], 16)
            for b in range(2):
                sp.wait_ge(S["h_psum"], b + 1)
                load_w12(b + 2, b)
            with sp.Fori(1, FULL_PAIRS) as p:
                serve_pair(p)
            with sp.If(n_extra > 0):
                with sp.Fori(0, PAIRS - FULL_PAIRS) as q:
                    with sp.If(q < n_extra):
                        serve_pair(q + FULL_PAIRS)
            last = n_extra * 2 + FULL
            for b in range(2):
                sp.wait_ge(S["y_ready"], last - 1 + b)
                store_y(last - 2 + b, b)
            for b in range(2):
                sp.wait_ge(y_stored[b], (n_extra + FULL_PAIRS) * 16)
            sp.sem_inc(S["all_y_stored"], 1)

            for t in range(2):
                sp.dma_start(x_end[:, t, :], x[t * P:(t + 1) * P, :]).then_inc(x_again[t], 16)
            for t in range(NT):
                sp.wait_ge(S["o_ready"], t + 1)
                sp.dma_start(out[t * P:(t + 1) * P, :], o_sb[:, t % 2, :]).then_inc(out_stored[t % 2], 16)
                if t + 2 < NT:
                    sp.dma_start(x_end[:, t % 2, :], x[(t + 2) * P:(t + 3) * P, :]).then_inc(x_again[t % 2], 16)
            for b in range(2):
                sp.wait_ge(out_stored[b], 16 * (NT // 2))

        @block.gpsimd
        def _(pool):
            pool.memset(y_sb[:, 0, :], 0.0).then_inc(S["y_zero"], 1)
            pool.memset(ident[:], 0.0).then_inc(S["const_ready"], 1)
            pool.memset(ones[:], 1.0).then_inc(S["const_ready"], 1)
            pool.memset(zero1[:], 0.0).then_inc(S["const_ready"], 1)
            pool.memset(zero_list[:], 0).then_inc(S["const_ready"], 1)
            pool.iota(token_no[:], [[P, NT]], base=0, channel_multiplier=1).then_inc(S["const_ready"], 1)
            pool.iota(iota_i[:], [[1, LISTED]], base=0, channel_multiplier=0).then_inc(S["const_ready"], 1)
            pool.memset(gates[:, :, E:E + 1], 1.0).then_inc(S["const_ready"], 1)
            pool.memset(gateT[:].bitcast(F32), 0.0).then_inc(S["const_ready"], 1)
            pool.memset(b3_stack[:].bitcast(F32), 0.0).then_inc(S["const_ready"], 1)
            pool.wait_ge(S["const_ready"], 9)
            pool.affine_select(out=ident[:], in_=ident[:], compare_op=ALU.not_equal, fill=1.0, base=0,
                               pattern=[[-1, P]], channel_multiplier=1).then_inc(S["const_ready"], 1)
            pool.affine_select(out=before[:], in_=ones[:], compare_op=ALU.is_gt, fill=0.0, base=0,
                               pattern=[[1, P]], channel_multiplier=-1).then_inc(S["const_ready"], 1)
            list_view = slot_token_dram.rearrange("(p j) a -> p (j a)", p=P)
            pool.dma_start(list_view, zero_list[:]).then_inc(S["list_zeroed"], 16)

            def low_piece(src, c, done):
                a, b = PIECES[c]
                pool.wait_ge(S["w_high_ready"], done)
                pool.tensor_tensor(proj(w_low)[:, :, a:b], src[:, :, a:b], proj(w_high)[:, :, a:b].bitcast(F32),
                                   ALU.subtract).then_inc(S["w_split"], 1)

            for c in range(NP_):
                low_piece(wg_raw, c, c + 1)
            pool.wait_ge(S["sw12_high_ready"], 1)
            pool.tensor_tensor(sw12_low[:], sw12_raw[:], sw12_high[:].bitcast(F32), ALU.subtract).then_inc(S["sw12_split"], 1)

            pool.wait_ge(S["list_zeroed"], 16)
            n_extra = extra(pool)
            for t in range(NT):
                for k in range(TOP_K):
                    pool.indirect_dma_start(
                        out=slot_token_dram, out_offset=bass.IndirectOffsetOnAxis(ap=list_at[k][:, t:t + 1], axis=0),
                        in_=token_no[:, t:t + 1], in_offset=None).then_inc(S["list_scattered"], 16)
            pool.wait_ge(S["list_scattered"], 16 * NT * TOP_K)
            pool.dma_start(slot_token[:], list_view).then_inc(S["list_loaded"], 16)
            pool.wait_ge(S["list_loaded"], 16)
            pool.wait_ge(S["xn_stored"], 16)

            for c in range(NP_):
                low_piece(proj(w_raw), c, NP_ + c + 1)
            pool.wait_ge(S["shared_psum"], 4 * SC)

            def gather_tokens(j):
                if j >= 2:
                    pool.wait_ge(S["xgT_psum"], j - 1)
                pool.indirect_dma_start(
                    out=xg[:, j % 2, :], out_offset=None, in_=xn_rows,
                    in_offset=bass.IndirectOffsetOnAxis(ap=slot_token[:, j:j + 1], axis=0)
                ).then_inc(xg_loaded[j % 2], 16)

            def sum_bad(h):
                pool.wait_ge(bad_ready[h], 1)
                pool.partition_all_reduce(bad_all[:], bad[:], P, bass.bass_isa.ReduceOp.add).then_inc(bad_summed[h], 1)

            def low_down(k):
                pool.wait_ge(S["wd_high_ready"], k // 4 + 1)
                rows = slice(0, P if k < IC - 1 else I_LAST)
                pool.tensor_tensor(down(w_low)[rows, k, :], down(w_raw)[rows, k, :], down(w_high)[rows, k, :].bitcast(F32),
                                   ALU.subtract).then_inc(S["wd_split"], 1)

            for j in range(FULL):
                gather_tokens(j)
                if j == 1:
                    sum_bad(0)
                if j == 12:
                    sum_bad(1)
            for k in range(BY_POOL):
                low_down(k)
            for q in range(PAIRS - FULL_PAIRS):
                with pool.If(n_extra > q):
                    for b in range(2):
                        gather_tokens(FULL + 2 * q + b)

            pool.wait_ge(S["all_y_stored"], 1)
            for t in range(NT):
                if t >= 2:
                    pool.wait_ge(S["mix_ready"], t - 1)
                for k in range(TOP_K):
                    pool.indirect_dma_start(
                        out=yk[k][:, t % 2, :], out_offset=None, in_=slot_y,
                        in_offset=bass.IndirectOffsetOnAxis(ap=slot_of[k][:, t:t + 1], axis=0)
                    ).then_inc(yk_loaded[t % 2], 16)

        @block.scalar
        def _(act):
            unit = [0]

            def silu_gate():
                t, c = GATE_UNITS[unit[0]]
                a, b = PIECES[c]
                act.wait_ge(S["gate_psum"], unit[0] + 1)
                if unit[0] == 0:
                    act.wait_ge(S["xn_ready"], NT)
                if unit[0] == tile_done(HALF - 1):
                    act.wait_ge(S["w_split"], NP_)
                nc.scalar.activation(s[:, t, a:b], bank[unit[0] % NP_][:, 0:b - a], ACT.Silu).then_inc(S["s_ready"], 1)
                unit[0] += 1
                if t < HALF and c == NP_ - 1:
                    magnitude(0, t)

            def magnitude(h, i):
                t = h * HALF + i
                act.wait_ge(S["s_ready"], tile_done(t))
                if t == 0:
                    act.wait_ge(S["xn_stored"], 16)
                    act.wait_ge(S["xnT_psum"], NT)
                nc.scalar.activation(mag[:, i, :], s[:, t, :], ACT.Abs, accum_out=sums[h][:, i:i + 1]
                                     ).then_inc(S["mag_ready"], 1)

            def high_piece(src, c):
                a, b = PIECES[c]
                nc.scalar.activation(proj(w_high)[:, :, a:b], src[:, :, a:b], ACT.Copy).then_inc(S["w_high_ready"], 1)

            def count_tile(h, i, n_round):
                act.wait_ge(thr_ready[h], n_round + 1)
                before_it = n_round * (HALF - BY_DVE[h]) + i - BY_DVE[h]
                if before_it > 0:
                    act.wait_ge(act_counted[h], before_it)
                nc.scalar.activation(act_junk[:], mag[:, i, :], ACT.Sign, bias=cur[h][:, 0, i:i + 1], scale=-1.0,
                                     accum_out=signs[h][:, i:i + 1]).then_inc(act_counted[h], 1)

            def count_tiles(h, n_round):
                for i in range(BY_DVE[h], HALF):
                    count_tile(h, i, n_round)

            def ln_root(b):
                act.wait_ge(S["ln_var"], b + 1)
                nc.scalar.activation(ln[:, 1, b * HALF:(b + 1) * HALF], ln[:, 0, b * HALF:(b + 1) * HALF],
                                     ACT.Sqrt).then_inc(S["ln_root"], 1)

            def transposed_high(t):
                act.wait_ge(S["xnT_psum"], t + 1)
                nc.scalar.activation(xnT_high[:, :, t * P:(t + 1) * P], xnT_bank(t),
                                     ACT.Copy).then_inc(S["xnT_high_ready"], 1)

            ln_root(0)
            act.wait_ge(gate_w_loaded[0], 16)
            high_piece(wg_raw, 0)
            for t in range(HALF):
                transposed_high(t)
            ln_root(1)
            act.wait_ge(S["router_loaded"], 16 * 3)
            nc.scalar.activation(rw_high[:], rw[:], ACT.Copy).then_inc(S["rw_high_ready"], 1)
            for c in range(1, NP_):
                act.wait_ge(gate_w_loaded[c], 16)
                high_piece(wg_raw, c)
            for _ in range(3):
                silu_gate()
            for t in range(HALF, NT):
                transposed_high(t)
            for _ in range(2):
                silu_gate()
            act.wait_ge(S["logitsT_psum"], 1)
            for b in range(2):
                ins = nc.scalar.activation(logitsT[:, b * BANK:(b + 1) * BANK], bank[6 + b][0:E, :], ACT.Copy)
            ins.then_inc(S["logitsT_ready"], 1)
            silu_gate()
            act.wait_ge(S["exp_in"], 1)
            nc.scalar.activation(ex_t, tmp_t[:], ACT.Exp).then_inc(S["exp_out"], 1)
            while unit[0] < tile_done(HALF - 1):
                silu_gate()
            act.wait_ge(S["shared_loaded"], 16 * 5)
            nc.scalar.activation(sw12_high[:], sw12_raw[:], ACT.Copy).then_inc(S["sw12_high_ready"], 1)
            act.wait_ge(S["const_ready"], 11)
            for n in (0, 2):
                nc.scalar.activation(b3_stack[STACKED[n], :], b3_all, ACT.Copy).then_inc(S["b3_high_ready"], 1)
            act.wait_ge(S["gateT_psum"], 1)
            for n in range(2):
                for q in range(2):
                    nc.scalar.activation(gateT[STACKED[n], q * BANK:(q + 1) * BANK], bank[6 + q][0:E + 1, :], ACT.Copy
                                         ).then_inc(S["gateT_high_ready"], 1)
            for t in range(HALF, NT):
                for _ in range(NP_):
                    silu_gate()
                n = t - HALF - 1
                if n >= 0:
                    count_tiles(0, n)

            act.wait_ge(S["y_zeroed"], 16)
            act.wait_ge(S["b3_split"], 1)
            for u in range(2 * SC):
                c = u // 2
                act.wait_ge(S["shared_psum"], 2 * u + 1)
                if u >= 2:
                    act.wait_ge(S["shT_ready"], u - 1)
                nc.scalar.activation(ssil[:, u % 2, :], bank[(3, 6)[u % 2]][:], ACT.Silu,
                                     bias=sb12[:, c:c + 1]).then_inc(S["ssil_ready"], 1)
                if u < NP_:
                    act.wait_ge(up_w_loaded[u], 16)
                    high_piece(proj(w_raw), u)
                if HALF - 1 + u < ROUNDS:
                    count_tiles(0, HALF - 1 + u)

            for i in range(HALF):
                act.wait_ge(S["s_masked"], i + 1)
                magnitude(1, i)
            for n in range(UP_ROUNDS):
                count_tiles(1, n)

            def copy_xgT(j, b):
                act.wait_ge(S["xgT_psum"], j + 1)
                nc.scalar.activation(xgT[:, b, :], bank[b][:], ACT.Copy).then_inc(S["xgT_ready"], 1)

            column = lambda j: slice(j, j + 1) if isinstance(j, int) else bass.ds(j, 1)

            def silu_h(j, b):
                act.wait_ge(S["h_psum"], j + 1)
                nc.scalar.activation(sil[:, b, :], bank[2 + b][:, 0:P], ACT.Silu,
                                     bias=tile_b12[:, 0, column(j)]).then_inc(S["sil_ready"], 1)

            def copy_y(j, b, stored):
                act.wait_ge(S["y_psum"], j + 1)
                if stored is not None:
                    act.wait_ge(y_stored[b], stored)
                nc.scalar.activation(y_sb[:, b, :], bank[4 + b][:], ACT.Copy).then_inc(S["y_ready"], 1)

            def pair(p, n_round=None, parts=()):
                first, second = (isinstance(p, int) and p == n for n in range(2))
                for b in range(2):
                    copy_xgT(p * 2 + b, b)
                for b in range(2):
                    if not first:
                        copy_y(p * 2 - 2 + b, b, None if second else p * 16 - 16)
                    if n_round is not None:
                        count_tile(1, BY_DVE[1] + b, n_round)
                    if parts:
                        rows, chunks = DOWN_PARTS[parts[b]]
                        nc.scalar.activation(down(w_high)[rows, chunks, :], down(w_raw)[rows, chunks, :], ACT.Copy
                                             ).then_inc(S["wd_high_ready"], 1)
                    silu_h(p * 2 + b, b)

            n_extra = extra(act)
            act.wait_ge(S["tile_b12_ready"], 1)
            for n in range(UP_ROUNDS, ROUNDS):
                pair(n - UP_ROUNDS, n)
            act.wait_ge(S["down_w_loaded"], 32)
            for n in range(2):
                pair(ROUNDS - UP_ROUNDS + n, parts=(2 * n, 2 * n + 1))
            with act.Fori(ROUNDS - UP_ROUNDS + 2, FULL_PAIRS) as p:
                pair(p)
            with act.If(n_extra > 0):
                with act.Fori(0, PAIRS - FULL_PAIRS) as q:
                    with act.If(q < n_extra):
                        pair(q + FULL_PAIRS)
            def product_high(t):
                for q in range(3):
                    n = min(4, IC - 4 * q)
                    act.wait_ge(S["sdT_psum"], 3 * t + q + 1)
                    if q == 0 and t >= 2:
                        act.wait_ge(S["down_psum"], t - 1)
                    nc.scalar.activation(sdT_high[:, t % 2, 4 * q * P:(4 * q + n) * P],
                                         bank[q][:, 0:n * P], ACT.Copy).then_inc(S["sdT_high_ready"], 1)

            product_high(0)
            act.wait_ge(S["s_masked"], NT)
            nc.scalar.activation(sw3_high[:], sw3[:], ACT.Copy).then_inc(S["z_high_ready"], 1)
            nc.scalar.activation(shT_high[:], shT[:], ACT.Copy).then_inc(S["z_high_ready"], 1)
            for b in range(2):
                copy_y(n_extra * 2 + (FULL - 2 + b), b, n_extra * 16 + (FULL_PAIRS - 1) * 16)
            for t in range(NT):
                if t + 1 < NT:
                    product_high(t + 1)
                act.wait_ge(S["mix_ready"], t + 1)
                if t >= 1:
                    act.wait_ge(S["o_ready"], t)
                nc.scalar.activation(g, mix, ACT.Silu).then_inc(S["g_ready"], 1)

        @block.vector
        def _(dve):
            V = nc.vector
            steps = [0]

            def step(ins):
                steps[0] += 1
                ins.then_inc(S["dve_step"], 1)
                dve.wait_ge(S["dve_step"], steps[0])

            def link(ins, sem_, at):
                ins.then_inc(sem_, 1)
                dve.wait_ge(sem_, at)

            def transposed_low(t):
                dve.wait_ge(S["xnT_high_ready"], t + 1)
                V.tensor_tensor(xnT_low[:, :, t * P:(t + 1) * P], xnT_bank(t),
                                xnT_high[:, :, t * P:(t + 1) * P].bitcast(F32), ALU.subtract).then_inc(S["xnT_split"], 1)

            def normalise(b):
                for t in range(b * HALF, (b + 1) * HALF):
                    for n, part in enumerate(X_PARTS):
                        if part[0] == t:
                            dve.wait_ge(x_loaded[n], 16)
                    V.bn_stats(stats[:, t, :], x_in[:, t, :]).then_inc(S["dve_step"], 1)
                steps[0] += HALF
                dve.wait_ge(S["dve_step"], steps[0])
                for t in range(b * HALF, (b + 1) * HALF):
                    V.bn_aggr(mv[:, t, :], stats[:, t, :]).then_inc(S["dve_step"], 1)
                steps[0] += HALF
                dve.wait_ge(S["dve_step"], steps[0])
                V.tensor_scalar(ln[:, 0, b * HALF:(b + 1) * HALF], mv[:, b * HALF:(b + 1) * HALF, 1], EPS, None,
                                ALU.add).then_inc(S["ln_var"], 1)
                var, r, u = (ln[:, q, b * HALF:(b + 1) * HALF] for q in range(3))
                dve.wait_ge(S["ln_root"], b + 1)
                step(V.reciprocal(r, r))
                step(V.tensor_tensor(u, r, r, ALU.mult))
                step(V.tensor_tensor(u, u, var, ALU.mult))
                step(V.tensor_scalar(u, u, -0.5, 1.5, ALU.mult, ALU.add))
                step(V.tensor_tensor(r, r, u, ALU.mult))
                for t in range(b * HALF, (b + 1) * HALF):
                    V.tensor_scalar(xn[:, t, :], x_in[:, t, :], mv[:, t, 0:1], ln[:, 1, t:t + 1], ALU.subtract,
                                    ALU.mult).then_inc(S["xn_ready"], 1)

            normalise(0)
            for t in range(HALF):
                transposed_low(t)
            normalise(1)
            dve.wait_ge(S["rw_high_ready"], 1)
            V.tensor_tensor(rw_low[:], rw[:], rw_high[:].bitcast(F32), ALU.subtract).then_inc(S["rw_split"], 1)
            for t in range(HALF, NT):
                transposed_low(t)

            dve.wait_ge(S["const_ready"], 11)
            step(V.tensor_scalar(rank_e[:], iota_i[:, 0:E], -1.0, float(E), ALU.mult, ALU.add))
            step(V.tensor_copy(iota_j[:], iota_i[:]))
            dve.wait_ge(S["logits_ready"], 1)
            lg = bank[5][:, 0:NT * E].rearrange("p (t e) -> p t e", t=NT)
            over_t = lambda v: v[:, None, :].to_broadcast([P, NT, E])
            over_e = lambda v, n=E: v[:, :, None].to_broadcast([P, NT, n])
            step(V.tensor_tensor(sc_t[:], lg, over_t(rb_all[:, 0, :]), ALU.add))
            step(V.tensor_reduce(red[:], sc_t[:], AX_X, ALU.max))
            V.tensor_tensor(tmp_t[:], sc_t[:], over_e(red[:]), ALU.subtract).then_inc(S["exp_in"], 1)
            dve.wait_ge(S["exp_out"], 1)
            step(V.tensor_reduce(red[:], ex_t, AX_X, ALU.add))
            step(V.reciprocal(red[:], red[:]))
            step(V.tensor_tensor(sc_t[:], ex_t, over_e(red[:]), ALU.mult))
            step(V.tensor_tensor(sc_t[:], sc_t[:], over_t(rb_all[:, 1, :]), ALU.add))

            def first_max(onehot, table, tmp, n):
                weight = rank_e[:, E - n:E]
                w = weight[:, None, :].to_broadcast([P, NT, n])
                step(V.tensor_reduce(red[:], table, AX_X, ALU.max))
                step(V.tensor_tensor(tmp, table, over_e(red[:], n), ALU.is_equal))
                step(V.tensor_tensor(tmp, tmp, w, ALU.mult))
                step(V.tensor_reduce(red2[:], tmp, AX_X, ALU.max))
                step(V.tensor_tensor(onehot, w, over_e(red2[:], n), ALU.is_equal))

            step(V.tensor_reduce(gm[:], sc_t[:].rearrange("p t (g e) -> p t g e", g=GROUPS), AX_X, ALU.max))
            first_max(gpick[0][:], gm[:], gtmp[:], GROUPS)
            step(V.scalar_tensor_tensor(gm[:], gpick[0][:], -BIG, gm[:], ALU.mult, ALU.add))
            first_max(gpick[1][:], gm[:], gtmp[:], GROUPS)
            step(V.tensor_tensor(gtmp[:], gpick[0][:], gpick[1][:], ALU.add))
            step(V.tensor_scalar(gtmp[:], gtmp[:], BIG, -BIG, ALU.mult, ALU.add))
            step(V.tensor_tensor(msk_t.rearrange("p t (g e) -> p t g e", g=GROUPS),
                                 sc_t[:].rearrange("p t (g e) -> p t g e", g=GROUPS),
                                 gtmp[:, :, :, None].to_broadcast([P, NT, GROUPS, PER_GROUP]), ALU.add))
            first_max(pick[0][:], msk_t, tmp_t[:], E)
            step(V.scalar_tensor_tensor(msk_t, pick[0][:], -BIG, msk_t, ALU.mult, ALU.add))
            first_max(pick[1][:], msk_t, tmp_t[:], E)
            V.tensor_tensor(hits[:], pick[0][:], pick[1][:], ALU.add).then_inc(S["picks_ready"], 1)
            for k in range(TOP_K):
                step(V.tensor_tensor(tmp_t[:], pick[k][:], sc_t[:], ALU.mult))
                step(V.tensor_reduce(val[k][:], tmp_t[:], AX_X, ALU.add))
            step(V.tensor_tensor(tmp_t[:], pick[0][:], over_e(val[0][:]), ALU.mult))
            step(V.tensor_tensor(msk_t, pick[1][:], over_e(val[1][:]), ALU.mult))
            V.tensor_tensor(gates[:, :, 0:E], tmp_t[:], msk_t, ALU.add).then_inc(S["gates_ready"], 1)

            dve.wait_ge(S["rank_ready"], 1)
            rank_ps = bank[5][:, P:2 * P].rearrange("p (t e) -> p t e", t=NT)
            total_ps = bank[5][:, 2 * P:3 * P].rearrange("p (t e) -> p t e", t=NT)
            step(V.tensor_copy(tot_t, total_ps))
            step(V.memset(run_t[:], 0.0))
            for t in range(NT):
                step(V.tensor_tensor(pos_t[:, t, :], run_t[:], rank_ps[:, t, :], ALU.add))
                step(V.tensor_tensor(run_t[:], run_t[:], tot_t[:, t, :], ALU.add))
            step(V.tensor_scalar(tiles_i[:], run_t[:], float(P - 1), None, ALU.add))
            step(V.tensor_scalar(tiles_i[:], tiles_i[:], P.bit_length() - 1, None, ALU.arith_shift_right))
            step(V.tensor_copy(tiles_f[:], tiles_i[:]))
            step(V.tensor_tensor_scan(tiles_end[:], zero1[:].to_broadcast([P, E]), tiles_f[:], 0.0, ALU.add, ALU.add))
            step(V.tensor_tensor(first_tile[:], tiles_end[:], tiles_f[:], ALU.subtract))
            step(V.tensor_scalar(run_t[:], first_tile[:], float(P), None, ALU.mult))
            step(V.tensor_tensor(pos_t, pos_t, over_t(run_t[:]), ALU.add))
            for k in range(TOP_K):
                step(V.tensor_tensor(tmp_t[:], pick[k][:], pos_t, ALU.mult))
                step(V.tensor_reduce(slot_f[:], tmp_t[:], AX_X, ALU.add))
                step(V.tensor_copy(slot_of[k][:], slot_f[:]))
                step(V.tensor_scalar(slot_blk[:], slot_of[k][:], P.bit_length() - 1, None, ALU.arith_shift_right))
                step(V.tensor_copy(slot_bf[:], slot_blk[:]))
                step(V.tensor_scalar(slot_f[:], slot_f[:], float(SLOT_TILES), None, ALU.mult))
                step(V.scalar_tensor_tensor(list_at[k][:], slot_bf[:], float(1 - P * SLOT_TILES), slot_f[:],
                                            ALU.mult, ALU.add))
            step(V.tensor_scalar(extra_pairs[:], tiles_end[:, E - 1:E], float(1 - FULL), None, ALU.add))
            step(V.tensor_scalar(extra_pairs[:], extra_pairs[:], 1, None, ALU.arith_shift_right))
            step(V.tensor_tensor(te_cmp, first_tile[:, None, :].to_broadcast([P, LISTED, E]),
                                 iota_j[:, :, None].to_broadcast([P, LISTED, E]), ALU.is_le))
            step(V.tensor_reduce(te_f[:], te_cmp, AX_X, ALU.add))
            V.tensor_scalar(tile_expert[:], te_f[:], -1.0, None, ALU.add).then_inc(S["lists_ready"], 1)
            dve.wait_ge(S["b12_loaded"], 16)
            step(V.tensor_scalar(te_f[:], te_f[:], -1.0, None, ALU.add))
            step(V.tensor_tensor(te_cmp, te_f[:, :, None].to_broadcast([P, LISTED, E]),
                                 iota_j[:, None, 0:E].to_broadcast([P, LISTED, E]), ALU.is_equal))
            for m in range(2):
                step(V.tensor_tensor(te_bias, te_cmp, b12[:, m:m + 1, :].to_broadcast([P, LISTED, E]), ALU.mult))
                ins = V.tensor_reduce(tile_b12[:, m, :], te_bias, AX_X, ALU.add)
                if m == 0:
                    step(ins)
            ins.then_inc(S["tile_b12_ready"], 1)
            dve.wait_ge(S["gateT_psum"], 1)
            dve.wait_ge(S["gateT_high_ready"], 4)
            for q in range(2):
                cols = slice(q * BANK, (q + 1) * BANK)
                ins = V.tensor_tensor(gateT[STACKED[2], cols], bank[6 + q][0:E + 1, :], gateT[STACKED[0], cols].bitcast(F32),
                                      ALU.subtract)
            ins.then_inc(S["gateT_ready"], 1)
            dve.wait_ge(S["b3_high_ready"], 2)
            V.tensor_tensor(b3_stack[STACKED[1], :], b3_all, b3_stack[STACKED[0], :].bitcast(F32), ALU.subtract
                            ).then_inc(S["b3_split"], 1)

            def search_start(h):
                dve.wait_ge(S["mag_ready"], (h + 1) * HALF)
                step(V.memset(low[h][:], 0.0))
                step(V.memset(high[h][:], 0.9 * I))
                step(V.tensor_scalar(high[h][:, 0, :], sums[h][:], 2.001 / I, None, ALU.mult))
                V.tensor_scalar(cur[h][:, 0, :], sums[h][:], 0.79 / I, None, ALU.mult).then_inc(thr_ready[h], 1)
                dve.wait_ge(thr_ready[h], 1)

            def count(h, i, at=None):
                ins = V.tensor_scalar(junk, mag[:, i, :], cur[h][:, 0, i:i + 1], None, ALU.is_le, ALU.add,
                                      accum_out=cur[h][:, 1, i:i + 1])
                step(ins) if at is None else link(ins, S["dve_step"], at)

            def narrow(h, n_round, at=None):
                n = [0]

                def done(ins):
                    n[0] += 1
                    step(ins) if at is None else link(ins, S["dve_step"], at + n[0])

                dve.wait_ge(act_counted[h], (n_round + 1) * (HALF - BY_DVE[h]))
                by_act = slice(BY_DVE[h], HALF)
                done(V.tensor_scalar(cur[h][:, 1, by_act], signs[h][:, by_act], 0.5, 0.5 * I, ALU.mult, ALU.add))
                c = cur[h][:, 1:2, :].to_broadcast([P, 2, HALF])
                done(V.scalar_tensor_tensor(span[:], c, float(N_DROP + WINDOW), cur[h][:], ALU.is_le, ALU.mult))
                done(V.tensor_tensor(low[h][:], low[h][:], span[:], ALU.max))
                done(V.tensor_scalar(span[:], c, float(N_DROP), BIG, ALU.is_lt, ALU.mult))
                done(V.tensor_tensor(span[:], span[:], cur[h][:], ALU.max))
                done(V.tensor_tensor(high[h][:], high[h][:], span[:], ALU.min))
                done(V.tensor_tensor(span[:], high[h][:], low[h][:], ALU.subtract))
                done(V.tensor_scalar(step_a[:], span[:, 1, :], 1.0, None, ALU.add))
                done(V.reciprocal(step_a[:], step_a[:]))
                done(V.scalar_tensor_tensor(step_b[:], low[h][:, 1, :], -(N_DROP + 0.5 * WINDOW + 0.75), span[:, 0, :],
                                            ALU.add, ALU.mult))
                done(V.tensor_tensor(step_b[:], step_b[:], step_a[:], ALU.mult))
                V.tensor_tensor(cur[h][:, 0, :], low[h][:, 0, :], step_b[:], ALU.subtract).then_inc(thr_ready[h], 1)
                dve.wait_ge(thr_ready[h], n_round + 2)

            NARROW = 11

            def largest_counted(h, i):
                step(V.scalar_tensor_tensor(work[:], mag[:, i, :], low[h][:, 0, i:i + 1], mag[:, i, :], ALU.is_le, ALU.mult))
                step(V.max(top8[:, i, :], work[:]))

            def exact_threshold(h):
                step(V.tensor_scalar(step_a[:], low[h][:, 1, :], -float(N_DROP), None, ALU.add))
                step(V.tensor_tensor(hit8[:], top8[:], low[h][:, 0, :, None].to_broadcast([P, HALF, 8]), ALU.is_equal))
                step(V.tensor_reduce(above[:], hit8[:], AX_X, ALU.add))
                by_act = slice(BY_DVE[h], HALF)
                step(V.scalar_tensor_tensor(step_a[:, by_act], above[:, by_act], 0.5, step_a[:, by_act], ALU.mult, ALU.add))
                step(V.tensor_tensor(hit8[:], iota_j[:, None, 0:8].to_broadcast([P, HALF, 8]),
                                     step_a[:, :, None].to_broadcast([P, HALF, 8]), ALU.subtract))
                step(V.scalar_tensor_tensor(hit8[:], hit8[:], 0.0, top8[:], ALU.is_ge, ALU.mult))
                step(V.tensor_reduce(cut[h][:], hit8[:], AX_X, ALU.max))

            def check_cut(h):
                step(V.tensor_tensor(hit8[:], top8[:], cut[h][:, :, None].to_broadcast([P, HALF, 8]), ALU.is_gt))
                step(V.tensor_reduce(above[:], hit8[:], AX_X, ALU.add))
                step(V.tensor_tensor(above[:], above[:], step_a[:], ALU.is_equal))
                step(V.scalar_tensor_tensor(above[:], step_a[:], 0.0, above[:], ALU.is_ge, ALU.mult))
                step(V.tensor_scalar(above[:], above[:], -1.0, 1.0, ALU.mult, ALU.add))
                V.tensor_reduce(bad[:], above[:], AX_X, ALU.add).then_inc(bad_ready[h], 1)

            def general_search(h):
                dve.wait_ge(bad_summed[h], 1)
                step(V.tensor_copy(bad_i[h][:], bad_all[:]))
                n_bad = dve.value_load(bad_i[h][0:1, 0:1], min_val=0, max_val=T)
                F = fall_step[h]
                with dve.If(n_bad > 0):
                    link(V.memset(bit_f[:], float(2 ** (BITS - 1))), F, 1)
                    link(V.memset(thr[:], 0), F, 2)
                    with dve.Fori(0, BITS) as bit:
                        at = bit * (HALF + 5) + 2
                        link(V.tensor_copy(bit_i[:], bit_f[:]), F, at + 1)
                        link(V.tensor_tensor(cand[:], thr[:], bit_i[:].to_broadcast([P, HALF]), ALU.bitwise_or), F, at + 2)
                        for i in range(HALF):
                            link(V.tensor_scalar(junk, mag[:, i, :], cand[:, i:i + 1].bitcast(F32), None, ALU.is_lt,
                                                 ALU.add, accum_out=cnt[:, i:i + 1]), F, at + 3 + i)
                        link(V.tensor_scalar(add[:], cnt[:], float(N_DROP), bit_f[:], ALU.is_lt, ALU.mult), F, at + HALF + 3)
                        link(V.tensor_tensor(thr[:], thr[:], add[:], ALU.bitwise_or), F, at + HALF + 4)
                        link(V.tensor_scalar(bit_f[:], bit_f[:], 0.5, None, ALU.mult), F, at + HALF + 5)
                    at = BITS * (HALF + 5) + 2
                    thr_f = thr[:].bitcast(F32)
                    for i in range(HALF):
                        link(V.tensor_scalar(junk, mag[:, i, :], thr_f[:, i:i + 1], None, ALU.is_lt, ALU.add,
                                             accum_out=cnt[:, i:i + 1]), F, at + 1 + i)
                    at += HALF + 1
                    link(V.tensor_scalar(need[:], cnt[:], -1.0, float(N_DROP), ALU.mult, ALU.add), F, at)
                    for i in range(HALF):
                        th = thr_f[:, i:i + 1]
                        link(V.tensor_scalar(eq, mag[:, i, :], th, None, ALU.is_equal), F, at + 1)
                        link(V.tensor_tensor_scan(ties, zero1[:].to_broadcast([P, I]), eq, 0.0, ALU.add, ALU.add), F, at + 2)
                        link(V.scalar_tensor_tensor(eq, ties, need[:, i:i + 1], eq, ALU.is_gt, ALU.mult), F, at + 3)
                        link(V.scalar_tensor_tensor(mag[:, i, :], mag[:, i, :], th, eq, ALU.is_gt, ALU.add), F, at + 4)
                        at += 4
                    link(V.memset(cut[h][:], 0.5), F, at + 1)

            def apply_mask(h, i):
                t = h * HALF + i
                V.scalar_tensor_tensor(s[:, t, :], mag[:, i, :], cut[h][:, i:i + 1], s[:, t, :], ALU.is_gt,
                                       ALU.mult).then_inc(S["s_masked"], 1)

            def mul_shared(u):
                c, half = u // 2, u % 2
                dve.wait_ge(S["ssil_ready"], u + 1)
                dve.wait_ge(S["shared_psum"], 2 * u + 2)
                V.scalar_tensor_tensor(shT[:, c, half * BANK:(half + 1) * BANK], bank[(4, 7)[u % 2]][:],
                                       sb12[:, SC + c:SC + c + 1], ssil[:, u % 2, :],
                                       ALU.add, ALU.mult).then_inc(S["shT_ready"], 1)

            def multiply_up(t):
                if t >= HALF:
                    dve.wait_ge(S["mag_ready"], t + 1)
                for c, (a, b) in enumerate(PIECES):
                    dve.wait_ge(S["up_psum"], t * NP_ + c + 1)
                    V.tensor_tensor(s[:, t, a:b], s[:, t, a:b], bank[3 * (t % 2) + c][:, 0:b - a],
                                    ALU.mult).then_inc(S["su_ready"], 1)

            search_start(0)
            for n in range(ROUNDS):
                for i in range(BY_DVE[0]):
                    count(0, i)
                if n >= 3:
                    mul_shared(n - 3)
                narrow(0, n)
            mul_shared(2 * SC - 1)
            for i in range(HALF):
                largest_counted(0, i)
                if i >= 2:
                    multiply_up(i - 2)
            exact_threshold(0)
            check_cut(0)
            dve.wait_ge(S["su_ready"], 2 * NP_)
            general_search(0)
            for i in range(2):
                apply_mask(0, i)
            for i in range(2, HALF):
                multiply_up(i)
                dve.wait_ge(S["su_ready"], (i + 1) * NP_)
                apply_mask(0, i)
            multiply_up(HALF)
            search_start(1)
            for n in range(UP_ROUNDS):
                for i in range(BY_DVE[1]):
                    count(1, i)
                narrow(1, n)
                multiply_up(HALF + 1 + n)

            def mul_h(j, b):
                dve.wait_ge(S["sil_ready"], j + 1)
                column = slice(j, j + 1) if isinstance(j, int) else bass.ds(j, 1)
                V.scalar_tensor_tensor(hT[:, b, :], bank[2 + b][:, P:2 * P], tile_b12[:, 1, column],
                                       sil[:, b, :], ALU.add, ALU.mult).then_inc(S["hT_ready"], 1)

            n_extra = extra(dve)
            for n in range(UP_ROUNDS, ROUNDS):
                j = (n - UP_ROUNDS) * 2
                for i in range(BY_DVE[1]):
                    count(1, i)
                    mul_h(j + i, i)
                narrow(1, n)
            j = (ROUNDS - UP_ROUNDS) * 2
            for i in range(HALF):
                largest_counted(1, i)
                mul_h(j + i, (j + i) % 2)
            exact_threshold(1)
            mul_h(j + HALF, (j + HALF) % 2)
            check_cut(1)
            mul_h(j + HALF + 1, (j + HALF + 1) % 2)
            general_search(1)
            for i in range(HALF):
                mul_h(j + HALF + 2 + i, (j + HALF + 2 + i) % 2)
                apply_mask(1, i)
                k = BY_POOL + i
                rows = slice(0, P if k < IC - 1 else I_LAST)
                dve.wait_ge(S["wd_high_ready"], len(DOWN_PARTS))
                V.tensor_tensor(down(w_low)[rows, k, :], down(w_raw)[rows, k, :], down(w_high)[rows, k, :].bitcast(F32),
                                ALU.subtract).then_inc(S["wd_split"], 1)
            with dve.If(n_extra > 0):
                with dve.Fori(0, PAIRS - FULL_PAIRS) as q:
                    with dve.If(q < n_extra):
                        for b in range(2):
                            mul_h(q * 2 + (FULL + b), b)

            def product_low(t):
                for q in range(3):
                    n = min(4, IC - 4 * q)
                    dve.wait_ge(S["sdT_high_ready"], 3 * t + q + 1)
                    cols = slice(4 * q * P, (4 * q + n) * P)
                    V.tensor_tensor(sdT_low[:, t % 2, cols], bank[q][:, 0:n * P],
                                    sdT_high[:, t % 2, cols].bitcast(F32), ALU.subtract).then_inc(S["sdT_split"], 1)

            def mix_experts(t):
                b = t % 2
                dve.wait_ge(yk_loaded[b], 16 * TOP_K * (t // 2 + 1))
                dve.wait_ge(S["z_psum"], t + 1)
                if t >= 1:
                    dve.wait_ge(S["g_ready"], t)
                step(V.scalar_tensor_tensor(mix, yk[0][:, b, :], val[0][:, t:t + 1], bank[Z_BANKS[b]][:], ALU.mult, ALU.add))
                V.scalar_tensor_tensor(mix, yk[1][:, b, :], val[1][:, t:t + 1], mix, ALU.mult,
                                       ALU.add).then_inc(S["mix_ready"], 1)

            def finish(t):
                b = t % 2
                dve.wait_ge(S["g_ready"], t + 1)
                dve.wait_ge(S["down_psum"], t + 1)
                if t >= 2:
                    dve.wait_ge(out_stored[b], 16 * (t // 2))
                step(V.tensor_tensor(o_sb[:, b, :], g, bank[DOWN_BANKS[b]][:], ALU.mult))
                dve.wait_ge(x_again[b], 16 * (t // 2 + 1))
                V.tensor_tensor(o_sb[:, b, :], o_sb[:, b, :], x_end[:, b, :], ALU.add).then_inc(S["o_ready"], 1)

            product_low(0)
            dve.wait_ge(S["z_high_ready"], 1)
            V.tensor_tensor(sw3_low[:], sw3[:], sw3_high[:].bitcast(F32), ALU.subtract).then_inc(S["z_split"], 1)
            dve.wait_ge(S["z_high_ready"], 2)
            V.tensor_tensor(shT_low[:], shT[:], shT_high[:].bitcast(F32), ALU.subtract).then_inc(S["z_split"], 1)
            for t in range(NT):
                if t + 1 < NT:
                    product_low(t + 1)
                mix_experts(t)
                finish(t)

        @block.tensor
        def _(pe):
            TE = nc.tensor
            pe.wait_ge(S["const_ready"], 11)
            def product3(dst, stat_high, stat_low, mov_high, mov_low, first, last):
                TE.matmul(dst, stat_high, mov_high, start=first, stop=False)
                TE.matmul(dst, stat_high, mov_low, start=False, stop=False)
                return TE.matmul(dst, stat_low, mov_high, start=False, stop=last)

            def transpose_rows(t):
                pe.wait_ge(S["xn_ready"], t + 1)
                if t >= 4:
                    pe.wait_ge(S["xnT_split"], t - 3)
                for k in range(HC):
                    ins = TE.transpose(xnT_bank(t)[:, k, :], xn[:, t, k * P:(k + 1) * P], ident[:])
                ins.then_inc(S["xnT_psum"], 1)

            def project(t, c, dst):
                a, b = PIECES[c]
                for k in range(HC):
                    rows = slice(t * P, (t + 1) * P)
                    ins = product3(dst[:, 0:b - a], xnT_high[:, k, rows], xnT_low[:, k, rows],
                                   proj(w_high)[:, k, a:b], proj(w_low)[:, k, a:b], k == 0, k == HC - 1)
                return ins

            for t in range(HALF):
                transpose_rows(t)
            for n, (t, c) in enumerate(GATE_UNITS):
                if n == 3:
                    for later in range(HALF, NT):
                        transpose_rows(later)
                if c == 0 or t == 0:
                    pe.wait_ge(S["xnT_split"], t + 1)
                    pe.wait_ge(S["w_split"], c + 1)
                if n >= NP_:
                    pe.wait_ge(S["s_ready"], n - NP_ + 1)
                project(t, c, bank[n % NP_]).then_inc(S["gate_psum"], 1)
                if n == 4:
                    pe.wait_ge(S["xnT_split"], NT)
                    pe.wait_ge(S["rw_split"], 1)
                    for b in range(2):
                        for k in range(HC):
                            cols = slice(b * BANK, (b + 1) * BANK)
                            ins = product3(bank[6 + b][0:E, :], rw_high[:, k, :], rw_low[:, k, :], xnT_high[:, k, cols],
                                           xnT_low[:, k, cols], k == 0, k == HC - 1)
                    ins.then_inc(S["logitsT_psum"], 1)
                if n == 5:
                    pe.wait_ge(S["logitsT_ready"], 1)
                    for q in range(NT):
                        ins = TE.transpose(bank[5][:, q * E:(q + 1) * E], logitsT[:, q * P:(q + 1) * P], ident[0:E, 0:E])
                    ins.then_inc(S["logits_ready"], 1)
                if (t, c) == (HALF - 1, NP_ - 1):
                    pe.wait_ge(S["picks_ready"], 1)
                    flat = hits[:].rearrange("p t e -> p (t e)")
                    TE.matmul(bank[5][:, P:2 * P], before[:], flat, start=True, stop=True)
                    TE.matmul(bank[5][:, 2 * P:3 * P], ones[:], flat, start=True, stop=True).then_inc(S["rank_ready"], 1)
                    pe.wait_ge(S["gates_ready"], 1)
                    for q in range(NT):
                        ins = TE.transpose(bank[6 + q // 4][0:E + 1, (q % 4) * P:(q % 4 + 1) * P], gates[:, q, :], ident[:])
                    ins.then_inc(S["gateT_psum"], 1)

            pe.wait_ge(S["sw12_split"], 1)
            pe.wait_ge(S["gateT_ready"], 1)
            for u in range(2 * SC):
                c, half = u // 2, u % 2
                for m in range(2):
                    if u >= 2:
                        pe.wait_ge(S["shT_ready"], u - 1)
                    dst = bank[((3, 4), (6, 7))[u % 2][m]]
                    for k in range(HC):
                        rows, cols = slice(c * P, (c + 1) * P), slice(half * BANK, (half + 1) * BANK)
                        ins = product3(dst[:], sw12_high[:, m * HC + k, rows], sw12_low[:, m * HC + k, rows],
                                       xnT_high[:, k, cols], xnT_low[:, k, cols], k == 0, k == HC - 1)
                    ins.then_inc(S["shared_psum"], 1)

            for t in range(NT):
                for c in range(NP_):
                    if t == 0:
                        pe.wait_ge(S["w_split"], NP_ + c + 1)
                        if c == 0:
                            pe.wait_ge(S["s_ready"], NT * NP_)
                    elif t == 1:
                        pe.wait_ge(S["shT_ready"], 2 * SC)
                    else:
                        pe.wait_ge(S["su_ready"], (t - 2) * NP_ + c + 1)
                    project(t, c, bank[3 * (t % 2) + c]).then_inc(S["up_psum"], 1)

            def transpose_xg(j, b, loaded):
                pe.wait_ge(xg_loaded[b], loaded)
                for k in range(HC):
                    ins = TE.transpose(bank[b][:, k * P:(k + 1) * P], xg[:, b, k * P:(k + 1) * P], ident[:])
                ins.then_inc(S["xgT_psum"], 1)

            def project_h(j, b, loaded):
                pe.wait_ge(S["xgT_ready"], j + 1)
                pe.wait_ge(w12_loaded[b], loaded)
                for m in range(2):
                    for k in range(HC):
                        ins = TE.matmul(bank[2 + b][:, m * P:(m + 1) * P], w12[:, b, (m * HC + k) * M:(m * HC + k + 1) * M],
                                        xgT[:, b, k * P:(k + 1) * P], start=(k == 0), stop=(k == HC - 1))
                ins.then_inc(S["h_psum"], 1)

            def project_y(j, b, loaded, emptied):
                pe.wait_ge(S["hT_ready"], j + 1)
                pe.wait_ge(w3_loaded[b], loaded)
                if emptied is not None:
                    pe.wait_ge(S["y_ready"], emptied)
                TE.matmul(bank[4 + b][:], hT[:, b, :], w3[:, b, 0:H], start=True,
                          stop=True).then_inc(S["y_psum"], 1)

            def pair(p):
                first, second = (isinstance(p, int) and p == n for n in range(2))
                for b in range(2):
                    transpose_xg(p * 2 + b, b, p * 16 + 16)
                for b in range(2):
                    if not first:
                        project_y(p * 2 - 2 + b, b, p * 16, None if second else p * 2 - 3 + b)
                    project_h(p * 2 + b, b, p * 16 + 16)

            n_extra = extra(pe)
            pe.wait_ge(S["su_ready"], NT * NP_)
            pair(0)
            pair(1)
            with pe.Fori(2, FULL_PAIRS) as p:
                pair(p)
            with pe.If(n_extra > 0):
                with pe.Fori(0, PAIRS - FULL_PAIRS) as q:
                    with pe.If(q < n_extra):
                        pair(q + FULL_PAIRS)
            def transpose_products(t):
                pe.wait_ge(S["s_masked"], t + 1)
                for q in range(3):
                    if t >= 1:
                        pe.wait_ge(S["sdT_split"], 3 * (t - 1) + q + 1)
                    for k in range(4 * q, min(4 * q + 4, IC)):
                        a, b = CHUNKS[k]
                        ins = TE.transpose(bank[q][0:b - a, (k % 4) * P:(k % 4 + 1) * P], s[:, t, a:b], ident[:])
                    ins.then_inc(S["sdT_psum"], 1)

            pe.wait_ge(S["hT_ready"], n_extra * 2 + (FULL - 1))
            transpose_products(0)
            for b in range(2):
                project_y(n_extra * 2 + (FULL - 2 + b), b, n_extra * 16 + FULL_PAIRS * 16, n_extra * 2 + (FULL - 3 + b))
            def shared_third(t):
                if t >= 2:
                    pe.wait_ge(S["mix_ready"], t - 1)
                dst, rows = bank[Z_BANKS[t % 2]], slice(t * P, (t + 1) * P)
                TE.matmul(dst[:], gateT[:, rows], b3_stack[:], start=True, stop=False)
                for k in range(SC):
                    ins = product3(dst[:], shT_high[:, k, rows], shT_low[:, k, rows], sw3_high[:, k, :], sw3_low[:, k, :],
                                   False, k == SC - 1)
                ins.then_inc(S["z_psum"], 1)

            for t in range(NT):
                if t + 1 < NT:
                    transpose_products(t + 1)
                if t >= 1:
                    shared_third(t)
                if t == 0:
                    pe.wait_ge(S["wd_split"], IC)
                elif t >= 2:
                    pe.wait_ge(S["o_ready"], t - 1)
                for k in range(IC):
                    a, b = CHUNKS[k]
                    if k % 4 == 0:
                        pe.wait_ge(S["sdT_split"], 3 * t + k // 4 + 1)
                    cols = slice(k * P, (k + 1) * P)
                    ins = product3(bank[DOWN_BANKS[t % 2]][:], sdT_high[0:b - a, t % 2, cols], sdT_low[0:b - a, t % 2, cols],
                                   down(w_high)[0:b - a, k, :], down(w_low)[0:b - a, k, :], k == 0, k == IC - 1)
                ins.then_inc(S["down_psum"], 1)
                if t == 0:
                    pe.wait_ge(S["b3_split"], 1)
                    pe.wait_ge(S["z_split"], 2)
                    pe.wait_ge(S["y_ready"], n_extra * 2 + FULL)
                    shared_third(0)


def kernel(L0_attn_x, L0_attn_w_gate, L0_attn_w_up, L0_attn_w_down, L0_ffn_router_w, L0_ffn_router_b,
           L0_ffn_router_bias, L0_ffn_ew1, L0_ffn_eb1, L0_ffn_ew2, L0_ffn_eb2, L0_ffn_ew3, L0_ffn_eb3,
           L0_ffn_sw1, L0_ffn_sb1, L0_ffn_sw2, L0_ffn_sb2, L0_ffn_sw3, L0_ffn_sb3):
    import numpy as np
    import concourse.bacc as bacc
    from concourse.bass_utils import run_bass_kernel_spmd

    x = np.asarray(L0_attn_x)
    B, S_, H = x.shape
    ew1, ew2, ew3 = (np.asarray(w) for w in (L0_ffn_ew1, L0_ffn_ew2, L0_ffn_ew3))
    E, _, M = ew1.shape

    def by_partition(w):
        return w.reshape(E, H // P, P, M).transpose(0, 2, 1, 3).reshape(E * P, H // P * M)

    expert_w12 = np.concatenate([by_partition(ew1), by_partition(ew2)], axis=1)
    expert_b12 = np.concatenate([np.asarray(L0_ffn_eb1).T, np.asarray(L0_ffn_eb2).T], axis=1)
    sb1, sb2 = (np.asarray(b).reshape(-1, P).T for b in (L0_ffn_sb1, L0_ffn_sb2))
    arrays = {
        "x": x.reshape(B * S_, H),
        "w_gate_t": np.asarray(L0_attn_w_gate).T,
        "w_up_t": np.asarray(L0_attn_w_up).T,
        "w_down_t": np.asarray(L0_attn_w_down).T,
        "router_w": np.asarray(L0_ffn_router_w),
        "router_b": np.asarray(L0_ffn_router_b).reshape(1, E),
        "router_bias": np.asarray(L0_ffn_router_bias).reshape(1, E),
        "expert_w12": expert_w12,
        "expert_w3": ew3.reshape(E * M, H),
        "expert_b12": expert_b12,
        "expert_b3": np.asarray(L0_ffn_eb3),
        "shared_w12": np.concatenate([np.asarray(L0_ffn_sw1), np.asarray(L0_ffn_sw2)], axis=0),
        "shared_b12": np.concatenate([sb1, sb2], axis=1),
        "shared_w3": np.asarray(L0_ffn_sw3),
        "shared_b3": np.asarray(L0_ffn_sb3).reshape(1, H),
    }
    arrays = {n: np.ascontiguousarray(a) for n, a in arrays.items()}
    nc = bacc.Bacc("TRN2", target_bir_lowering=False, num_devices=1)
    args = [nc.dram_tensor(n, a.shape, mybir.dt.from_np(a.dtype), kind="ExternalInput").ap() for n, a in arrays.items()]
    out = nc.dram_tensor("out", (B * S_, H), F32, kind="ExternalOutput").ap()
    gated_block_kernel(nc, *args, out)
    r = run_bass_kernel_spmd(nc, [arrays], core_ids=[0])
    return r.results[0]["out"].reshape(B, S_, H)
```

```python
from contextlib import ExitStack

import concourse.bass as bass
from concourse import mybir

F32 = mybir.dt.float32
F32R = mybir.dt.float32r
BF16 = mybir.dt.bfloat16
I32 = mybir.dt.int32
ALU = mybir.AluOpType
ACT = mybir.ActivationFunctionType
AX_X = mybir.AxisListType.X

P = 128
EPS = 1e-5
GROUPS, GROUP_LIMIT, TOP_K = 4, 2, 2
KEEP_FACTOR = 0.5
BIG = 3e38
BANK = 512


def gated_block_kernel(nc, x, w_gate_t, w_up_t, w_down_t, router_w, router_b, router_bias, expert_w12,
                       expert_w3, expert_b12, expert_b3, shared_w12, shared_b12, shared_w3, shared_b3, out):
    T, H = x.shape
    I = w_gate_t.shape[1]
    E = router_w.shape[1]
    M = P
    SM = shared_w3.shape[0]
    NT = T // P
    HC = H // P
    IC = -(-I // P)
    I_LAST = I - (IC - 1) * P
    SC = SM // P
    N_DROP = int(KEEP_FACTOR * I)
    PER_GROUP = E // GROUPS
    FULL = T * TOP_K // P
    SLOT_TILES = FULL + E
    SLOTS = SLOT_TILES * P
    LISTED = SLOT_TILES + 2
    TABLES = max(4 * NT * E, LISTED * E)
    PAIRS, FULL_PAIRS = SLOT_TILES // 2, FULL // 2
    W12 = 2 * HC * M
    PIECES = [(a, min(a + BANK, I)) for a in range(0, I, BANK)]
    NP_ = len(PIECES)
    HALF = NT // 2
    GATE_SPLITS = 1 + HC + NP_ - 1
    BITS = 31
    ROUNDS = 6
    STACKED = [slice(32 * n, 32 * n + E + 1) for n in range(3)]
    STACK = 64 + E + 1
    X_PARTS = ((0, 2), (2, HALF), (HALF, NT))
    BY_DVE = (2, 2)
    BY_POOL = IC - HALF
    UP_ROUNDS = 3
    WINDOW = 7
    CHUNKS = [(k * P, min((k + 1) * P, I)) for k in range(IC)]
    assert (ROUNDS - UP_ROUNDS) * 2 + 2 * HALF + 2 == FULL and BY_DVE[1] == 2
    assert FULL_PAIRS % 2 == 0 and PAIRS % 2 == 0
    assert HC == HALF and H == BANK and FULL % 2 == 0 and E % 2 == 0 and T == 8 * P and I % 2 == 0

    with ExitStack() as ctx:
        def sb(name, shape, dt=F32):
            return ctx.enter_context(nc.sbuf_tensor(name, shape, dt))

        def sem(name):
            return ctx.enter_context(nc.semaphore(name))

        bank = [ctx.enter_context(nc.psum_tensor(f"bank{i}", [P, BANK], F32)) for i in range(8)]

        xn_rows = nc.dram_tensor("xn_rows", [T, H], F32).ap()
        slot_token_dram = nc.dram_tensor("slot_token_dram", [SLOTS, 1], I32).ap()
        slot_y = nc.dram_tensor("slot_y", [SLOTS, H], F32).ap()

        def overlay(*layouts):
            made = []
            for layout in layouts[:-1]:
                with ExitStack() as phase:
                    made += [phase.enter_context(nc.sbuf_tensor(n, shape, dt)) for n, shape, dt in layout]
            return made + [sb(n, shape, dt) for n, shape, dt in layouts[-1]]

        W_SIZE = max(HC * (I + E), IC * H)
        w_high = sb("w_high", [P, W_SIZE], F32R)
        w_raw, w_low = overlay([("w_raw", [P, W_SIZE], F32)], [("w_low", [P, W_SIZE], F32R)])
        proj = lambda w: w[:, 0:HC * (I + E)].rearrange("p (k n) -> p k n", k=HC)
        down = lambda w: w[:, 0:IC * H].rearrange("p (k n) -> p k n", k=IC)
        sw12_raw, sw12_low, w12 = overlay([("sw12_raw", [P, 2 * HC, SM], F32)], [("sw12_low", [P, 2 * HC, SM], F32R)],
                                          [("w12", [P, 2, W12], F32)])
        x_late, sw12_high, xg, xgT = overlay([("x_late", [P, HALF, H], F32)], [("sw12_high", [P, 2 * HC, SM], F32R)],
                                     [("xg", [P, 2, H], F32), ("xgT", [P, 2, H], F32)])
        sw3, sw3_low = overlay([("sw3", [P, SC, H], F32)], [("sw3_low", [P, SC, H], F32R)])
        sb12 = sb("sb12", [P, 2 * SC])
        rw = sb("rw", [P, HC, E])
        b3_stack = sb("b3_stack", [STACK, H], F32R)
        rb_all = sb("rb_all", [P, 2, E])
        xg_more, sdT_high, mix_g, xnT_high = overlay(
            [("xg_more", [P, 2, H], F32)], [("sdT_high", [P, 2, IC * P], F32R), ("mix_g", [P, 2, H], F32)],
            [("xnT_high", [P, HC, T], F32R)])
        sdT_low, x_end, xnT_low = overlay([("sdT_low", [P, 2, IC * P], F32R), ("x_end", [P, 2, H], F32)],
                                          [("xnT_low", [P, HC, T], F32R)])
        mix, g = mix_g[:, 0, :], mix_g[:, 1, :]
        s = sb("s", [P, NT, I])
        wg_raw = s[:, NT - HC:NT, :]
        w3 = sb("w3", [P, 2, H])
        b12 = sb("b12", [P, 2, E])
        tile_b12 = sb("tile_b12", [P, 2, LISTED])
        x_early = s[:].rearrange("p t n -> p (t n)")[:, 0:HALF * H].rearrange("p (t h) -> p t h", t=HALF)
        x_tiles = lambda a, b: x_early[:, a:b, :] if b <= HALF else x_late[:, a - HALF:b - HALF, :]
        shT_high, sw3_high, mag_rows = overlay([("shT_high", [P, SC, T], F32R), ("sw3_high", [P, SC, H], F32R)],
                                               [("mag_rows", [P, HALF * I], F32)])
        mag = mag_rows[:].rearrange("p (t n) -> p t n", t=HALF)
        xn = mag_rows[:, 0:NT * H].rearrange("p (t h) -> p t h", t=NT)
        shT, shT_low = overlay([("shT", [P, SC, T], F32)], [("shT_low", [P, SC, T], F32R)])
        gateT = sb("gateT", [STACK, T], F32R)
        ident = sb("ident", [P, P])
        before = sb("before", [P, P])
        ones = sb("ones", [P, P])
        zero1 = sb("zero1", [P, 1])

        stats = sb("stats", [P, NT, 6])
        mv = sb("mv", [P, NT, 2])
        ln = sb("ln", [P, 3, NT])

        sc_t = sb("sc_t", [P, NT, E])
        spare = sb("spare", [P, TABLES + LISTED * E])
        table = lambda n: spare[:, n * NT * E:(n + 1) * NT * E].rearrange("p (t e) -> p t e", t=NT)
        ex_t = table(0)
        tmp_t = sb("tmp_t", [P, NT, E])
        msk_t = table(1)
        pick = [sb(f"pick{k}", [P, NT, E]) for k in range(TOP_K)]
        hits = sb("hits", [P, NT, E])
        pos_t = table(2)
        tot_t = table(3)
        run_t = sb("run_t", [P, E])
        tiles_i = sb("tiles_i", [P, E], I32)
        tiles_f = sb("tiles_f", [P, E])
        tiles_end = sb("tiles_end", [P, E])
        first_tile = sb("first_tile", [P, E])
        gm = sb("gm", [P, NT, GROUPS])
        gtmp = sb("gtmp", [P, NT, GROUPS])
        gpick = [sb(f"gpick{k}", [P, NT, GROUPS]) for k in range(GROUP_LIMIT)]
        red = sb("red", [P, NT])
        red2 = sb("red2", [P, NT])
        val = [sb(f"val{k}", [P, NT]) for k in range(TOP_K)]
        gates = sb("gates", [P, NT, E + 1])
        rank_e = sb("rank_e", [P, E])
        iota_j = sb("iota_j", [P, LISTED])
        iota_i = sb("iota_i", [P, LISTED], I32)
        te_cmp = spare[:, TABLES:TABLES + LISTED * E].rearrange("p (j e) -> p j e", e=E)
        te_bias = spare[:, 0:LISTED * E].rearrange("p (j e) -> p j e", e=E)
        te_f = sb("te_f", [P, LISTED])
        tile_expert = sb("tile_expert", [P, LISTED], I32)
        slot_f = sb("slot_f", [P, NT])
        slot_of = [sb(f"slot_of{k}", [P, NT], I32) for k in range(TOP_K)]
        slot_blk = sb("slot_blk", [P, NT], I32)
        slot_bf = sb("slot_bf", [P, NT])
        list_at = [sb(f"list_at{k}", [P, NT], I32) for k in range(TOP_K)]
        extra_pairs = sb("extra_pairs", [P, 1], I32)
        token_no = sb("token_no", [P, NT], I32)
        zero_list = sb("zero_list", [P, SLOT_TILES], I32)
        slot_token = sb("slot_token", [P, SLOT_TILES], I32)

        low = [sb(f"low{h}", [P, 2, HALF]) for h in range(2)]
        high = [sb(f"high{h}", [P, 2, HALF]) for h in range(2)]
        cur = [sb(f"cur{h}", [P, 2, HALF]) for h in range(2)]
        sums = [sb(f"sums{h}", [P, HALF]) for h in range(2)]
        signs = [sb(f"signs{h}", [P, HALF]) for h in range(2)]
        span = sb("span", [P, 2, HALF])
        step_a = sb("step_a", [P, HALF])
        step_b = sb("step_b", [P, HALF])
        top8 = sb("top8", [P, HALF, 8])
        hit8 = sb("hit8", [P, HALF, 8])
        cut = [sb(f"cut{h}", [P, HALF]) for h in range(2)]
        above = sb("above", [P, HALF])
        bad = sb("bad", [P, 1])
        bad_all = sb("bad_all", [P, 1])
        bad_i = [sb(f"bad_i{h}", [P, 1], I32) for h in range(2)]
        cnt = sb("cnt", [P, HALF])
        thr = sb("thr", [P, HALF], I32)
        cand = sb("cand", [P, HALF], I32)
        add = sb("add", [P, HALF], I32)
        bit_f = sb("bit_f", [P, 1])
        bit_i = sb("bit_i", [P, 1], I32)
        need = sb("need", [P, HALF])
        work = sb("work", [P, I])
        junk = work[:].bitcast(BF16)[:, 0:I]
        eq = work[:].bitcast(BF16)[:, I:2 * I]
        act_junk = sb("act_junk", [P, I], BF16)
        ties = act_junk[:].bitcast(mybir.dt.int16)

        sil = sb("sil", [P, 2, P])
        hT = sb("hT", [P, 2, P])
        y_sb = sb("y_sb", [P, 2, H])
        ssil = y_sb
        b3_all = y_sb[0:E + 1, 1, :]

        xg_slots = [xg[:, 0, :], xg[:, 1, :], xg_more[:, 0, :], xg_more[:, 1, :]]
        yk = [xg, xgT]
        o_sb = y_sb

        names = """const_ready x_loaded0 x_loaded1 x_loaded2 rw_loaded router_loaded gate_w_loaded0 gate_w_loaded1 gate_w_loaded2
            up_w_loaded0 up_w_loaded1 up_w_loaded2 shared_loaded down_w_loaded0 down_w_loaded1 down_w_loaded2 down_w_loaded3
            ln_var ln_root xn_ready xn_stored xnT_psum xnT_high_ready xnT_split w_high_ready w_split
            sw12_high_ready sw12_split wd_high_ready wd_split
            logits_ready exp_in exp_out picks_ready
            rank_ready gates_ready gateT_psum gateT_high_ready gateT_ready b3_high_ready b3_split z_high_ready z_split lists_ready b12_loaded tile_b12_ready list_zeroed list_scattered list_loaded
            gate_psum s_ready mag_ready thr_ready0 thr_ready1 act_counted0 act_counted1 bad_ready0 bad_ready1
            bad_summed0 bad_summed1 fall_step0 fall_step1 s_masked
            shared_psum ssil_ready shT_ready
            w12_loaded0 w12_loaded1 w3_loaded0 w3_loaded1 xg_loaded0 xg_loaded1 xg_loaded2 xg_loaded3 xgT_psum xgT_ready
            h_psum sil_ready hT_ready y_psum y_ready y_stored0 y_stored1 all_y_stored y_zero y_zeroed
            up_psum su_ready sdT_psum sdT_high_ready sdT_split down_psum z_psum yk_loaded0 yk_loaded1
            x_again0 x_again1 mix_ready g_ready o_ready out_stored0 out_stored1 dve_step""".split()
        S = {n: sem(n) for n in names}
        pair_of = lambda n: [S[n + "0"], S[n + "1"]]
        x_loaded = [S[f"x_loaded{n}"] for n in range(len(X_PARTS))]
        out_stored, yk_loaded = pair_of("out_stored"), pair_of("yk_loaded")
        w12_loaded, w3_loaded = pair_of("w12_loaded"), pair_of("w3_loaded")
        xg_loaded = [S[f"xg_loaded{n}"] for n in range(4)]
        y_stored, x_again = pair_of("y_stored"), pair_of("x_again")
        thr_ready, act_counted = pair_of("thr_ready"), pair_of("act_counted")
        gate_w_loaded = [S[f"gate_w_loaded{c}"] for c in range(NP_)]
        down_w_loaded = [S[f"down_w_loaded{n}"] for n in range(4)]
        up_w_loaded = [S[f"up_w_loaded{c}"] for c in range(NP_)]
        bad_ready, bad_summed, fall_step = pair_of("bad_ready"), pair_of("bad_summed"), pair_of("fall_step")

        LAST = NP_ - 1
        assert NP_ == 3
        GATE_UNITS = [(t, LAST) for t in range(NT)] + [(t, c) for t in range(NT) for c in range(LAST)]
        tile_done = lambda t: max(n for n, u in enumerate(GATE_UNITS) if u[0] == t) + 1

        DOWN_BANKS, Z_BANKS = (3, 6), (7, 4)
        xnT_bank = lambda t: bank[(3, 4, 6, 7)[t % 4]][:].rearrange("p (k m) -> p k m", k=HC)

        DOWN_PARTS = [(slice(0, P), slice(k, min(k + 4, IC - 1))) for k in range(0, IC - 1, 4)] + \
                     [(slice(0, I_LAST), slice(IC - 1, IC))]

        def extra(eng):
            eng.wait_ge(S["lists_ready"], 1)
            return eng.value_load(extra_pairs[0:1, 0:1], min_val=0, max_val=PAIRS - FULL_PAIRS)

        block = ctx.enter_context(nc.Block())

        @block.sync
        def _(sp):
            def load_gate_piece(c):
                a, b = PIECES[c]
                sp.dma_start(wg_raw[:, :, a:b], w_gate_t[:, a:b].rearrange("(k p) n -> p k n", p=P)
                             ).then_inc(gate_w_loaded[c], 16)

            def load_x(n):
                a, b = X_PARTS[n]
                sp.dma_start(x_tiles(a, b), x[a * P:b * P, :].rearrange("(t p) n -> p t n", p=P)
                             ).then_inc(x_loaded[n], 16)

            load_x(0)
            load_x(1)
            sp.dma_start(rw[:], router_w.rearrange("(k p) e -> p k e", p=P)).then_inc(S["rw_loaded"], 16)
            load_gate_piece(LAST)
            load_x(2)
            load_gate_piece(0)
            sp.dma_start(rb_all[:, 0, :], router_b.broadcast_to([P, E])).then_inc(S["router_loaded"], 16)
            sp.dma_start(rb_all[:, 1, :], router_bias.broadcast_to([P, E])).then_inc(S["router_loaded"], 16)
            load_gate_piece(1)
            sp.dma_start(b12[:], expert_b12.rearrange("p (m e) -> p m e", m=2)).then_inc(S["b12_loaded"], 16)
            sp.wait_ge(S["xn_ready"], NT)
            sp.dma_start(xn_rows.rearrange("(t p) n -> p t n", p=P), xn).then_inc(S["xn_stored"], 16)
            sp.dma_start(sw12_raw[:], shared_w12.rearrange("(k p) n -> p k n", p=P)).then_inc(S["shared_loaded"], 16)
            sp.dma_start(sw3[:], shared_w3.rearrange("(k p) n -> p k n", p=P)).then_inc(S["shared_loaded"], 16)
            sp.dma_start(sb12[:], shared_b12).then_inc(S["shared_loaded"], 16)
            sp.dma_start(b3_all[0:E, :], expert_b3).then_inc(S["shared_loaded"], 16)
            sp.dma_start(b3_all[E:E + 1, :], shared_b3).then_inc(S["shared_loaded"], 16)
            sp.wait_ge(S["y_zero"], 1)
            sp.dma_start(slot_y[FULL * P:SLOTS, :].rearrange("(j p) n -> p j n", p=P),
                         y_sb[:, 0:1, :].to_broadcast([P, SLOT_TILES - FULL, H])).then_inc(S["y_zeroed"], 16)

            def expert_of(j):
                return sp.value_load(tile_expert[0:1, bass.ds(j, 1)], min_val=0, max_val=E - 1)

            def load_w12(j, b, there=None):
                e = expert_of(j)

                def load():
                    sp.dma_start(w12[:, b, :], expert_w12[bass.ds(e * P, P), :]).then_inc(w12_loaded[b], 16)

                if there is None:
                    load()
                else:
                    with sp.If(e == there):
                        sp.sem_inc(w12_loaded[b], 16)
                    with sp.If(e != there):
                        load()
                return e

            def load_w3(j, b):
                e = expert_of(j)
                sp.dma_start(w3[:, b, :], expert_w3[bass.ds(e * P, P), :]).then_inc(w3_loaded[b], 16)
                return e

            def store_y(j, b):
                sp.dma_start(slot_y[bass.ds(j * P, P), :], y_sb[:, b, :]).then_inc(y_stored[b], 16)

            def serve_pair(p):
                for b in range(2):
                    j = p * 2 + b
                    sp.wait_ge(S["y_psum"], j - 1)
                    there = load_w3(j, b)
                    sp.wait_ge(S["h_psum"], j + 1)
                    load_w12(j + 2, b, there)
                    sp.wait_ge(S["y_ready"], j - 1)
                    store_y(j - 2, b)

            sp.wait_ge(S["gate_psum"], NT * NP_)
            for c, (a, b) in enumerate(PIECES):
                sp.dma_start(proj(w_raw)[:, :, a:b], w_up_t[:, a:b].rearrange("(k p) n -> p k n", p=P)
                             ).then_inc(up_w_loaded[c], 16)
            n_extra = extra(sp)
            sp.wait_ge(S["shared_psum"], 4 * SC)
            there = [load_w12(b, b) for b in range(2)]
            for b in range(2):
                load_w3(b, b)
            def load_down_part(n):
                rows, chunks = DOWN_PARTS[n]
                first = chunks.start * P
                src = w_down_t[first:min(chunks.stop * P, I), :]
                sp.dma_start(down(w_raw)[rows, chunks, :], src.rearrange("(k p) n -> p k n", p=rows.stop)
                             ).then_inc(down_w_loaded[n], 16)

            for b in range(2):
                sp.wait_ge(S["h_psum"], b + 1)
                load_w12(b + 2, b, there[b])
            load_down_part(0)
            serve_pair(1)
            load_down_part(1)
            serve_pair(2)
            load_down_part(2)
            load_down_part(3)
            with sp.Fori(3, FULL_PAIRS) as p:
                serve_pair(p)
            with sp.If(n_extra > 0):
                with sp.Fori(0, PAIRS - FULL_PAIRS) as q:
                    with sp.If(q < n_extra):
                        serve_pair(q + FULL_PAIRS)
            last = n_extra * 2 + FULL
            for b in range(2):
                sp.wait_ge(S["y_ready"], last - 1 + b)
                store_y(last - 2 + b, b)
            for b in range(2):
                sp.wait_ge(y_stored[b], (n_extra + FULL_PAIRS) * 16)
            sp.sem_inc(S["all_y_stored"], 1)

            for t in range(2):
                sp.dma_start(x_end[:, t, :], x[t * P:(t + 1) * P, :]).then_inc(x_again[t], 16)
            for t in range(NT):
                sp.wait_ge(S["o_ready"], t + 1)
                sp.dma_start(out[t * P:(t + 1) * P, :], o_sb[:, t % 2, :]).then_inc(out_stored[t % 2], 16)
                if t + 2 < NT:
                    sp.dma_start(x_end[:, t % 2, :], x[(t + 2) * P:(t + 3) * P, :]).then_inc(x_again[t % 2], 16)
            for b in range(2):
                sp.wait_ge(out_stored[b], 16 * (NT // 2))

        @block.gpsimd
        def _(pool):
            pool.memset(y_sb[:, 0, :], 0.0).then_inc(S["y_zero"], 1)
            pool.memset(ident[:], 0.0).then_inc(S["const_ready"], 1)
            pool.memset(ones[:], 1.0).then_inc(S["const_ready"], 1)
            pool.memset(zero1[:], 0.0).then_inc(S["const_ready"], 1)
            pool.memset(zero_list[:], 0).then_inc(S["const_ready"], 1)
            pool.iota(token_no[:], [[P, NT]], base=0, channel_multiplier=1).then_inc(S["const_ready"], 1)
            pool.iota(iota_i[:], [[1, LISTED]], base=0, channel_multiplier=0).then_inc(S["const_ready"], 1)
            pool.memset(gates[:, :, E:E + 1], 1.0).then_inc(S["const_ready"], 1)
            pool.memset(gateT[:].bitcast(F32), 0.0).then_inc(S["const_ready"], 1)
            pool.memset(b3_stack[:].bitcast(F32), 0.0).then_inc(S["const_ready"], 1)
            pool.wait_ge(S["const_ready"], 9)
            pool.affine_select(out=ident[:], in_=ident[:], compare_op=ALU.not_equal, fill=1.0, base=0,
                               pattern=[[-1, P]], channel_multiplier=1).then_inc(S["const_ready"], 1)
            pool.affine_select(out=before[:], in_=ones[:], compare_op=ALU.is_gt, fill=0.0, base=0,
                               pattern=[[1, P]], channel_multiplier=-1).then_inc(S["const_ready"], 1)
            list_view = slot_token_dram.rearrange("(p j) a -> p (j a)", p=P)
            pool.dma_start(list_view, zero_list[:]).then_inc(S["list_zeroed"], 16)

            def low_piece(src, c, done, rows=slice(0, HC)):
                a, b = PIECES[c]
                pool.wait_ge(S["w_high_ready"], done)
                pool.tensor_tensor(proj(w_low)[:, rows, a:b], src[:, rows, a:b], proj(w_high)[:, rows, a:b].bitcast(F32),
                                   ALU.subtract).then_inc(S["w_split"], 1)

            pool.wait_ge(S["w_high_ready"], 1)
            pool.tensor_tensor(proj(w_low)[:, :, I:I + E], rw[:], proj(w_high)[:, :, I:I + E].bitcast(F32), ALU.subtract
                               ).then_inc(S["w_split"], 1)
            for k in range(HC):
                low_piece(wg_raw, LAST, k + 2, slice(k, k + 1))
            for c in range(LAST):
                low_piece(wg_raw, c, HC + c + 2)
            pool.wait_ge(S["sw12_high_ready"], 1)
            pool.tensor_tensor(sw12_low[:], sw12_raw[:], sw12_high[:].bitcast(F32), ALU.subtract).then_inc(S["sw12_split"], 1)

            pool.wait_ge(S["list_zeroed"], 16)
            n_extra = extra(pool)
            for t in range(NT):
                for k in range(TOP_K):
                    pool.indirect_dma_start(
                        out=slot_token_dram, out_offset=bass.IndirectOffsetOnAxis(ap=list_at[k][:, t:t + 1], axis=0),
                        in_=token_no[:, t:t + 1], in_offset=None).then_inc(S["list_scattered"], 16)
            pool.wait_ge(S["list_scattered"], 16 * NT * TOP_K)
            pool.dma_start(slot_token[:], list_view).then_inc(S["list_loaded"], 16)
            pool.wait_ge(S["list_loaded"], 16)
            pool.wait_ge(S["xn_stored"], 16)

            for c in range(NP_):
                low_piece(proj(w_raw), c, GATE_SPLITS + c + 1)
            pool.wait_ge(S["shared_psum"], 4 * SC)

            def gather_tokens(j):
                if j >= 4:
                    pool.wait_ge(S["xgT_psum"], j - 3)
                elif j == 2:
                    pool.wait_ge(S["up_psum"], NT * NP_)
                pool.indirect_dma_start(
                    out=xg_slots[j % 4], out_offset=None, in_=xn_rows,
                    in_offset=bass.IndirectOffsetOnAxis(ap=slot_token[:, j:j + 1], axis=0)
                ).then_inc(xg_loaded[j % 4], 16)

            def sum_bad(h):
                pool.wait_ge(bad_ready[h], 1)
                pool.partition_all_reduce(bad_all[:], bad[:], P, bass.bass_isa.ReduceOp.add).then_inc(bad_summed[h], 1)

            def low_down(k):
                pool.wait_ge(S["wd_high_ready"], k // 4 + 1)
                rows = slice(0, P if k < IC - 1 else I_LAST)
                pool.tensor_tensor(down(w_low)[rows, k, :], down(w_raw)[rows, k, :], down(w_high)[rows, k, :].bitcast(F32),
                                   ALU.subtract).then_inc(S["wd_split"], 1)

            for j in range(FULL):
                gather_tokens(j)
                if j == 1:
                    sum_bad(0)
                if j == 13:
                    sum_bad(1)
            for k in range(BY_POOL):
                low_down(k)
            for q in range(PAIRS - FULL_PAIRS):
                with pool.If(n_extra > q):
                    for b in range(2):
                        gather_tokens(FULL + 2 * q + b)

            pool.wait_ge(S["all_y_stored"], 1)
            for t in range(NT):
                if t >= 2:
                    pool.wait_ge(S["mix_ready"], t - 1)
                for k in range(TOP_K):
                    pool.indirect_dma_start(
                        out=yk[k][:, t % 2, :], out_offset=None, in_=slot_y,
                        in_offset=bass.IndirectOffsetOnAxis(ap=slot_of[k][:, t:t + 1], axis=0)
                    ).then_inc(yk_loaded[t % 2], 16)

        @block.scalar
        def _(act):
            unit = [0]

            def silu_gate():
                n = unit[0]
                t, c = GATE_UNITS[n]
                a, b = PIECES[c]
                act.wait_ge(S["gate_psum"], n + 1)
                if n == 0:
                    act.wait_ge(S["xn_ready"], HALF)
                if c == LAST:
                    nc.scalar.activation(sc_t[:, t, :], bank[n % NP_][:, b - a:b - a + E], ACT.Copy
                                         ).then_inc(S["logits_ready"], 1)
                if (t, c) in ((NT - HC, LAST), (NT - HC, 0)):
                    act.wait_ge(S["w_split"], 1 + HC if c == LAST else GATE_SPLITS)
                nc.scalar.activation(s[:, t, a:b], bank[unit[0] % NP_][:, 0:b - a], ACT.Silu).then_inc(S["s_ready"], 1)
                unit[0] += 1
                if t < HALF and unit[0] == tile_done(t):
                    magnitude(0, t)

            def magnitude(h, i):
                t = h * HALF + i
                act.wait_ge(S["s_ready"], tile_done(t))
                if t == 0:
                    act.wait_ge(S["xn_stored"], 16)
                    act.wait_ge(S["xnT_psum"], NT)
                nc.scalar.activation(mag[:, i, :], s[:, t, :], ACT.Abs, accum_out=sums[h][:, i:i + 1]
                                     ).then_inc(S["mag_ready"], 1)

            def high_piece(src, c, rows=slice(0, HC)):
                a, b = PIECES[c]
                nc.scalar.activation(proj(w_high)[:, rows, a:b], src[:, rows, a:b], ACT.Copy).then_inc(S["w_high_ready"], 1)

            def count_tile(h, i, n_round):
                act.wait_ge(thr_ready[h], n_round + 1)
                before_it = n_round * (HALF - BY_DVE[h]) + i - BY_DVE[h]
                if before_it > 0:
                    act.wait_ge(act_counted[h], before_it)
                nc.scalar.activation(act_junk[:], mag[:, i, :], ACT.Sign, bias=cur[h][:, 0, i:i + 1], scale=-1.0,
                                     accum_out=signs[h][:, i:i + 1]).then_inc(act_counted[h], 1)

            def count_tiles(h, n_round):
                for i in range(BY_DVE[h], HALF):
                    count_tile(h, i, n_round)

            def ln_root(b):
                act.wait_ge(S["ln_var"], b + 1)
                nc.scalar.activation(ln[:, 1, b * HALF:(b + 1) * HALF], ln[:, 0, b * HALF:(b + 1) * HALF],
                                     ACT.Sqrt).then_inc(S["ln_root"], 1)

            def transposed_high(t):
                act.wait_ge(S["xnT_psum"], t + 1)
                nc.scalar.activation(xnT_high[:, :, t * P:(t + 1) * P], xnT_bank(t),
                                     ACT.Copy).then_inc(S["xnT_high_ready"], 1)

            ln_root(0)
            act.wait_ge(S["rw_loaded"], 16)
            nc.scalar.activation(proj(w_high)[:, :, I:I + E], rw[:], ACT.Copy).then_inc(S["w_high_ready"], 1)
            act.wait_ge(gate_w_loaded[LAST], 16)
            for k in range(HC):
                high_piece(wg_raw, LAST, slice(k, k + 1))
            for t in range(HALF):
                transposed_high(t)
            ln_root(1)
            silu_gate()
            act.wait_ge(gate_w_loaded[0], 16)
            high_piece(wg_raw, 0)
            while unit[0] < HALF - 1:
                silu_gate()
            for t in range(HALF, NT):
                transposed_high(t)
            silu_gate()
            act.wait_ge(gate_w_loaded[1], 16)
            high_piece(wg_raw, 1)
            while unit[0] < NT + 1:
                silu_gate()
            act.wait_ge(S["exp_in"], 1)
            nc.scalar.activation(ex_t, tmp_t[:], ACT.Exp).then_inc(S["exp_out"], 1)
            while unit[0] < tile_done(HALF - 1):
                silu_gate()
            act.wait_ge(S["shared_loaded"], 16 * 5)
            act.wait_ge(S["xn_ready"], NT)
            nc.scalar.activation(sw12_high[:], sw12_raw[:], ACT.Copy).then_inc(S["sw12_high_ready"], 1)
            act.wait_ge(S["const_ready"], 11)
            for n in (0, 2):
                nc.scalar.activation(b3_stack[STACKED[n], :], b3_all, ACT.Copy).then_inc(S["b3_high_ready"], 1)
            act.wait_ge(S["gateT_psum"], 1)
            for n in range(2):
                for q in range(2):
                    nc.scalar.activation(gateT[STACKED[n], q * BANK:(q + 1) * BANK], bank[6 + q][0:E + 1, :], ACT.Copy
                                         ).then_inc(S["gateT_high_ready"], 1)
            for t in range(HALF, NT):
                while unit[0] < tile_done(t):
                    silu_gate()
                if t < NT - 1:
                    count_tiles(0, t - HALF)

            act.wait_ge(S["y_zeroed"], 16)
            act.wait_ge(S["b3_split"], 1)
            for u in range(2 * SC):
                c = u // 2
                if HALF - 1 + u < ROUNDS:
                    count_tiles(0, HALF - 1 + u)
                act.wait_ge(S["shared_psum"], 2 * u + 1)
                if u >= 2:
                    act.wait_ge(S["shT_ready"], u - 1)
                nc.scalar.activation(ssil[:, u % 2, :], bank[(3, 6)[u % 2]][:], ACT.Silu,
                                     bias=sb12[:, c:c + 1]).then_inc(S["ssil_ready"], 1)
                if u < NP_:
                    act.wait_ge(up_w_loaded[u], 16)
                    high_piece(proj(w_raw), u)

            for i in range(HALF):
                act.wait_ge(S["s_masked"], i + 1)
                magnitude(1, i)
            for n in range(UP_ROUNDS):
                count_tiles(1, n)

            def copy_xgT(j, b):
                act.wait_ge(S["xgT_psum"], j + 1)
                nc.scalar.activation(xgT[:, b, :], bank[b][:], ACT.Copy).then_inc(S["xgT_ready"], 1)

            column = lambda j: slice(j, j + 1) if isinstance(j, int) else bass.ds(j, 1)

            def silu_h(j, b):
                act.wait_ge(S["h_psum"], j + 1)
                nc.scalar.activation(sil[:, b, :], bank[2 + b][:, 0:P], ACT.Silu,
                                     bias=tile_b12[:, 0, column(j)]).then_inc(S["sil_ready"], 1)

            def copy_y(j, b, stored):
                act.wait_ge(S["y_psum"], j + 1)
                if stored is not None:
                    act.wait_ge(y_stored[b], stored)
                nc.scalar.activation(y_sb[:, b, :], bank[4 + b][:], ACT.Copy).then_inc(S["y_ready"], 1)

            def pair(p, n_round=None, parts=()):
                first, second = (isinstance(p, int) and p == n for n in range(2))
                for b in range(2):
                    copy_xgT(p * 2 + b, b)
                for b in range(2):
                    if not first:
                        copy_y(p * 2 - 2 + b, b, None if second else p * 16 - 16)
                    if n_round is not None:
                        count_tile(1, BY_DVE[1] + b, n_round)
                    if parts:
                        rows, chunks = DOWN_PARTS[parts[b]]
                        act.wait_ge(down_w_loaded[parts[b]], 16)
                        nc.scalar.activation(down(w_high)[rows, chunks, :], down(w_raw)[rows, chunks, :], ACT.Copy
                                             ).then_inc(S["wd_high_ready"], 1)
                    silu_h(p * 2 + b, b)

            n_extra = extra(act)
            act.wait_ge(S["tile_b12_ready"], 1)
            for n in range(UP_ROUNDS, ROUNDS):
                pair(n - UP_ROUNDS, n)
            for n in range(2):
                pair(ROUNDS - UP_ROUNDS + n, parts=(2 * n, 2 * n + 1))
            with act.Fori(ROUNDS - UP_ROUNDS + 2, FULL_PAIRS) as p:
                pair(p)
            with act.If(n_extra > 0):
                with act.Fori(0, PAIRS - FULL_PAIRS) as q:
                    with act.If(q < n_extra):
                        pair(q + FULL_PAIRS)
            def product_high(t):
                for q in range(3):
                    n = min(4, IC - 4 * q)
                    act.wait_ge(S["sdT_psum"], 3 * t + q + 1)
                    if q == 0 and t >= 2:
                        act.wait_ge(S["down_psum"], t - 1)
                    nc.scalar.activation(sdT_high[:, t % 2, 4 * q * P:(4 * q + n) * P],
                                         bank[q][:, 0:n * P], ACT.Copy).then_inc(S["sdT_high_ready"], 1)

            product_high(0)
            for b in range(2):
                copy_y(n_extra * 2 + (FULL - 2 + b), b, n_extra * 16 + (FULL_PAIRS - 1) * 16)
            act.wait_ge(S["s_masked"], NT)
            nc.scalar.activation(sw3_high[:], sw3[:], ACT.Copy).then_inc(S["z_high_ready"], 1)
            nc.scalar.activation(shT_high[:], shT[:], ACT.Copy).then_inc(S["z_high_ready"], 1)
            for t in range(NT):
                if t + 1 < NT:
                    product_high(t + 1)
                act.wait_ge(S["mix_ready"], t + 1)
                if t >= 1:
                    act.wait_ge(S["o_ready"], t)
                nc.scalar.activation(g, mix, ACT.Silu).then_inc(S["g_ready"], 1)

        @block.vector
        def _(dve):
            V = nc.vector
            steps = [0]

            def step(ins):
                steps[0] += 1
                ins.then_inc(S["dve_step"], 1)
                dve.wait_ge(S["dve_step"], steps[0])

            def link(ins, sem_, at):
                ins.then_inc(sem_, 1)
                dve.wait_ge(sem_, at)

            def transposed_low(t):
                dve.wait_ge(S["xnT_high_ready"], t + 1)
                V.tensor_tensor(xnT_low[:, :, t * P:(t + 1) * P], xnT_bank(t),
                                xnT_high[:, :, t * P:(t + 1) * P].bitcast(F32), ALU.subtract).then_inc(S["xnT_split"], 1)

            def normalise(b):
                for t in range(b * HALF, (b + 1) * HALF):
                    for n, part in enumerate(X_PARTS):
                        if part[0] == t:
                            dve.wait_ge(x_loaded[n], 16)
                    V.bn_stats(stats[:, t, :], x_tiles(t, t + 1)[:, 0, :]).then_inc(S["dve_step"], 1)
                steps[0] += HALF
                dve.wait_ge(S["dve_step"], steps[0])
                for t in range(b * HALF, (b + 1) * HALF):
                    V.bn_aggr(mv[:, t, :], stats[:, t, :]).then_inc(S["dve_step"], 1)
                steps[0] += HALF
                dve.wait_ge(S["dve_step"], steps[0])
                V.tensor_scalar(ln[:, 0, b * HALF:(b + 1) * HALF], mv[:, b * HALF:(b + 1) * HALF, 1], EPS, None,
                                ALU.add).then_inc(S["ln_var"], 1)
                var, r, u = (ln[:, q, b * HALF:(b + 1) * HALF] for q in range(3))
                dve.wait_ge(S["ln_root"], b + 1)
                step(V.reciprocal(r, r))
                step(V.tensor_tensor(u, r, r, ALU.mult))
                step(V.tensor_tensor(u, u, var, ALU.mult))
                step(V.tensor_scalar(u, u, -0.5, 1.5, ALU.mult, ALU.add))
                step(V.tensor_tensor(r, r, u, ALU.mult))
                for t in range(b * HALF, (b + 1) * HALF):
                    V.tensor_scalar(xn[:, t, :], x_tiles(t, t + 1)[:, 0, :], mv[:, t, 0:1], ln[:, 1, t:t + 1], ALU.subtract,
                                    ALU.mult).then_inc(S["xn_ready"], 1)

            normalise(0)
            for t in range(HALF):
                transposed_low(t)
            normalise(1)
            for t in range(HALF, NT):
                transposed_low(t)

            dve.wait_ge(S["const_ready"], 11)
            step(V.tensor_scalar(rank_e[:], iota_i[:, 0:E], -1.0, float(E), ALU.mult, ALU.add))
            step(V.tensor_copy(iota_j[:], iota_i[:]))
            dve.wait_ge(S["router_loaded"], 16 * 2)
            dve.wait_ge(S["logits_ready"], NT)
            over_t = lambda v: v[:, None, :].to_broadcast([P, NT, E])
            over_e = lambda v, n=E: v[:, :, None].to_broadcast([P, NT, n])
            step(V.tensor_tensor(sc_t[:], sc_t[:], over_t(rb_all[:, 0, :]), ALU.add))
            step(V.tensor_reduce(red[:], sc_t[:], AX_X, ALU.max))
            V.tensor_tensor(tmp_t[:], sc_t[:], over_e(red[:]), ALU.subtract).then_inc(S["exp_in"], 1)
            dve.wait_ge(S["exp_out"], 1)
            step(V.tensor_reduce(red[:], ex_t, AX_X, ALU.add))
            step(V.reciprocal(red[:], red[:]))
            step(V.tensor_tensor(sc_t[:], ex_t, over_e(red[:]), ALU.mult))
            step(V.tensor_tensor(sc_t[:], sc_t[:], over_t(rb_all[:, 1, :]), ALU.add))

            def first_max(onehot, table, tmp, n):
                weight = rank_e[:, E - n:E]
                w = weight[:, None, :].to_broadcast([P, NT, n])
                step(V.tensor_reduce(red[:], table, AX_X, ALU.max))
                step(V.tensor_tensor(tmp, table, over_e(red[:], n), ALU.is_equal))
                step(V.tensor_tensor(tmp, tmp, w, ALU.mult))
                step(V.tensor_reduce(red2[:], tmp, AX_X, ALU.max))
                step(V.tensor_tensor(onehot, w, over_e(red2[:], n), ALU.is_equal))

            step(V.tensor_reduce(gm[:], sc_t[:].rearrange("p t (g e) -> p t g e", g=GROUPS), AX_X, ALU.max))
            first_max(gpick[0][:], gm[:], gtmp[:], GROUPS)
            step(V.scalar_tensor_tensor(gm[:], gpick[0][:], -BIG, gm[:], ALU.mult, ALU.add))
            first_max(gpick[1][:], gm[:], gtmp[:], GROUPS)
            step(V.tensor_tensor(gtmp[:], gpick[0][:], gpick[1][:], ALU.add))
            step(V.tensor_scalar(gtmp[:], gtmp[:], BIG, -BIG, ALU.mult, ALU.add))
            step(V.tensor_tensor(msk_t.rearrange("p t (g e) -> p t g e", g=GROUPS),
                                 sc_t[:].rearrange("p t (g e) -> p t g e", g=GROUPS),
                                 gtmp[:, :, :, None].to_broadcast([P, NT, GROUPS, PER_GROUP]), ALU.add))
            first_max(pick[0][:], msk_t, tmp_t[:], E)
            step(V.scalar_tensor_tensor(msk_t, pick[0][:], -BIG, msk_t, ALU.mult, ALU.add))
            first_max(pick[1][:], msk_t, tmp_t[:], E)
            V.tensor_tensor(hits[:], pick[0][:], pick[1][:], ALU.add).then_inc(S["picks_ready"], 1)
            for k in range(TOP_K):
                step(V.tensor_tensor(tmp_t[:], pick[k][:], sc_t[:], ALU.mult))
                step(V.tensor_reduce(val[k][:], tmp_t[:], AX_X, ALU.add))
            step(V.tensor_tensor(tmp_t[:], pick[0][:], over_e(val[0][:]), ALU.mult))
            step(V.tensor_tensor(msk_t, pick[1][:], over_e(val[1][:]), ALU.mult))
            V.tensor_tensor(gates[:, :, 0:E], tmp_t[:], msk_t, ALU.add).then_inc(S["gates_ready"], 1)

            dve.wait_ge(S["rank_ready"], 1)
            rank_ps = bank[5][:, P:2 * P].rearrange("p (t e) -> p t e", t=NT)
            total_ps = bank[5][:, 2 * P:3 * P].rearrange("p (t e) -> p t e", t=NT)
            step(V.tensor_copy(tot_t, total_ps))
            step(V.memset(run_t[:], 0.0))
            for t in range(NT):
                step(V.tensor_tensor(pos_t[:, t, :], run_t[:], rank_ps[:, t, :], ALU.add))
                step(V.tensor_tensor(run_t[:], run_t[:], tot_t[:, t, :], ALU.add))
            step(V.tensor_scalar(tiles_i[:], run_t[:], float(P - 1), None, ALU.add))
            step(V.tensor_scalar(tiles_i[:], tiles_i[:], P.bit_length() - 1, None, ALU.arith_shift_right))
            step(V.tensor_copy(tiles_f[:], tiles_i[:]))
            step(V.tensor_tensor_scan(tiles_end[:], zero1[:].to_broadcast([P, E]), tiles_f[:], 0.0, ALU.add, ALU.add))
            step(V.tensor_tensor(first_tile[:], tiles_end[:], tiles_f[:], ALU.subtract))
            step(V.tensor_scalar(run_t[:], first_tile[:], float(P), None, ALU.mult))
            step(V.tensor_tensor(pos_t, pos_t, over_t(run_t[:]), ALU.add))
            for k in range(TOP_K):
                step(V.tensor_tensor(tmp_t[:], pick[k][:], pos_t, ALU.mult))
                step(V.tensor_reduce(slot_f[:], tmp_t[:], AX_X, ALU.add))
                step(V.tensor_copy(slot_of[k][:], slot_f[:]))
                step(V.tensor_scalar(slot_blk[:], slot_of[k][:], P.bit_length() - 1, None, ALU.arith_shift_right))
                step(V.tensor_copy(slot_bf[:], slot_blk[:]))
                step(V.tensor_scalar(slot_f[:], slot_f[:], float(SLOT_TILES), None, ALU.mult))
                step(V.scalar_tensor_tensor(list_at[k][:], slot_bf[:], float(1 - P * SLOT_TILES), slot_f[:],
                                            ALU.mult, ALU.add))
            step(V.tensor_scalar(extra_pairs[:], tiles_end[:, E - 1:E], float(1 - FULL), None, ALU.add))
            step(V.tensor_scalar(extra_pairs[:], extra_pairs[:], 1, None, ALU.arith_shift_right))
            step(V.tensor_tensor(te_cmp, first_tile[:, None, :].to_broadcast([P, LISTED, E]),
                                 iota_j[:, :, None].to_broadcast([P, LISTED, E]), ALU.is_le))
            step(V.tensor_reduce(te_f[:], te_cmp, AX_X, ALU.add))
            V.tensor_scalar(tile_expert[:], te_f[:], -1.0, None, ALU.add).then_inc(S["lists_ready"], 1)
            dve.wait_ge(S["b12_loaded"], 16)
            step(V.tensor_scalar(te_f[:], te_f[:], -1.0, None, ALU.add))
            step(V.tensor_tensor(te_cmp, te_f[:, :, None].to_broadcast([P, LISTED, E]),
                                 iota_j[:, None, 0:E].to_broadcast([P, LISTED, E]), ALU.is_equal))
            for m in range(2):
                step(V.tensor_tensor(te_bias, te_cmp, b12[:, m:m + 1, :].to_broadcast([P, LISTED, E]), ALU.mult))
                ins = V.tensor_reduce(tile_b12[:, m, :], te_bias, AX_X, ALU.add)
                if m == 0:
                    step(ins)
            ins.then_inc(S["tile_b12_ready"], 1)
            dve.wait_ge(S["gateT_psum"], 1)
            dve.wait_ge(S["gateT_high_ready"], 4)
            for q in range(2):
                cols = slice(q * BANK, (q + 1) * BANK)
                ins = V.tensor_tensor(gateT[STACKED[2], cols], bank[6 + q][0:E + 1, :], gateT[STACKED[0], cols].bitcast(F32),
                                      ALU.subtract)
            ins.then_inc(S["gateT_ready"], 1)
            dve.wait_ge(S["b3_high_ready"], 2)
            V.tensor_tensor(b3_stack[STACKED[1], :], b3_all, b3_stack[STACKED[0], :].bitcast(F32), ALU.subtract
                            ).then_inc(S["b3_split"], 1)

            def search_start(h):
                dve.wait_ge(S["mag_ready"], (h + 1) * HALF)
                step(V.memset(low[h][:], 0.0))
                step(V.memset(high[h][:], 0.9 * I))
                step(V.tensor_scalar(high[h][:, 0, :], sums[h][:], 2.001 / I, None, ALU.mult))
                V.tensor_scalar(cur[h][:, 0, :], sums[h][:], 0.79 / I, None, ALU.mult).then_inc(thr_ready[h], 1)
                dve.wait_ge(thr_ready[h], 1)

            def count(h, i, at=None):
                ins = V.tensor_scalar(junk, mag[:, i, :], cur[h][:, 0, i:i + 1], None, ALU.is_le, ALU.add,
                                      accum_out=cur[h][:, 1, i:i + 1])
                step(ins) if at is None else link(ins, S["dve_step"], at)

            def narrow(h, n_round, at=None):
                n = [0]

                def done(ins):
                    n[0] += 1
                    step(ins) if at is None else link(ins, S["dve_step"], at + n[0])

                dve.wait_ge(act_counted[h], (n_round + 1) * (HALF - BY_DVE[h]))
                by_act = slice(BY_DVE[h], HALF)
                done(V.tensor_scalar(cur[h][:, 1, by_act], signs[h][:, by_act], 0.5, 0.5 * I, ALU.mult, ALU.add))
                c = cur[h][:, 1:2, :].to_broadcast([P, 2, HALF])
                done(V.scalar_tensor_tensor(span[:], c, float(N_DROP + WINDOW), cur[h][:], ALU.is_le, ALU.mult))
                done(V.tensor_tensor(low[h][:], low[h][:], span[:], ALU.max))
                done(V.tensor_scalar(span[:], c, float(N_DROP), BIG, ALU.is_lt, ALU.mult))
                done(V.tensor_tensor(span[:], span[:], cur[h][:], ALU.max))
                done(V.tensor_tensor(high[h][:], high[h][:], span[:], ALU.min))
                done(V.tensor_tensor(span[:], high[h][:], low[h][:], ALU.subtract))
                done(V.tensor_scalar(step_a[:], span[:, 1, :], 1.0, None, ALU.add))
                done(V.reciprocal(step_a[:], step_a[:]))
                done(V.scalar_tensor_tensor(step_b[:], low[h][:, 1, :], -(N_DROP + 0.5 * WINDOW + 0.75), span[:, 0, :],
                                            ALU.add, ALU.mult))
                done(V.tensor_tensor(step_b[:], step_b[:], step_a[:], ALU.mult))
                V.tensor_tensor(cur[h][:, 0, :], low[h][:, 0, :], step_b[:], ALU.subtract).then_inc(thr_ready[h], 1)
                dve.wait_ge(thr_ready[h], n_round + 2)


            def largest_counted(h, i):
                step(V.scalar_tensor_tensor(work[:], mag[:, i, :], low[h][:, 0, i:i + 1], mag[:, i, :], ALU.is_le, ALU.mult))
                step(V.max(top8[:, i, :], work[:]))

            def exact_threshold(h):
                step(V.tensor_scalar(step_a[:], low[h][:, 1, :], -float(N_DROP), None, ALU.add))
                step(V.tensor_tensor(hit8[:], top8[:], low[h][:, 0, :, None].to_broadcast([P, HALF, 8]), ALU.is_equal))
                step(V.tensor_reduce(above[:], hit8[:], AX_X, ALU.add))
                by_act = slice(BY_DVE[h], HALF)
                step(V.scalar_tensor_tensor(step_a[:, by_act], above[:, by_act], 0.5, step_a[:, by_act], ALU.mult, ALU.add))
                step(V.tensor_tensor(hit8[:], iota_j[:, None, 0:8].to_broadcast([P, HALF, 8]),
                                     step_a[:, :, None].to_broadcast([P, HALF, 8]), ALU.subtract))
                step(V.scalar_tensor_tensor(hit8[:], hit8[:], 0.0, top8[:], ALU.is_ge, ALU.mult))
                step(V.tensor_reduce(cut[h][:], hit8[:], AX_X, ALU.max))

            def check_cut(h):
                step(V.tensor_tensor(hit8[:], top8[:], cut[h][:, :, None].to_broadcast([P, HALF, 8]), ALU.is_gt))
                step(V.tensor_reduce(above[:], hit8[:], AX_X, ALU.add))
                step(V.tensor_tensor(above[:], above[:], step_a[:], ALU.is_equal))
                step(V.scalar_tensor_tensor(above[:], step_a[:], 0.0, above[:], ALU.is_ge, ALU.mult))
                step(V.tensor_scalar(above[:], above[:], -1.0, 1.0, ALU.mult, ALU.add))
                V.tensor_reduce(bad[:], above[:], AX_X, ALU.add).then_inc(bad_ready[h], 1)

            def general_search(h):
                dve.wait_ge(bad_summed[h], 1)
                step(V.tensor_copy(bad_i[h][:], bad_all[:]))
                n_bad = dve.value_load(bad_i[h][0:1, 0:1], min_val=0, max_val=T)
                F = fall_step[h]
                with dve.If(n_bad > 0):
                    link(V.memset(bit_f[:], float(2 ** (BITS - 1))), F, 1)
                    link(V.memset(thr[:], 0), F, 2)
                    with dve.Fori(0, BITS) as bit:
                        at = bit * (HALF + 5) + 2
                        link(V.tensor_copy(bit_i[:], bit_f[:]), F, at + 1)
                        link(V.tensor_tensor(cand[:], thr[:], bit_i[:].to_broadcast([P, HALF]), ALU.bitwise_or), F, at + 2)
                        for i in range(HALF):
                            link(V.tensor_scalar(junk, mag[:, i, :], cand[:, i:i + 1].bitcast(F32), None, ALU.is_lt,
                                                 ALU.add, accum_out=cnt[:, i:i + 1]), F, at + 3 + i)
                        link(V.tensor_scalar(add[:], cnt[:], float(N_DROP), bit_f[:], ALU.is_lt, ALU.mult), F, at + HALF + 3)
                        link(V.tensor_tensor(thr[:], thr[:], add[:], ALU.bitwise_or), F, at + HALF + 4)
                        link(V.tensor_scalar(bit_f[:], bit_f[:], 0.5, None, ALU.mult), F, at + HALF + 5)
                    at = BITS * (HALF + 5) + 2
                    thr_f = thr[:].bitcast(F32)
                    for i in range(HALF):
                        link(V.tensor_scalar(junk, mag[:, i, :], thr_f[:, i:i + 1], None, ALU.is_lt, ALU.add,
                                             accum_out=cnt[:, i:i + 1]), F, at + 1 + i)
                    at += HALF + 1
                    link(V.tensor_scalar(need[:], cnt[:], -1.0, float(N_DROP), ALU.mult, ALU.add), F, at)
                    for i in range(HALF):
                        th = thr_f[:, i:i + 1]
                        link(V.tensor_scalar(eq, mag[:, i, :], th, None, ALU.is_equal), F, at + 1)
                        link(V.tensor_tensor_scan(ties, zero1[:].to_broadcast([P, I]), eq, 0.0, ALU.add, ALU.add), F, at + 2)
                        link(V.scalar_tensor_tensor(eq, ties, need[:, i:i + 1], eq, ALU.is_gt, ALU.mult), F, at + 3)
                        link(V.scalar_tensor_tensor(mag[:, i, :], mag[:, i, :], th, eq, ALU.is_gt, ALU.add), F, at + 4)
                        at += 4
                    link(V.memset(cut[h][:], 0.5), F, at + 1)

            def apply_mask(h, i):
                t = h * HALF + i
                V.scalar_tensor_tensor(s[:, t, :], mag[:, i, :], cut[h][:, i:i + 1], s[:, t, :], ALU.is_gt,
                                       ALU.mult).then_inc(S["s_masked"], 1)

            def mul_shared(u):
                c, half = u // 2, u % 2
                dve.wait_ge(S["ssil_ready"], u + 1)
                dve.wait_ge(S["shared_psum"], 2 * u + 2)
                V.scalar_tensor_tensor(shT[:, c, half * BANK:(half + 1) * BANK], bank[(4, 7)[u % 2]][:],
                                       sb12[:, SC + c:SC + c + 1], ssil[:, u % 2, :],
                                       ALU.add, ALU.mult).then_inc(S["shT_ready"], 1)

            def multiply_up(t):
                if t >= HALF:
                    dve.wait_ge(S["mag_ready"], t + 1)
                for c, (a, b) in enumerate(PIECES):
                    dve.wait_ge(S["up_psum"], t * NP_ + c + 1)
                    V.tensor_tensor(s[:, t, a:b], s[:, t, a:b], bank[3 * (t % 2) + c][:, 0:b - a],
                                    ALU.mult).then_inc(S["su_ready"], 1)

            search_start(0)
            for n in range(ROUNDS):
                for i in range(BY_DVE[0]):
                    count(0, i)
                if n >= 3:
                    mul_shared(n - 3)
                narrow(0, n)
            mul_shared(2 * SC - 1)
            for i in range(HALF):
                largest_counted(0, i)
                if i % 2:
                    multiply_up(i // 2)
            exact_threshold(0)
            check_cut(0)
            dve.wait_ge(S["su_ready"], 2 * NP_)
            general_search(0)
            for i in range(2):
                apply_mask(0, i)
            for i in range(2, HALF):
                multiply_up(i)
                dve.wait_ge(S["su_ready"], (i + 1) * NP_)
                apply_mask(0, i)
            multiply_up(HALF)
            search_start(1)
            for n in range(UP_ROUNDS):
                for i in range(BY_DVE[1]):
                    count(1, i)
                if n < UP_ROUNDS - 1:
                    narrow(1, n)
                multiply_up(HALF + 1 + n)
            narrow(1, UP_ROUNDS - 1)

            def mul_h(j, b):
                dve.wait_ge(S["sil_ready"], j + 1)
                column = slice(j, j + 1) if isinstance(j, int) else bass.ds(j, 1)
                V.scalar_tensor_tensor(hT[:, b, :], bank[2 + b][:, P:2 * P], tile_b12[:, 1, column],
                                       sil[:, b, :], ALU.add, ALU.mult).then_inc(S["hT_ready"], 1)

            n_extra = extra(dve)
            for n in range(UP_ROUNDS, ROUNDS):
                j = (n - UP_ROUNDS) * 2
                for i in range(BY_DVE[1]):
                    count(1, i)
                    mul_h(j + i, i)
                narrow(1, n)
            j = (ROUNDS - UP_ROUNDS) * 2
            for i in range(HALF):
                largest_counted(1, i)
                mul_h(j + i, (j + i) % 2)
            exact_threshold(1)
            mul_h(j + HALF, (j + HALF) % 2)
            check_cut(1)
            mul_h(j + HALF + 1, (j + HALF + 1) % 2)
            general_search(1)
            for i in range(HALF):
                mul_h(j + HALF + 2 + i, (j + HALF + 2 + i) % 2)
                if i < HALF - 1:
                    apply_mask(1, i)
                k = BY_POOL + i
                rows = slice(0, P if k < IC - 1 else I_LAST)
                dve.wait_ge(S["wd_high_ready"], len(DOWN_PARTS))
                V.tensor_tensor(down(w_low)[rows, k, :], down(w_raw)[rows, k, :], down(w_high)[rows, k, :].bitcast(F32),
                                ALU.subtract).then_inc(S["wd_split"], 1)
            with dve.If(n_extra > 0):
                with dve.Fori(0, PAIRS - FULL_PAIRS) as q:
                    with dve.If(q < n_extra):
                        for b in range(2):
                            mul_h(q * 2 + (FULL + b), b)

            def product_low(t):
                for q in range(3):
                    n = min(4, IC - 4 * q)
                    dve.wait_ge(S["sdT_high_ready"], 3 * t + q + 1)
                    cols = slice(4 * q * P, (4 * q + n) * P)
                    V.tensor_tensor(sdT_low[:, t % 2, cols], bank[q][:, 0:n * P],
                                    sdT_high[:, t % 2, cols].bitcast(F32), ALU.subtract).then_inc(S["sdT_split"], 1)

            def mix_experts(t):
                b = t % 2
                dve.wait_ge(yk_loaded[b], 16 * TOP_K * (t // 2 + 1))
                dve.wait_ge(S["z_psum"], t + 1)
                if t >= 1:
                    dve.wait_ge(S["g_ready"], t)
                step(V.scalar_tensor_tensor(mix, yk[0][:, b, :], val[0][:, t:t + 1], bank[Z_BANKS[b]][:], ALU.mult, ALU.add))
                V.scalar_tensor_tensor(mix, yk[1][:, b, :], val[1][:, t:t + 1], mix, ALU.mult,
                                       ALU.add).then_inc(S["mix_ready"], 1)

            def finish(t):
                b = t % 2
                dve.wait_ge(S["g_ready"], t + 1)
                dve.wait_ge(S["down_psum"], t + 1)
                if t >= 2:
                    dve.wait_ge(out_stored[b], 16 * (t // 2))
                step(V.tensor_tensor(o_sb[:, b, :], g, bank[DOWN_BANKS[b]][:], ALU.mult))
                dve.wait_ge(x_again[b], 16 * (t // 2 + 1))
                V.tensor_tensor(o_sb[:, b, :], o_sb[:, b, :], x_end[:, b, :], ALU.add).then_inc(S["o_ready"], 1)

            product_low(0)
            apply_mask(1, HALF - 1)
            dve.wait_ge(S["z_high_ready"], 1)
            V.tensor_tensor(sw3_low[:], sw3[:], sw3_high[:].bitcast(F32), ALU.subtract).then_inc(S["z_split"], 1)
            dve.wait_ge(S["z_high_ready"], 2)
            V.tensor_tensor(shT_low[:], shT[:], shT_high[:].bitcast(F32), ALU.subtract).then_inc(S["z_split"], 1)
            for t in range(NT):
                if t + 1 < NT:
                    product_low(t + 1)
                mix_experts(t)
                finish(t)

        @block.tensor
        def _(pe):
            TE = nc.tensor
            pe.wait_ge(S["const_ready"], 11)
            def product3(dst, stat_high, stat_low, mov_high, mov_low, first, last):
                TE.matmul(dst, stat_high, mov_high, start=first, stop=False)
                TE.matmul(dst, stat_high, mov_low, start=False, stop=False)
                return TE.matmul(dst, stat_low, mov_high, start=False, stop=last)

            def transpose_rows(t):
                pe.wait_ge(S["xn_ready"], t + 1)
                if t >= 4:
                    pe.wait_ge(S["xnT_split"], t - 3)
                for k in range(HC):
                    ins = TE.transpose(xnT_bank(t)[:, k, :], xn[:, t, k * P:(k + 1) * P], ident[:])
                ins.then_inc(S["xnT_psum"], 1)

            def project(t, c, dst, by_chunk=False, router=False):
                a, b = PIECES[c]
                if router:
                    b += E
                for k in range(HC):
                    if by_chunk:
                        pe.wait_ge(S["w_split"], k + 2)
                    rows = slice(t * P, (t + 1) * P)
                    ins = product3(dst[:, 0:b - a], xnT_high[:, k, rows], xnT_low[:, k, rows],
                                   proj(w_high)[:, k, a:b], proj(w_low)[:, k, a:b], k == 0, k == HC - 1)
                return ins

            for t in range(HALF):
                transpose_rows(t)
            for n, (t, c) in enumerate(GATE_UNITS):
                if n == HALF:
                    for later in range(HALF, NT):
                        transpose_rows(later)
                if c == LAST:
                    pe.wait_ge(S["xnT_split"], t + 1)
                elif t == 0:
                    pe.wait_ge(S["w_split"], 1 + HC + c + 1)
                if n >= NP_:
                    pe.wait_ge(S["s_ready"], n - NP_ + 1)
                    if n <= NT:
                        pe.wait_ge(S["logits_ready"], n - NP_ + 1)
                project(t, c, bank[n % NP_], by_chunk=(n == 0), router=(c == LAST)).then_inc(S["gate_psum"], 1)
                if n == NT + HALF:
                    pe.wait_ge(S["picks_ready"], 1)
                    flat = hits[:].rearrange("p t e -> p (t e)")
                    TE.matmul(bank[5][:, P:2 * P], before[:], flat, start=True, stop=True)
                    TE.matmul(bank[5][:, 2 * P:3 * P], ones[:], flat, start=True, stop=True).then_inc(S["rank_ready"], 1)
                if n == NT + HALF + 1:
                    pe.wait_ge(S["gates_ready"], 1)
                    for q in range(NT):
                        ins = TE.transpose(bank[6 + q // 4][0:E + 1, (q % 4) * P:(q % 4 + 1) * P], gates[:, q, :], ident[:])
                    ins.then_inc(S["gateT_psum"], 1)

            pe.wait_ge(S["sw12_split"], 1)
            pe.wait_ge(S["gateT_ready"], 1)
            for u in range(2 * SC):
                c, half = u // 2, u % 2
                for m in range(2):
                    if u >= 2:
                        pe.wait_ge(S["shT_ready"], u - 1)
                    dst = bank[((3, 4), (6, 7))[u % 2][m]]
                    for k in range(HC):
                        rows, cols = slice(c * P, (c + 1) * P), slice(half * BANK, (half + 1) * BANK)
                        ins = product3(dst[:], sw12_high[:, m * HC + k, rows], sw12_low[:, m * HC + k, rows],
                                       xnT_high[:, k, cols], xnT_low[:, k, cols], k == 0, k == HC - 1)
                    ins.then_inc(S["shared_psum"], 1)

            for t in range(NT):
                for c in range(NP_):
                    if t == 0:
                        pe.wait_ge(S["w_split"], GATE_SPLITS + c + 1)
                        if c == 0:
                            pe.wait_ge(S["s_ready"], NT * NP_)
                    elif t == 1:
                        pe.wait_ge(S["shT_ready"], 2 * SC)
                    else:
                        pe.wait_ge(S["su_ready"], (t - 2) * NP_ + c + 1)
                    project(t, c, bank[3 * (t % 2) + c]).then_inc(S["up_psum"], 1)

            def transpose_xg(b, slot, loaded):
                pe.wait_ge(xg_loaded[slot], loaded)
                for k in range(HC):
                    ins = TE.transpose(bank[b][:, k * P:(k + 1) * P], xg_slots[slot][:, k * P:(k + 1) * P], ident[:])
                ins.then_inc(S["xgT_psum"], 1)

            def project_h(j, b, loaded):
                pe.wait_ge(S["xgT_ready"], j + 1)
                pe.wait_ge(w12_loaded[b], loaded)
                for m in range(2):
                    for k in range(HC):
                        ins = TE.matmul(bank[2 + b][:, m * P:(m + 1) * P], w12[:, b, (m * HC + k) * M:(m * HC + k + 1) * M],
                                        xgT[:, b, k * P:(k + 1) * P], start=(k == 0), stop=(k == HC - 1))
                ins.then_inc(S["h_psum"], 1)

            def project_y(j, b, loaded, emptied):
                pe.wait_ge(S["hT_ready"], j + 1)
                pe.wait_ge(w3_loaded[b], loaded)
                if emptied is not None:
                    pe.wait_ge(S["y_ready"], emptied)
                TE.matmul(bank[4 + b][:], hT[:, b, :], w3[:, b, 0:H], start=True,
                          stop=True).then_inc(S["y_psum"], 1)

            def pair(p, round4, odd):
                first, second = (isinstance(p, int) and p == n for n in range(2))
                for b in range(2):
                    transpose_xg(b, odd * 2 + b, round4 * 16 + 16)
                for b in range(2):
                    if not first:
                        project_y(p * 2 - 2 + b, b, p * 16, None if second else p * 2 - 3 + b)
                    project_h(p * 2 + b, b, p * 16 + 16)

            n_extra = extra(pe)
            pe.wait_ge(S["su_ready"], NT * NP_)
            pair(0, 0, 0)
            pair(1, 0, 1)
            with pe.Fori(1, FULL_PAIRS // 2) as r:
                for odd in range(2):
                    pair(r * 2 + odd, r, odd)
            with pe.If(n_extra > 0):
                with pe.Fori(0, (PAIRS - FULL_PAIRS) // 2) as r:
                    for odd in range(2):
                        with pe.If(r * 2 + odd < n_extra):
                            pair(r * 2 + (odd + FULL_PAIRS), r + FULL_PAIRS // 2, odd)
            def transpose_products(t):
                pe.wait_ge(S["s_masked"], t + 1)
                for q in range(3):
                    if t >= 1:
                        pe.wait_ge(S["sdT_split"], 3 * (t - 1) + q + 1)
                    for k in range(4 * q, min(4 * q + 4, IC)):
                        a, b = CHUNKS[k]
                        ins = TE.transpose(bank[q][0:b - a, (k % 4) * P:(k % 4 + 1) * P], s[:, t, a:b], ident[:])
                    ins.then_inc(S["sdT_psum"], 1)

            pe.wait_ge(S["hT_ready"], n_extra * 2 + (FULL - 1))
            transpose_products(0)
            for b in range(2):
                project_y(n_extra * 2 + (FULL - 2 + b), b, n_extra * 16 + FULL_PAIRS * 16, n_extra * 2 + (FULL - 3 + b))
            def shared_third(t):
                if t >= 2:
                    pe.wait_ge(S["mix_ready"], t - 1)
                dst, rows = bank[Z_BANKS[t % 2]], slice(t * P, (t + 1) * P)
                TE.matmul(dst[:], gateT[:, rows], b3_stack[:], start=True, stop=False)
                for k in range(SC):
                    ins = product3(dst[:], shT_high[:, k, rows], shT_low[:, k, rows], sw3_high[:, k, :], sw3_low[:, k, :],
                                   False, k == SC - 1)
                ins.then_inc(S["z_psum"], 1)

            for t in range(NT):
                if t + 1 < NT:
                    transpose_products(t + 1)
                if t >= 1:
                    shared_third(t)
                if t == 0:
                    pe.wait_ge(S["wd_split"], IC)
                elif t >= 2:
                    pe.wait_ge(S["o_ready"], t - 1)
                for k in range(IC):
                    a, b = CHUNKS[k]
                    if k % 4 == 0:
                        pe.wait_ge(S["sdT_split"], 3 * t + k // 4 + 1)
                    cols = slice(k * P, (k + 1) * P)
                    ins = product3(bank[DOWN_BANKS[t % 2]][:], sdT_high[0:b - a, t % 2, cols], sdT_low[0:b - a, t % 2, cols],
                                   down(w_high)[0:b - a, k, :], down(w_low)[0:b - a, k, :], k == 0, k == IC - 1)
                ins.then_inc(S["down_psum"], 1)
                if t == 0:
                    pe.wait_ge(S["b3_split"], 1)
                    pe.wait_ge(S["z_split"], 2)
                    pe.wait_ge(S["y_ready"], n_extra * 2 + FULL)
                    shared_third(0)


def kernel(L0_attn_x, L0_attn_w_gate, L0_attn_w_up, L0_attn_w_down, L0_ffn_router_w, L0_ffn_router_b,
           L0_ffn_router_bias, L0_ffn_ew1, L0_ffn_eb1, L0_ffn_ew2, L0_ffn_eb2, L0_ffn_ew3, L0_ffn_eb3,
           L0_ffn_sw1, L0_ffn_sb1, L0_ffn_sw2, L0_ffn_sb2, L0_ffn_sw3, L0_ffn_sb3):
    import numpy as np
    import concourse.bacc as bacc
    from concourse.bass_utils import run_bass_kernel_spmd

    x = np.asarray(L0_attn_x)
    B, S_, H = x.shape
    ew1, ew2, ew3 = (np.asarray(w) for w in (L0_ffn_ew1, L0_ffn_ew2, L0_ffn_ew3))
    E, _, M = ew1.shape

    def by_partition(w):
        return w.reshape(E, H // P, P, M).transpose(0, 2, 1, 3).reshape(E * P, H // P * M)

    expert_w12 = np.concatenate([by_partition(ew1), by_partition(ew2)], axis=1)
    expert_b12 = np.concatenate([np.asarray(L0_ffn_eb1).T, np.asarray(L0_ffn_eb2).T], axis=1)
    sb1, sb2 = (np.asarray(b).reshape(-1, P).T for b in (L0_ffn_sb1, L0_ffn_sb2))
    arrays = {
        "x": x.reshape(B * S_, H),
        "w_gate_t": np.asarray(L0_attn_w_gate).T,
        "w_up_t": np.asarray(L0_attn_w_up).T,
        "w_down_t": np.asarray(L0_attn_w_down).T,
        "router_w": np.asarray(L0_ffn_router_w),
        "router_b": np.asarray(L0_ffn_router_b).reshape(1, E),
        "router_bias": np.asarray(L0_ffn_router_bias).reshape(1, E),
        "expert_w12": expert_w12,
        "expert_w3": ew3.reshape(E * M, H),
        "expert_b12": expert_b12,
        "expert_b3": np.asarray(L0_ffn_eb3),
        "shared_w12": np.concatenate([np.asarray(L0_ffn_sw1), np.asarray(L0_ffn_sw2)], axis=0),
        "shared_b12": np.concatenate([sb1, sb2], axis=1),
        "shared_w3": np.asarray(L0_ffn_sw3),
        "shared_b3": np.asarray(L0_ffn_sb3).reshape(1, H),
    }
    arrays = {n: np.ascontiguousarray(a) for n, a in arrays.items()}
    nc = bacc.Bacc("TRN2", target_bir_lowering=False, num_devices=1)
    args = [nc.dram_tensor(n, a.shape, mybir.dt.from_np(a.dtype), kind="ExternalInput").ap() for n, a in arrays.items()]
    out = nc.dram_tensor("out", (B * S_, H), F32, kind="ExternalOutput").ap()
    gated_block_kernel(nc, *args, out)
    r = run_bass_kernel_spmd(nc, [arrays], core_ids=[0])
    return r.results[0]["out"].reshape(B, S_, H)
```
